# Optimizing a Trainium2 kernel written in Bass

```python
import numpy as np
import jax
import jax.numpy as jnp

def _softmax(x, axis=-1):
    return jax.nn.softmax(x, axis=axis)

def _gelu(x):
    return jax.nn.gelu(x, approximate=True)

def _silu(x):
    return jax.nn.silu(x)

def _sigmoid(x):
    return jax.nn.sigmoid(x)

def _layernorm(x, axis=-1, eps=1e-05):
    m = jnp.mean(x, axis=axis, keepdims=True)
    v = jnp.var(x, axis=axis, keepdims=True)
    return (x - m) / jnp.sqrt(v + eps)

def _scatter_add(tgt, idx, src, axis=0):
    return tgt.at[idx].add(src)

def _segment_sum(src, seg, n):
    return jax.ops.segment_sum(src, seg, n)
kernel_name = 'mk_early_fusion_d1_tok_img1024_r4_497c3c'

def setup_inputs(seed: int=0):
    np.random.seed(seed)
    _w = jnp.asarray

    def _rec_inputs():
        import jax
        import jax.numpy as jnp
        _rk = jax.random.key(seed)
        x = -0.000222058 + 0.999998 * jax.random.normal(jax.random.fold_in(_rk, 1), (64, 3, 224, 224), jnp.float32)
        txt = 0.00193382 + 0.183443 * jax.random.normal(jax.random.fold_in(_rk, 2), (64, 32, 256), jnp.float32)
        return (x, txt)
    x, txt = _rec_inputs()

    def _L0_tok_setup():
        import jax, jax.numpy as jnp
        import numpy as np
        P = 16
        C = 3
        D = 256

        def _patchify(x, p):
            B, Cc, H, W = x.shape
            gh, gw = (H // p, W // p)
            x = x.reshape(B, Cc, gh, p, gw, p)
            x = x.transpose(0, 2, 4, 1, 3, 5)
            return x.reshape(B, gh * gw, Cc * p * p)
        key = jax.random.key(seed)
        k1, k2, k3, k4, k5 = jax.random.split(key, 5)
        patch_dim = C * P * P
        s1 = 1.0 / np.sqrt(patch_dim)
        s2 = 1.0 / np.sqrt(D)
        return {'x': jax.random.normal(k1, (32, C, 128, 128), dtype=jnp.float32), 'W1': jax.random.uniform(k2, (patch_dim, D), jnp.float32, -s1, s1), 'b1': jax.random.uniform(k3, (D,), jnp.float32, -s1, s1), 'W2': jax.random.uniform(k4, (D, D), jnp.float32, -s2, s2), 'b2': jax.random.uniform(k5, (D,), jnp.float32, -s2, s2)}
    _L0_tok_all = _L0_tok_setup()
    _L0_tok_in = {k: v for k, v in _L0_tok_all.items() if k in ('W1', 'b1', 'W2', 'b2')}
    del _L0_tok_all

    def _L0_attn_setup():
        import jax, jax.numpy as jnp
        import numpy as np
        import math
        EMBED = 256
        HEADS = 16
        HEAD_DIM = EMBED // HEADS
        HIDDEN = 1024
        NUM_BUCKETS = 32
        MAX_DISTANCE = 128
        LN_EPS = 1e-06
        KQ_EPS = 1e-06

        def _rms_norm(xs, weight):
            xf = xs.astype(jnp.float32)
            var = jnp.mean(jnp.square(xf), axis=-1, keepdims=True)
            ys = xs * jax.lax.rsqrt(var + LN_EPS) * weight
            return ys.astype(xs.dtype)

        def _normalize_kq(kq):
            ss = jnp.sum(jnp.square(kq), axis=-1, keepdims=True)
            return kq * jax.lax.rsqrt(ss + KQ_EPS)

        def _rel_position_bucket(rp):
            rp = -jnp.minimum(rp, 0)
            max_exact = NUM_BUCKETS // 2
            is_small = rp < max_exact
            safe = jnp.maximum(rp, 1).astype(jnp.float32)
            large = max_exact + (jnp.log(safe / max_exact) / math.log(MAX_DISTANCE / max_exact) * (NUM_BUCKETS - max_exact)).astype(jnp.int32)
            large = jnp.minimum(large, NUM_BUCKETS - 1)
            return jnp.where(is_small, rp, large)
        key = jax.random.key(seed)
        ks = jax.random.split(key, 8)
        B, S = (2, 512)
        w = 0.02
        return {'x': jax.random.normal(ks[0], (B, S, EMBED), dtype=jnp.float32), 'ln1_w': jnp.ones((EMBED,), jnp.float32), 'Wq': jax.random.normal(ks[1], (EMBED, EMBED), jnp.float32) * w, 'Wk': jax.random.normal(ks[2], (EMBED, EMBED), jnp.float32) * w, 'Wv': jax.random.normal(ks[3], (EMBED, EMBED), jnp.float32) * w, 'rel_bias': jax.random.normal(ks[4], (NUM_BUCKETS, HEADS), jnp.float32) * w, 'scale': jnp.ones((HEADS,), jnp.float32), 'Wo': jax.random.normal(ks[5], (EMBED, EMBED), jnp.float32) * w, 'ln2_w': jnp.ones((EMBED,), jnp.float32), 'W1': jax.random.normal(ks[6], (EMBED, HIDDEN), jnp.float32) * w, 'W2': jax.random.normal(ks[7], (HIDDEN, EMBED), jnp.float32) * w}
    _L0_attn_all = _L0_attn_setup()
    _L0_attn_in = {k: v for k, v in _L0_attn_all.items() if k in ('ln1_w', 'Wq', 'Wk', 'Wv', 'rel_bias', 'scale', 'Wo', 'ln2_w', 'W1', 'W2')}
    del _L0_attn_all

    def _L0_ffn_setup():
        import jax, jax.numpy as jnp
        import numpy as np
        from math import ceil
        CAPACITY_FACTOR = 2.0
        MIN_CAPACITY = 4
        key = jax.random.key(seed)
        ks = jax.random.split(key, 4)
        B, S, D, Di, E = (4, 512, 256, 1024, 8)
        x = jax.random.normal(ks[0], (B, S, D), dtype=jnp.float32)
        Wr = jax.random.normal(ks[1], (D, E), dtype=jnp.float32) * D ** (-0.5)
        W1 = jax.random.normal(ks[2], (E, D, Di), dtype=jnp.float32) * D ** (-0.5)
        b1 = jnp.zeros((E, Di), dtype=jnp.float32)
        W2 = jax.random.normal(ks[3], (E, Di, D), dtype=jnp.float32) * Di ** (-0.5)
        b2 = jnp.zeros((E, D), dtype=jnp.float32)
        return {'x': x, 'Wr': Wr, 'W1': W1, 'b1': b1, 'W2': W2, 'b2': b2}
    _L0_ffn_all = _L0_ffn_setup()
    _L0_ffn_in = {k: v for k, v in _L0_ffn_all.items() if k in ('Wr', 'W1', 'b1', 'W2', 'b2')}
    del _L0_ffn_all
    return {'x': x, 'txt': txt, 'L0_tok_W1': _L0_tok_in['W1'], 'L0_tok_b1': _L0_tok_in['b1'], 'L0_tok_W2': _L0_tok_in['W2'], 'L0_tok_b2': _L0_tok_in['b2'], 'L0_attn_ln1_w': _L0_attn_in['ln1_w'], 'L0_attn_Wq': _L0_attn_in['Wq'], 'L0_attn_Wk': _L0_attn_in['Wk'], 'L0_attn_Wv': _L0_attn_in['Wv'], 'L0_attn_rel_bias': _L0_attn_in['rel_bias'], 'L0_attn_scale': _L0_attn_in['scale'], 'L0_attn_Wo': _L0_attn_in['Wo'], 'L0_attn_ln2_w': _L0_attn_in['ln2_w'], 'L0_attn_W1': _L0_attn_in['W1'], 'L0_attn_W2': _L0_attn_in['W2'], 'L0_ffn_Wr': _L0_ffn_in['Wr'], 'L0_ffn_W1': _L0_ffn_in['W1'], 'L0_ffn_b1': _L0_ffn_in['b1'], 'L0_ffn_W2': _L0_ffn_in['W2'], 'L0_ffn_b2': _L0_ffn_in['b2']}

def reference(x, txt, L0_tok_W1, L0_tok_b1, L0_tok_W2, L0_tok_b2, L0_attn_ln1_w, L0_attn_Wq, L0_attn_Wk, L0_attn_Wv, L0_attn_rel_bias, L0_attn_scale, L0_attn_Wo, L0_attn_ln2_w, L0_attn_W1, L0_attn_W2, L0_ffn_Wr, L0_ffn_W1, L0_ffn_b1, L0_ffn_W2, L0_ffn_b2):
    import jax
    import jax.numpy as jnp

    def _L0_tok_ref(x, W1, b1, W2, b2):
        import jax, jax.numpy as jnp
        import numpy as np
        P = 16
        C = 3
        D = 256

        def _patchify(x, p):
            B, Cc, H, W = x.shape
            gh, gw = (H // p, W // p)
            x = x.reshape(B, Cc, gh, p, gw, p)
            x = x.transpose(0, 2, 4, 1, 3, 5)
            return x.reshape(B, gh * gw, Cc * p * p)
        patches = _patchify(x, P)
        h = jax.nn.silu(jnp.einsum('blk,kd->bld', patches, W1) + b1)
        return jnp.einsum('bld,de->ble', h, W2) + b2

    def _L0_attn_ref(x, ln1_w, Wq, Wk, Wv, rel_bias, scale, Wo, ln2_w, W1, W2):
        import jax, jax.numpy as jnp
        import numpy as np
        import math
        EMBED = 256
        HEADS = 16
        HEAD_DIM = EMBED // HEADS
        HIDDEN = 1024
        NUM_BUCKETS = 32
        MAX_DISTANCE = 128
        LN_EPS = 1e-06
        KQ_EPS = 1e-06

        def _rms_norm(xs, weight):
            xf = xs.astype(jnp.float32)
            var = jnp.mean(jnp.square(xf), axis=-1, keepdims=True)
            ys = xs * jax.lax.rsqrt(var + LN_EPS) * weight
            return ys.astype(xs.dtype)

        def _normalize_kq(kq):
            ss = jnp.sum(jnp.square(kq), axis=-1, keepdims=True)
            return kq * jax.lax.rsqrt(ss + KQ_EPS)

        def _rel_position_bucket(rp):
            rp = -jnp.minimum(rp, 0)
            max_exact = NUM_BUCKETS // 2
            is_small = rp < max_exact
            safe = jnp.maximum(rp, 1).astype(jnp.float32)
            large = max_exact + (jnp.log(safe / max_exact) / math.log(MAX_DISTANCE / max_exact) * (NUM_BUCKETS - max_exact)).astype(jnp.int32)
            large = jnp.minimum(large, NUM_BUCKETS - 1)
            return jnp.where(is_small, rp, large)
        B, S, E = x.shape
        xn = _rms_norm(x, ln1_w)
        q = (xn @ Wq).reshape(B, S, HEADS, HEAD_DIM)
        k = (xn @ Wk).reshape(B, S, HEADS, HEAD_DIM)
        v = (xn @ Wv).reshape(B, S, HEADS, HEAD_DIM)
        q = _normalize_kq(q)
        k = _normalize_kq(k)
        pos = jnp.arange(S, dtype=jnp.int32)
        bucket = _rel_position_bucket(pos[None, :] - pos[:, None])
        bias = rel_bias[bucket]
        bias = jnp.transpose(bias, (2, 0, 1))[None]
        attn = jnp.einsum('bqhd,bkhd->bhqk', q, k) + bias
        attn = attn * scale[None, :, None, None]
        causal = pos[None, :] - pos[:, None] < 0
        attn = jnp.where(causal[None, None], attn, -1000000.0)
        attn = jax.nn.softmax(attn, axis=-1)
        y = jnp.einsum('bhqk,bkhd->bqhd', attn, v).reshape(B, S, E)
        y = y @ Wo + x
        z = _rms_norm(y, ln2_w)
        z = jax.nn.relu(z @ W1) @ W2
        return z + y

    def _L0_ffn_ref(x, Wr, W1, b1, W2, b2):
        import jax, jax.numpy as jnp
        import numpy as np
        from math import ceil
        CAPACITY_FACTOR = 2.0
        MIN_CAPACITY = 4
        B, S, D = x.shape
        E = Wr.shape[1]
        N = B * S
        k = max(MIN_CAPACITY, ceil(N * CAPACITY_FACTOR / E))
        xt = x.reshape(N, D)
        scores = jax.nn.softmax(xt @ Wr, axis=-1)
        G, idx = jax.lax.top_k(scores.T, k)
        X_in = xt[idx]
        h = jax.nn.gelu(jnp.einsum('ekd,edh->ekh', X_in, W1) + b1[:, None, :], approximate=False)
        X_e = jnp.einsum('ekh,ehd->ekd', h, W2) + b2[:, None, :]
        contrib = (G[..., None] * X_e).reshape(E * k, D)
        out = jnp.zeros((N, D), dtype=x.dtype).at[idx.reshape(-1)].add(contrib)
        return out.reshape(B, S, D)
    h = _L0_tok_ref(x, L0_tok_W1, L0_tok_b1, L0_tok_W2, L0_tok_b2)
    h = jnp.concatenate([h, txt], axis=1)
    h = h + _L0_attn_ref(_layernorm(h, axis=-1), L0_attn_ln1_w, L0_attn_Wq, L0_attn_Wk, L0_attn_Wv, L0_attn_rel_bias, L0_attn_scale, L0_attn_Wo, L0_attn_ln2_w, L0_attn_W1, L0_attn_W2)
    h = h + _L0_ffn_ref(_layernorm(h, axis=-1), L0_ffn_Wr, L0_ffn_W1, L0_ffn_b1, L0_ffn_W2, L0_ffn_b2)
    return h

_drawn_inputs = setup_inputs


def setup_inputs(seed=0):
    import zlib

    import numpy as np

    out = dict(_drawn_inputs(seed))
    spreads = {'L0_attn_ln1_w': (1.0, 0.6),
     'L0_attn_scale': (1.0, 0.6),
     'L0_attn_ln2_w': (1.0, 0.2),
     'L0_ffn_b1': (0.0, 0.323),
     'L0_ffn_b2': (0.0, 0.1)}
    factors = {'L0_attn_Wq': 31.172, 'L0_attn_Wk': 29.482, 'L0_attn_rel_bias': 51.703}
    for name, (base, spread) in spreads.items():
        noise = np.random.default_rng([zlib.crc32(name.encode()), seed]).standard_normal(out[name].shape)
        drawn = base * np.exp(spread * noise) if base else spread * noise
        out[name] = jnp.asarray(drawn.astype(out[name].dtype))
    for name, factor in factors.items():
        out[name] = (out[name] * factor).astype(out[name].dtype)
    return out
```

```python
import concourse.bass as bass
from concourse import mybir
from contextlib import ExitStack
import numpy as np


def relative_bucket_runs(distances, buckets, max_distance):
    exact = buckets // 2
    n = np.arange(1, distances, dtype=np.int32)
    large = exact + (np.log(n.astype(np.float32) / np.float32(exact))
                     / np.float32(np.log(max_distance / exact)) * np.float32(buckets - exact)).astype(np.int32)
    bucket = np.where(n < exact, n, np.minimum(large, buckets - 1))
    runs = []
    for d, k in zip(n.tolist(), bucket.tolist()):
        if runs and runs[-1][2] == k:
            runs[-1][1] += 1
        else:
            runs.append([d, 1, k])
    return runs


class Chain:
    def __init__(self, eng, sem, wait_apart):
        self.wait_apart = wait_apart
        self.eng, self.sem, self.base, self.n, self.loops = eng, sem, 0, 0, []

    def step(self, ins, apart=False):
        ins.then_inc(self.sem, 1)
        self.n += 1
        value = self.base + self.n
        if apart and not isinstance(value, int):
            value = self.eng.snap(self.eng.to_reg(value))
            self.wait_apart()
        self.eng.wait_ge(self.sem, value)

    def enter(self, trip, steps):
        self.loops.append((self.base, self.n, steps))
        self.base, self.n = trip * steps + (self.base + self.n), 0

    def leave(self, trips):
        base, n, steps = self.loops.pop()
        assert self.n == steps, (self.n, steps)
        self.base, self.n = base, n + trips * steps


def early_fusion_kernel(nc, x, txt, tok_W1, tok_b1, tok_W2, tok_b2, ln1_w, Wq, Wk, Wv, rel_bias, scale, Wo,
                        ln2_w, W1, W2, Wr, fW1, fb1, fW2, fb2, out):
    F32, BF16, F16, I32, U32 = mybir.dt.float32, mybir.dt.bfloat16, mybir.dt.float16, mybir.dt.int32, mybir.dt.uint32
    ALU, ACT, AX = mybir.AluOpType, mybir.ActivationFunctionType, mybir.AxisListType

    B, C, IMG, _ = x.shape
    TXT, D = txt.shape[1], txt.shape[2]
    PS = 16
    GP = IMG // PS
    NP_ = GP * GP
    S = NP_ + TXT
    T = S // 2
    LASTP = NP_ - T
    N = B * S
    PAIRS = B // 2
    NT = 4
    W = NT * T
    NTILES = N // T
    H = scale.shape[0]
    HD = D // H
    HV = HD + 1
    HP = 64
    NBUCK = rel_bias.shape[0]
    KC = D // 128
    HID = W1.shape[1]
    MC = HID // 128
    NE = Wr.shape[1]
    CAP = max(4, -(-2 * N // NE))
    GROUPS = CAP // W
    SLOTC = CAP // T
    R = 128 // NE
    GT = NTILES // R
    SEG = GT * T
    KROW = C * PS
    HALF = PS // 2
    QW = S + T
    XW = D + NE
    LN_EPS, RMS_EPS = 1e-5, 1e-6
    LT = NTILES // GROUPS
    SAFE = 75.0
    assert CAP == GROUPS * W and T <= 128 and LASTP > 0 and NTILES == R * GT and SLOTC == 32

    xd = nc.dram_tensor("xn_rows", (N, XW), F32)
    zrow_d = nc.dram_tensor("bias_by_distance", (H, T, 2 * S - 1 + T), F32)
    mrow_d = nc.dram_tensor("bias_row_maximum", (H, S), F32)
    out_rows = out.rearrange("b s d -> (b s) d")

    ctx = ExitStack()
    with ctx:
        def sb(name, shape, dt=F32, stack=ctx):
            return stack.enter_context(nc.sbuf_tensor(name, shape, dt))

        def sem(name):
            return ctx.enter_context(nc.semaphore(name))

        logits = sb("logits", [T, NTILES, NE])
        ident = sb("ident", [128, 128])
        group_ones = sb("group_ones", [128, 128])
        earlier_ones = sb("earlier_ones", [128, 128])
        diff = sb("diff", [128, 128], I32)
        difff = sb("difff", [128, 128])
        neg_half = sb("neg_half", [T, 128])
        ln_eps = sb("ln_eps", [T, 128])
        rms_eps = sb("rms_eps", [T, 128])
        tok_p = sb("tok_p", [T, 1])
        tok_pi = sb("tok_pi", [T, 1], I32)
        diff_low = sb("diff_low", [128, 128], I32)
        iota_i = sb("iota_i", [T, 128], I32)
        iota_b = sb("iota_b", [T, 128], BF16)
        first_col = sb("first_col", [T, T])
        fb1c = sb("fb1c", [128, NE, MC])

        p1 = ExitStack()

        def s1(name, shape, dt=F32):
            return sb(name, shape, dt, p1)

        w1t = s1("w1t", [2 * KROW, HALF, D])
        w2t = s1("w2t", [128, KC, D])
        b1t = s1("b1t", [128, KC])
        b2t = s1("b2t", [T, D])
        wqkv = s1("wqkv", [128, KC, 3 * D])
        wo = s1("wo", [128, KC, D])
        w1m = s1("w1m", [128, KC, HID])
        w2m = s1("w2m", [128, MC, D])
        wr = s1("wr", [128, KC, NE])
        lnw = s1("lnw", [128, 2, KC])
        relb = s1("relb", [H, NBUCK])
        sc_col = s1("sc_col", [H, 1])
        zrow = s1("zrow", [H, 2 * S - 1])
        mrow = s1("mrow", [H, S])
        bias_t = s1("bias_t", [T, H, QW])
        sc_bc = s1("sc_bc", [T, H])
        sc_q = s1("sc_q", [T, NT, H])
        shift = s1("shift", [T, 2, H])
        img = [s1(f"img{b}", [2 * KROW, GP * IMG]) for b in range(2)]
        hid = s1("hid", [128, KC, 2 * NP_])
        h0 = s1("h0", [T, NT, D])
        xa = s1("xa", [T, NT, D])
        xs = s1("xs", [T, NT, D])
        xsT = s1("xsT", [128, KC, W])
        qkraw = s1("qkraw", [T, NT, 2 * D])
        sqb = s1("sqb", [T, 2 * D])
        ss = s1("ss", [T, NT, 2 * H])
        rn = s1("rn", [T, NT, 2 * H])
        qkp = s1("qkp", [T, NT, 2 * H, HP], F16)
        qkT = s1("qkT", [128, H // 2, 2, W], F16)
        v1 = s1("v1", [T, NT, H, HV])
        p0 = [s1(f"p0_{k}", [T, 2, QW]) for k in range(2)]
        pm = [s1(f"pm_{k}", [T, 2, QW]) for k in range(2)]
        nwt = s1("nwt", [T, NT * 2 * H])
        ident_h = s1("ident_h", [T, T], F16)
        yrec = s1("yrec", [T, 2, H])
        yn = s1("yn", [T, NT, D])
        yT = s1("yT", [128, KC, W])
        y2 = s1("y2", [T, NT, D])
        hy = s1("hy", [T, NT, D])
        junk = s1("junk", [T, NT, D], BF16)
        hT = s1("hT", [128, MC, W])
        xn2 = s1("xn2", [T, NT, D])
        st = s1("st", [T, NT, 6])
        mv1 = s1("mv1", [T, NT, 2])
        mv2 = s1("mv2", [T, NT, 2])
        lt = s1("lt", [T, 6, NT])
        ss2 = s1("ss2", [T, NT])
        r2 = s1("r2", [T, NT])
        rstd2 = s1("rstd2", [T, NT])
        mtmp = [hT[0:T, :, :].rearrange("p m w -> p (m w)"), qkT[0:T, :, :, :].rearrange("p c s w -> p (c s w)").bitcast(F32)]
        p1.close()

        def s2(name, shape, dt=F32):
            return sb(name, shape, dt)

        score = s2("score", [T, NTILES, NE])
        by_group = s2("by_group", [T, GT, R * NE])
        smax = s2("smax", [T, NTILES])
        scoreT = s2("scoreT", [128, SEG])
        hit = s2("hit", [128, SEG])
        above = s2("above", [128, SEG])
        equal = s2("equal", [128, SEG])
        rank = s2("rank", [128, SEG])
        bitv = s2("bitv", [128, 1])
        biti = s2("biti", [128, 1], I32)
        cand = s2("cand", [128, 1], I32)
        kept = s2("kept", [128, 1], I32)
        thr = s2("thr", [128, 1], I32)
        cnt = s2("cnt", [128, 4])
        need = s2("need", [128, 2])
        posi = s2("posi", [T, NTILES, NE], I32)
        posh = s2("posh", [T, NTILES, NE], I32)
        slot_a = s2("slot_a", [T, NE + 1, NTILES], BF16)
        slot_b = s2("slot_b", [T, NE + 1, NTILES], BF16)
        oh_b = [s2(f"oh_b{k}", [T, LT, T], BF16) for k in range(2)]
        oh_a = [s2(f"oh_a{k}", [T, LT, 2, SLOTC], BF16) for k in range(2)]
        eq_a = [s2(f"eq_a{k}", [T, LT, SLOTC], BF16) for k in range(2)]
        zero_w = s2("zero_w", [T, T], BF16)
        idx_t = s2("idx_t", [T, 32])
        idx_all = s2("idx_all", [T, (NE + 1) * 32], U32)
        idx_cur = [s2(f"idx_cur{k}", [T, NT], U32) for k in range(2)]
        we1 = [s2(f"we1_{k}", [128, KC, HID]) for k in range(2)]
        we2 = [s2(f"we2_{k}", [128, MC, D]) for k in range(2)]
        fb2b = s2("fb2b", [T, NE, D])
        xg = [s2(f"xg{k}", [T, NT, XW]) for k in range(2)]
        xgT = s2("xgT", [128, KC, W])
        hTe = s2("hTe", [128, MC, W])
        biased = s2("biased", [T, 2, D])
        contrib = [s2(f"contrib{k}", [T, NT, D]) for k in range(2)]

        def pb(name, shape):
            return ctx.enter_context(nc.psum_tensor(name, shape, F32))

        G = [pb(f"G{k}", [128, 512]) for k in range(2)]
        SC = [pb(f"SC{k}", [128, 2, 512]) for k in range(2)]
        Y = [pb(f"Y{k}", [128, 512]) for k in range(2)]

        weights_in, consts_in = sem("weights_in"), sem("consts_in")
        pool_consts = sem("pool_consts")
        zrow_ready, rows_out, toeplitz_in = sem("zrow_ready"), sem("rows_out"), sem("toeplitz_in")
        table_diff, table_exp, setup_done = sem("table_diff"), sem("table_exp"), sem("setup_done")
        img_in = [sem(f"img_in{b}") for b in range(2)]
        text_in = sem("text_in")
        filled = [sem(f"filled{k}") for k in range(2)]
        evacuated = [sem(f"evacuated{k}") for k in range(2)]
        ln1_stats, ln1_scales, xs_done = sem("ln1_stats"), sem("ln1_scales"), sem("xs_done")
        qk_scaled, qk_high, qk_normed = sem("qk_scaled"), sem("qk_high"), sem("qk_normed")
        scores_done, exp_done, probs_done, pv_done, y_normed = (
            sem("scores_done"), sem("exp_done"), sem("probs_done"), sem("pv_done"), sem("y_normed"))
        hy_done, y2_sums, r2_done = sem("hy_done"), sem("y2_sums"), sem("r2_done")
        ln2_stats, ln2_scales, xn2_done = sem("ln2_stats"), sem("ln2_scales"), sem("xn2_done")
        h1_stored, xn2_stored = sem("h1_stored"), sem("xn2_stored")
        dve_step, pool_step = sem("dve_step"), sem("pool_step")
        exps_done, score_ready, score_stored = sem("exps_done"), sem("score_ready"), sem("score_stored")
        shifted = sem("shifted")
        scoreT_filled, counts_ready, counts_summed = sem("scoreT_filled"), sem("counts_ready"), sem("counts_summed")
        offs_ready, offs_summed, pos_ready, posT_filled, pos_copied = (
            sem("offs_ready"), sem("offs_summed"), sem("pos_ready"), sem("posT_filled"), sem("pos_copied"))
        phase2_init = sem("phase2_init")
        onehot_ready, onehot_used, list_filled, list_done = (
            sem("onehot_ready"), sem("onehot_used"), sem("list_filled"), sem("list_done"))
        idx_ready = sem("idx_ready")
        gathered = [sem(f"gathered{k}") for k in range(2)]
        scattered = [sem(f"scattered{k}") for k in range(2)]
        expert_in = [sem(f"expert_in{k}") for k in range(2)]
        fb2_in = sem("fb2_in")
        filled2 = [sem(f"filled2_{k}") for k in range(4)]
        evacuated2 = [sem(f"evacuated2_{k}") for k in range(4)]
        contrib_done = sem("contrib_done")

        FRONT_A = [("tok1", m) for m in range(KC)]
        FRONT_B = [("tok2", b) for b in range(2)]
        FRONT_C = [("xsT", c) for c in range(KC)] + [("qk", 0), ("qk", 1), ("v", 0), ("qk", 2), ("qk", 3), ("v", 1)]
        QKT = [("qkT", c) for c in range(H // 2)]
        ORDER = {
            "first": FRONT_A + FRONT_B + FRONT_C + QKT,
            "body": [("yT", 0), ("yT", 1)] + FRONT_A + [("wo", 0), ("wo", 1)] + FRONT_B + [("y2T", 0), ("y2T", 1)]
                    + [("w1", m) for m in range(4)] + FRONT_C + [("w1", m) for m in range(4, 8)] + QKT
                    + [("w2", 0), ("w2", 1), ("x2T", 0), ("x2T", 1), ("rt", 0), ("rt", 1)],
            "last": [("yT", 0), ("yT", 1), ("wo", 0), ("wo", 1), ("y2T", 0), ("y2T", 1)]
                    + [("w1", m) for m in range(8)]
                    + [("w2", 0), ("w2", 1), ("x2T", 0), ("x2T", 1), ("rt", 0), ("rt", 1)],
        }
        nf, nb = len(ORDER["first"]), len(ORDER["body"])
        assert nf % 2 == 0 and nb % 2 == 0

        class Part:
            def __init__(self, kind, i):
                self.kind, self.i, self.order = kind, i, ORDER[kind]
                self.base = 0 if kind == "first" else nf // 2 + (i - 1) * (nb // 2)

            def bank(self, *key):
                return self.order.index(key) % 2

            def count(self, *key):
                return self.base + (self.order.index(key) // 2 + 1)

            def wait_filled(self, eng, *key):
                eng.wait_ge(filled[self.bank(*key)], self.count(*key))

            def wait_evacuated(self, eng, *key):
                eng.wait_ge(evacuated[self.bank(*key)], self.count(*key))

            def wait_free(self, eng, *key):
                n = self.order.index(key)
                if self.kind != "first" or n >= 2:
                    eng.wait_ge(evacuated[n % 2], self.base + n // 2)

            def g(self, *key):
                return G[self.bank(*key)]

        pe = nc.tensor
        NG = H

        def pe_block(part, key, ins):
            ins.then_inc(filled[part.bank(*key)], 1)

        def pe_transposes(part, key, src):
            part.wait_free(pe, *key)
            for t in range(NT):
                last = pe.transpose(part.g(*key)[:, t * T:(t + 1) * T], src(t), ident[0:T, 0:T])
            pe_block(part, key, last)

        def pe_tok1(part, j):
            for b in range(2):
                pe.wait_ge(img_in[b], 16 * 2 * C * (j + 1))
            for m in range(KC):
                part.wait_free(pe, "tok1", m)
                for b in range(2):
                    for q in range(HALF):
                        last = pe.matmul(part.g("tok1", m)[:, b * NP_:(b + 1) * NP_], w1t[:, q, m * 128:(m + 1) * 128],
                                         img[b][:, q:q + PS * (NP_ - 1) + 1:PS], start=q == 0, stop=q == HALF - 1)
                pe_block(part, ("tok1", m), last)

        def pe_tok2(part, j):
            for m in range(KC):
                part.wait_evacuated(pe, "tok1", m)
            for b in range(2):
                part.wait_free(pe, "tok2", b)
                for half in range(2):
                    n = T if half == 0 else LASTP
                    at = b * NP_ + half * T
                    for m in range(KC):
                        last = pe.matmul(part.g("tok2", b)[0:n, half * D:(half + 1) * D], hid[:, m, at:at + n],
                                         w2t[:, m, :], start=m == 0, stop=m == KC - 1)
                pe_block(part, ("tok2", b), last)

        def pe_qkv(part, j):
            pe.wait_ge(xs_done, j + 1)
            for c in range(KC):
                pe_transposes(part, ("xsT", c), lambda t: xs[:, t, c * 128:(c + 1) * 128])
            for c in range(KC):
                part.wait_evacuated(pe, "xsT", c)
            for key in FRONT_C[KC:]:
                part.wait_free(pe, *key)
                if key[0] == "qk":
                    t = key[1]
                    for c in range(KC):
                        last = pe.matmul(part.g(*key)[0:T, :], xsT[:, c, t * T:(t + 1) * T], wqkv[:, c, 0:2 * D],
                                         start=c == 0, stop=c == KC - 1)
                else:
                    for half in range(2):
                        t = 2 * key[1] + half
                        for c in range(KC):
                            last = pe.matmul(part.g(*key)[0:T, half * D:(half + 1) * D], xsT[:, c, t * T:(t + 1) * T],
                                             wqkv[:, c, 2 * D:], start=c == 0, stop=c == KC - 1)
                pe_block(part, key, last)

        def pe_qkT(part, j):
            pe.wait_ge(qk_normed, j + 1)
            for key in QKT:
                part.wait_free(pe, *key)
                dst = part.g(*key)[:, 0:W].bitcast(F16)
                for s in range(2):
                    for t in range(NT):
                        h = s * H + 2 * key[1]
                        last = pe.transpose(dst[:, s * W + t * T:s * W + (t + 1) * T],
                                            qkp[:, t, h:h + 2, :].rearrange("p h d -> p (h d)"), ident_h[:, :])
                pe_block(part, key, last)

        def pe_scores(part, j, g, first):
            b, pair = g // (H // 2), g % (H // 2)
            if b == 0:
                part.wait_evacuated(pe, "qkT", pair)
            if not (first and g < 2):
                pe.wait_ge(exp_done, NG * j + (g - 1))
            for hh in range(2):
                lo = HP * hh
                rows = slice(lo, lo + HP)
                o = b * S
                dst = SC[g % 2]
                pe.matmul(dst[0:T, hh, 0:S], qkT[rows, pair, 1, o:o + T], qkT[rows, pair, 0, o:o + S],
                          start=True, stop=True)
                last = pe.matmul(dst[0:T, hh, S:QW], qkT[rows, pair, 1, o + T:o + S], qkT[rows, pair, 0, o + T:o + S],
                                 start=True, stop=True)
            last.then_inc(scores_done, 1)

        def pe_pv(part, j, g, first):
            b, pair = g // (H // 2), g % (H // 2)
            pe.wait_ge(probs_done, NG * j + (g + 1))
            if pair == 0:
                if not (first and b == 0):
                    pe.wait_ge(y_normed, 2 * j + b)
                pe.matmul(Y[0][0:T, 0:H * HV], first_col[:, :], v1[:, 2 * b + 1, :, :].rearrange("p h d -> p (h d)"),
                          start=True, stop=False, skip_group_check=True)
            for hh in range(2):
                h = 2 * pair + hh
                cols = slice(h * HV, (h + 1) * HV)
                pe.matmul(Y[1][0:T, cols], pm[g % 2][:, hh, T:S], v1[:, 2 * b, h, :],
                          start=h == 0, stop=False, skip_group_check=True)
                pe.matmul(Y[1][0:T, cols], pm[g % 2][:, hh, S:QW], v1[:, 2 * b + 1, h, :],
                          start=False, stop=h == H - 1, skip_group_check=True)
                last = pe.matmul(Y[0][0:T, cols], pm[g % 2][:, hh, 0:T], v1[:, 2 * b, h, :],
                                 start=False, stop=h == H - 1, skip_group_check=True)
            last.then_inc(pv_done, 1)

        def pe_w1(part, m):
            if m == 0:
                for c in range(KC):
                    part.wait_evacuated(pe, "y2T", c)
            part.wait_free(pe, "w1", m)
            for c in range(KC):
                last = pe.matmul(part.g("w1", m)[:, 0:W], w1m[:, c, m * 128:(m + 1) * 128], yT[:, c, :],
                                 start=c == 0, stop=c == KC - 1)
            pe_block(part, ("w1", m), last)

        def pe_w2(part, q):
            t, b = q // 2, q // 4
            if q == 0:
                for m in range(MC - 2, MC):
                    part.wait_evacuated(pe, "w1", m)
            if q % 4 == 0:
                part.wait_free(pe, "w2", b)
            for m in range(4 * (q % 2), 4 * (q % 2) + 4):
                last = pe.matmul(part.g("w2", b)[0:T, (t % 2) * D:(t % 2 + 1) * D], hT[:, m, t * T:(t + 1) * T],
                                 w2m[:, m, :], start=m == 0, stop=m == MC - 1)
            if q % 4 == 3:
                pe_block(part, ("w2", b), last)

        def pe_attention(part, j, first):
            for g in range(NG + 1):
                if g < NG:
                    pe_scores(part, j, g, first)
                    if not first:
                        if g % 2 == 0:
                            pe_w2(part, g // 2)
                if g:
                    pe_pv(part, j, g - 1, first)

        def pe_tail_a(part, j):
            pe.wait_ge(y_normed, 2 * (j + 1))
            for c in range(KC):
                pe_transposes(part, ("yT", c), lambda t: yn[:, t, c * 128:(c + 1) * 128])

        def pe_tail_b(part, j):
            for c in range(KC):
                part.wait_evacuated(pe, "yT", c)
            for b in range(2):
                part.wait_free(pe, "wo", b)
                for half in range(2):
                    t = 2 * b + half
                    for c in range(KC):
                        last = pe.matmul(part.g("wo", b)[0:T, half * D:(half + 1) * D], yT[:, c, t * T:(t + 1) * T],
                                         wo[:, c, :], start=c == 0, stop=c == KC - 1)
                pe_block(part, ("wo", b), last)

        def pe_tail_c(part, j):
            for b in range(2):
                part.wait_evacuated(pe, "wo", b)
            for c in range(KC):
                pe_transposes(part, ("y2T", c), lambda t: y2[:, t, c * 128:(c + 1) * 128])

        def pe_router(part, j):
            pe.wait_ge(xn2_done, j + 2)
            for c in range(KC):
                pe_transposes(part, ("x2T", c), lambda t: xn2[:, t, c * 128:(c + 1) * 128])
            for c in range(KC):
                part.wait_evacuated(pe, "x2T", c)
            for b in range(2):
                part.wait_free(pe, "rt", b)
                for half in range(2):
                    t = 2 * b + half
                    for c in range(KC):
                        last = pe.matmul(part.g("rt", b)[0:T, half * NE:(half + 1) * NE], xsT[:, c, t * T:(t + 1) * T],
                                         wr[:, c, :], start=c == 0, stop=c == KC - 1)
                pe_block(part, ("rt", b), last)

        G2 = [G[0], G[1], SC[0][:, 0, :], SC[0][:, 1, :]]
        BLK = {**{("w1", m): m for m in range(MC)}, ("xT", 0): MC, ("xT", 1): MC + 1, ("w2", 0): MC + 2,
               ("w2", 1): MC + 3}
        NBLK = len(BLK)
        assert NBLK % 4 == 0

        def bank2(key):
            return (2 + BLK[key]) % 4

        def count2(n, key):
            return n * (NBLK // 4) + ((2 + BLK[key]) // 4 + 1)

        def wait_evacuated2(eng, n, key):
            eng.wait_ge(evacuated2[bank2(key)], count2(n, key) + 1)

        def wait_free2(eng, n, key):
            eng.wait_ge(evacuated2[bank2(key)], n * (NBLK // 4) + ((2 + BLK[key]) // 4 + 1))

        def wait_apart(eng):
            eng.wait_ge(pool_consts, 6)

        block = ctx.enter_context(nc.Block())

        @block.sync
        def _(sp):
            for half in range(2):
                for c in range(C):
                    src = tok_W1[c * PS * PS:(c + 1) * PS * PS, :].rearrange("(y x) d -> y x d", x=PS)
                    lo = half * KROW + c * PS
                    sp.dma_start(w1t[lo:lo + PS, :, :], src[:, half * HALF:(half + 1) * HALF, :]).then_inc(weights_in, 16)
            for dst, src in ((w2t, tok_W2), (wo, Wo), (w1m, W1), (w2m, W2), (wr, Wr)):
                sp.dma_start(dst[:, :, :], src.rearrange("(c p) n -> p c n", p=128)).then_inc(weights_in, 16)
            for k, src in enumerate((Wq, Wk, Wv)):
                sp.dma_start(wqkv[:, :, k * D:(k + 1) * D], src.rearrange("(c p) n -> p c n", p=128)).then_inc(weights_in, 16)
            sp.dma_start(b2t[:, :], tok_b2.partition_broadcast(T)).then_inc(weights_in, 16)

            def load_images(j):
                for b in range(2):
                    for half in range(2):
                        for c in range(C):
                            lo = half * KROW + c * PS
                            src = x[2 * j + b] if isinstance(j, int) else x[bass.ds(2 * j + b, 1)].rearrange("o c y x -> (o c) y x")
                            src = src[c].rearrange("(g r) x -> r g x", r=PS)
                            n = IMG - half * HALF
                            dst = img[b][lo:lo + PS, :].rearrange("p (g x) -> p g x", x=IMG)
                            sp.dma_start(dst[:, :, 0:n], src[:, :, half * HALF:]).then_inc(img_in[b], 16)

            def load_text(j):
                src = txt[2 * j:2 * j + 2] if isinstance(j, int) else txt[bass.ds(2 * j, 2)]
                sp.dma_start(h0[LASTP:T, 1:NT:2, :], src.rearrange("b s d -> s b d")).then_inc(text_in, 16)

            def store_h1(part, j):
                for b in range(2):
                    part.wait_evacuated(sp, "w2", b)
                dst = out_rows[bass.ds(j * W, W)] if not isinstance(j, int) else out_rows[j * W:(j + 1) * W]
                sp.dma_start(dst.rearrange("(t p) d -> p t d", p=T), hy[:, :, :]).then_inc(h1_stored, 16)

            def store_xn2(j):
                sp.wait_ge(xn2_done, j + 2)
                dst = xd[bass.ds(j * W, W), 0:D] if not isinstance(j, int) else xd[j * W:(j + 1) * W, 0:D]
                sp.dma_start(dst.rearrange("(t p) d -> p t d", p=T), xn2[:, :, :]).then_inc(xn2_stored, 16)

            load_images(0)
            load_text(0)
            sp.wait_ge(zrow_ready, 1)
            pitch = 2 * S - 1 + T
            sp.dma_start(bass.AP(zrow_d, 0, [[T * pitch, H], [pitch + 1, T], [1, 2 * S - 1]]),
                         zrow[:, :].unsqueeze(1).to_broadcast([H, T, 2 * S - 1])).then_inc(rows_out, 16)
            sp.dma_start(mrow_d[:, :], mrow[:, :]).then_inc(rows_out, 16)
            sp.wait_ge(rows_out, 32)
            toep = lambda h, n: bass.AP(zrow_d, h * T * pitch + S - 1, [[pitch, T], [T * pitch, H // 2], [1, n]])
            mx = lambda h, o, n: bass.AP(mrow_d, h * S + o, [[0, T], [S, H // 2], [1, n]])
            for k in range(2):
                h = k * (H // 2)
                m = mtmp[k][:, 0:H // 2 * QW].rearrange("p (h q) -> p h q", q=QW)
                sp.dma_start(bias_t[:, h:h + H // 2, 0:S], toep(h, S)).then_inc(toeplitz_in, 16)
                sp.dma_start(bias_t[:, h:h + H // 2, S:QW], toep(h, T)).then_inc(toeplitz_in, 16)
                sp.dma_start(m[:, :, 0:S], mx(h, 0, S)).then_inc(toeplitz_in, 16)
                sp.dma_start(m[:, :, S:QW], mx(h, T, T)).then_inc(toeplitz_in, 16)
            first = Part("first", 0)
            first.wait_filled(sp, "tok1", 1)
            load_images(1)
            with sp.Fori(1, PAIRS - 1) as i:
                part = Part("body", i)
                sp.wait_ge(hy_done, 2 * i)
                load_text(i)
                part.wait_filled(sp, "tok1", 1)
                load_images(i + 1)
                store_h1(part, i - 1)
                store_xn2(i - 1)
            i = PAIRS - 1
            part = Part("body", i)
            sp.wait_ge(hy_done, 2 * i)
            load_text(i)
            store_h1(part, i - 1)
            store_xn2(i - 1)
            store_h1(Part("last", PAIRS), PAIRS - 1)
            store_xn2(PAIRS - 1)
            sp.wait_ge(phase2_init, 1)
            for e in range(2):
                sp.dma_start(we1[e][:, :, :], fW1[e].rearrange("(c p) n -> p c n", p=128)).then_inc(expert_in[e], 16)
                sp.dma_start(we2[e][:, :, :], fW2[e].rearrange("(c p) n -> p c n", p=128)).then_inc(expert_in[e], 16)
            sp.dma_start(fb2b[:, :, :], fb2.partition_broadcast(T)).then_inc(fb2_in, 16)
            sp.wait_ge(score_ready, 1)
            sp.dma_start(xd[:, D:XW].rearrange("(t p) e -> p t e", p=T), score[:, :, :]).then_inc(score_stored, 16)
            for e in range(2, NE):
                n = (e - 2) * GROUPS + GROUPS - 1
                sp.wait_ge(filled2[bank2(("w2", 1))], count2(n, ("w2", 1)))
                sp.dma_start(we1[e % 2][:, :, :], fW1[e].rearrange("(c p) n -> p c n", p=128)).then_inc(expert_in[e % 2], 16)
                sp.dma_start(we2[e % 2][:, :, :], fW2[e].rearrange("(c p) n -> p c n", p=128)).then_inc(expert_in[e % 2], 16)
            sp.wait_ge(h1_stored, 16 * (PAIRS + 1))
            sp.wait_ge(xn2_stored, 16 * (PAIRS + 1))
            sp.wait_ge(score_stored, 16)

        @block.tensor
        def _(eng):
            pe.wait_ge(weights_in, 16 * 15)
            pe.wait_ge(pool_consts, 6)
            part = Part("first", 0)
            pe_tok1(part, 0)
            pe_tok2(part, 0)
            pe.wait_ge(setup_done, 1)
            pe_qkv(part, 0)
            pe_qkT(part, 0)
            pe_attention(part, 0, True)
            with eng.Fori(1, PAIRS) as i:
                part = Part("body", i)
                pe_tail_a(part, i - 1)
                pe_tok1(part, i)
                pe_tail_b(part, i - 1)
                pe_tok2(part, i)
                pe_tail_c(part, i - 1)
                for m in range(4):
                    pe_w1(part, m)
                pe_qkv(part, i)
                for m in range(4, MC):
                    pe_w1(part, m)
                pe_qkT(part, i)
                pe_attention(part, i, False)
                pe_router(part, i - 1)
            part = Part("last", PAIRS)
            pe_tail_a(part, PAIRS - 1)
            pe_tail_b(part, PAIRS - 1)
            pe_tail_c(part, PAIRS - 1)
            for m in range(MC):
                pe_w1(part, m)
            for q in range(8):
                pe_w2(part, q)
            pe_router(part, PAIRS - 1)

            pe.wait_ge(score_ready, 2)
            for g in range(GT):
                last = pe.transpose(SC[1][:, g // 4, (g % 4) * T:(g % 4 + 1) * T], by_group[:, g, :],
                                    ident[0:T, 0:T])
            last.then_inc(scoreT_filled, 1)
            with eng.Fori(0, 30) as k:
                pe.wait_ge(counts_ready, k + 1)
                pe.matmul(Y[1][:, 0:1], group_ones[:, :], cnt[:, 0:1], start=True, stop=True).then_inc(counts_summed, 1)
            pe.wait_ge(counts_ready, 31)
            pe.matmul(Y[1][:, 1:2], group_ones[:, :], cnt[:, 1:2], start=True, stop=True)
            pe.matmul(Y[1][:, 2:3], earlier_ones[:, :], cnt[:, 2:3], start=True, stop=True).then_inc(offs_summed, 1)
            pe.wait_ge(offs_ready, 1)
            pe.matmul(Y[1][:, 3:4], earlier_ones[:, :], cnt[:, 3:4], start=True, stop=True).then_inc(offs_summed, 1)
            pe.wait_ge(pos_ready, 1)
            for g in range(GT):
                last = pe.transpose(SC[1][0:T, g // 4, (g % 4) * 128:(g % 4 + 1) * 128], rank[:, g * T:(g + 1) * T],
                                    ident[:, :])
            last.then_inc(posT_filled, 1)

            def clear_list():
                pe.matmul(Y[0][0:T, 0:2 * SLOTC], zero_w[:, :], iota_b[:, 0:2 * SLOTC],
                          start=True, stop=False, skip_group_check=True)

            def list_part(k, n):
                pe.wait_ge(onehot_ready, n + 1)
                for t in range(LT):
                    last = pe.matmul(Y[0][0:T, 0:2 * SLOTC], oh_b[k][:, t, :],
                                     oh_a[k][:, t, :, :].rearrange("p a b -> p (a b)"),
                                     start=False, stop=False, skip_group_check=True)
                last.then_inc(onehot_used, 1)

            def row_transposes(k, banks):
                for c in range(KC):
                    for t in range(NT):
                        last = pe.transpose(G2[banks[c]][:, t * T:(t + 1) * T], xg[k][:, t, c * 128:(c + 1) * 128],
                                            ident[0:T, 0:T])
                    last.then_inc(filled2[banks[c]], 1)

            def w1_block(eb, n, m):
                key = ("w1", m)
                wait_free2(pe, n, key)
                for c in range(KC):
                    last = pe.matmul(G2[bank2(key)][:, 0:W], we1[eb][:, c, m * 128:(m + 1) * 128], xgT[:, c, :],
                                     start=c == 0, stop=c == KC - 1)
                last.then_inc(filled2[bank2(key)], 1)

            def group(eb, half_n, k):
                n = half_n * 2 + k
                for m in range(MC // 2):
                    w1_block(eb, n, m)
                list_part(k, n + GROUPS)
                for m in range(MC // 2, MC):
                    w1_block(eb, n, m)
                pe.wait_ge(gathered[1 - k], (half_n + (1 + k)) * (16 * NT))
                for c in range(KC):
                    wait_free2(pe, n, ("xT", c))
                row_transposes(1 - k, [bank2(("xT", c)) for c in range(KC)])
                for m in range(MC - 4, MC):
                    wait_evacuated2(pe, n, ("w1", m))
                for b in range(2):
                    key = ("w2", b)
                    wait_free2(pe, n, key)
                    for half in range(2):
                        t = 2 * b + half
                        for m in range(MC):
                            last = pe.matmul(G2[bank2(key)][0:T, half * D:(half + 1) * D],
                                             hTe[:, m, t * T:(t + 1) * T], we2[eb][:, m, :],
                                             start=m == 0, stop=m == MC - 1)
                    last.then_inc(filled2[bank2(key)], 1)
                for c in range(KC):
                    wait_evacuated2(pe, n, ("xT", c))

            pe.wait_ge(onehot_ready, 1)
            clear_list()
            for p in range(GROUPS):
                list_part(p % 2, p)
            pe.wait_ge(gathered[0], 16 * NT)
            row_transposes(0, [0, 1])
            for c in range(KC):
                pe.wait_ge(evacuated2[c], 2)
            with eng.Fori(0, NE // 2) as E:
                for eb in range(2):
                    e = E * 2 + eb
                    pe.wait_ge(expert_in[eb], (E + 1) * 32)
                    pe.wait_ge(list_done, e + 1)
                    clear_list()
                    with eng.Fori(0, GROUPS // 2) as q:
                        for k in range(2):
                            group(eb, e * (GROUPS // 2) + q, k)

        act = nc.scalar

        def act_evacuate(part, key, dst, cols=W):
            part.wait_filled(act, *key)
            act.copy(dst, part.g(*key)[0:dst.shape[0], 0:cols]).then_inc(evacuated[part.bank(*key)], 1)

        @block.scalar
        def _(eng):
            with nc.allow_non_contiguous_dma(reason="small vectors of weights"):
                act.dma_start(relb[:, :], rel_bias.rearrange("k h -> h k")).then_inc(consts_in, 16)
                act.dma_start(sc_col[:, :], scale.rearrange("(h o) -> h o", o=1)).then_inc(consts_in, 16)
                act.dma_start(sc_bc[:, :], scale.partition_broadcast(T)).then_inc(consts_in, 16)
                act.dma_start(lnw[:, 0, :], ln1_w.rearrange("(c p) -> p c", p=128)).then_inc(consts_in, 16)
                act.dma_start(lnw[:, 1, :], ln2_w.rearrange("(c p) -> p c", p=128)).then_inc(consts_in, 16)
                act.dma_start(b1t[:, :], tok_b1.rearrange("(c p) -> p c", p=128)).then_inc(consts_in, 16)
                for e in range(NE):
                    act.dma_start(fb1c[:, e, :], fb1[e].rearrange("(m p) -> p m", p=128)).then_inc(consts_in, 16)

            def qkT_evacuate(eng, part, c):
                part.wait_filled(eng, "qkT", c)
                eng.copy(qkT[:, c, :, :].rearrange("p s w -> p (s w)"),
                         part.g("qkT", c)[:, 0:W].bitcast(F16)).then_inc(evacuated[part.bank("qkT", c)], 1)

            def silu(part):
                for m in range(KC):
                    part.wait_filled(act, "tok1", m)
                    act.activation(hid[:, m, :], part.g("tok1", m)[:, 0:2 * NP_], ACT.Silu,
                                   bias=b1t[:, m:m + 1]).then_inc(evacuated[part.bank("tok1", m)], 1)

            def xs_and_qk(part, j):
                for c in range(KC):
                    act_evacuate(part, ("xsT", c), xsT[:, c, :])
                if part.kind != "first":
                    act.wait_ge(qk_normed, j)
                for t in range(NT):
                    act_evacuate(part, ("qk", t), qkraw[:, t, :], 2 * D)
                act.wait_ge(qk_scaled, j + 1)
                for t in range(NT):
                    for s, step in ((0, 2 * HD), (H, HD)):
                        src = qkraw[:, t, s * HD:(s + H) * HD].rearrange("p (h d) -> p h d", d=HD)
                        last = act.copy(qkp[:, t, s:s + H, 0:HD], src)
                        last = act.copy(qkp[:, t, s:s + H, step:step + HD], src)
                    last.then_inc(qk_high, 1)
                for c in range(0, H // 2, 2):
                    qkT_evacuate(act, part, c)

            def exps(part, j, first):
                for g in range(NG):
                    act.wait_ge(scores_done, NG * j + (g + 1))
                    if not (first and g < 2):
                        act.wait_ge(probs_done, NG * j + (g - 1))
                    act.activation(p0[g % 2][:, :, :], SC[g % 2][0:T, :, 0:QW], ACT.Exp).then_inc(exp_done, 1)

            def squares(part):
                for b in range(2):
                    part.wait_evacuated(act, "wo", b)
                    for half in range(2):
                        t = 2 * b + half
                        last = act.activation(junk[:, t, :], y2[:, t, :], ACT.Square, scale=D ** -0.5,
                                              accum_out=ss2[:, t:t + 1])
                last.then_inc(y2_sums, 1)

            def y2_transposed(part):
                for c in range(KC):
                    act_evacuate(part, ("y2T", c), yT[:, c, :])

            def relu(part, ms):
                for m in ms:
                    part.wait_filled(act, "w1", m)
                    act.activation(hT[:, m, :], part.g("w1", m)[:, 0:W], ACT.Relu).then_inc(evacuated[part.bank("w1", m)], 1)

            act.wait_ge(consts_in, 16 * (6 + NE))
            act.wait_ge(table_diff, 1)
            act.activation(bias_t[:, :, :], bias_t[:, :, :], ACT.Exp).then_inc(table_exp, 1)
            part = Part("first", 0)
            silu(part)
            xs_and_qk(part, 0)
            exps(part, 0, True)
            with eng.Fori(1, PAIRS) as i:
                part = Part("body", i)
                for c in range(KC):
                    act_evacuate(part, ("yT", c), yT[:, c, :])
                silu(part)
                squares(part)
                y2_transposed(part)
                relu(part, range(4))
                xs_and_qk(part, i)
                exps(part, i, False)
                for c in range(KC):
                    act_evacuate(part, ("x2T", c), xsT[:, c, :])
            part = Part("last", PAIRS)
            for c in range(KC):
                act_evacuate(part, ("yT", c), yT[:, c, :])
            squares(part)
            y2_transposed(part)
            relu(part, range(4))
            for c in range(KC):
                act_evacuate(part, ("x2T", c), xsT[:, c, :])

            act.wait_ge(shifted, 1)
            act.activation(score[:, :, :], score[:, :, :], ACT.Exp).then_inc(exps_done, 1)
            act.wait_ge(filled2[0], 1)
            act.copy(xgT[:, 0, :], G2[0][:, 0:W]).then_inc(evacuated2[0], 1)
            with eng.Fori(0, NE) as e:
                with eng.Fori(0, GROUPS) as g:
                    n = e * GROUPS + g
                    for m in range(MC):
                        key = ("w1", m)
                        act.wait_ge(filled2[bank2(key)], count2(n, key))
                        bias = fb1c[:, :, :].rearrange("p e m -> p (e m)")[:, bass.ds(e * MC + m, 1)]
                        act.activation(hTe[:, m, :], G2[bank2(key)][:, 0:W], ACT.Gelu,
                                       bias=bias).then_inc(evacuated2[bank2(key)], 1)
                    key = ("xT", 0)
                    act.wait_ge(filled2[bank2(key)], count2(n, key))
                    act.copy(xgT[:, 0, :], G2[bank2(key)][:, 0:W]).then_inc(evacuated2[bank2(key)], 1)

        dve = nc.vector

        @block.vector
        def _(eng):
            chain = Chain(dve, dve_step, lambda: wait_apart(dve))
            step = chain.step

            dve.wait_ge(pool_consts, 6)
            dve.tensor_scalar(diff_low[:, :], diff[:, :], NE - 1, None, ALU.bitwise_and)
            step(dve.tensor_scalar(difff[:, :], diff[:, :], 128.0, None, ALU.is_gt))
            step(dve.tensor_scalar(group_ones[:, :], diff_low[:, :], 0.0, None, ALU.is_equal))
            dve.tensor_tensor(earlier_ones[:, :], difff[:, :], group_ones[:, :], ALU.mult)
            dve.tensor_copy(iota_b[:, :], iota_i[:, :])
            dve.tensor_copy(tok_p[:, :], tok_pi[:, :])
            dve.memset(zrow[:, 0:S], -3.0e38)
            dve.memset(mrow[:, 0:1], 0.0)
            dve.wait_ge(consts_in, 16 * (6 + NE))
            step(dve.tensor_scalar(relb[:, :], relb[:, :], sc_col[:, 0:1], None, ALU.mult))
            for d, n, k in relative_bucket_runs(S, NBUCK, 128):
                last = dve.tensor_copy(zrow[:, S - 1 + d:S - 1 + d + n], relb[:, k:k + 1].to_broadcast([H, n]))
            step(last)
            dve.tensor_tensor_scan(mrow[:, 1:S], zrow[:, S:2 * S - 1], zrow[:, S:2 * S - 1], -3.0e38,
                                   ALU.max, ALU.max).then_inc(zrow_ready, 1)
            step(dve.tensor_scalar(shift[:, 0, :], sc_bc[:, :], -1.0, None, ALU.mult))
            step(dve.tensor_tensor(shift[:, 0, :], shift[:, 0, :], sc_bc[:, :], ALU.max))
            step(dve.tensor_scalar(shift[:, 1, :], shift[:, 0, :], -1.0, SAFE, ALU.mult, ALU.add))
            step(dve.tensor_scalar(shift[:, 1, :], shift[:, 1, :], 0.0, None, ALU.min))
            dve.memset(v1[:, :, :, :], 1.0)
            step(dve.memset(qkp[:, :, :, :], 0.0))
            for t in range(NT):
                dve.tensor_copy(qkp[:, t, 0:H, 3 * HD], shift[:, 1, :])
                last = dve.tensor_copy(sc_q[:, t, :], sc_bc[:, :])
            step(last)
            dve.memset(qkp[:, :, H:2 * H, 3 * HD:3 * HD + 1], 1.0)
            dve.memset(qkp[0:1, 0:NT:2, 0:H, 3 * HD:3 * HD + 1], 0.0)
            dve.tensor_copy(ident_h[:, :], ident[0:T, 0:T])
            dve.memset(sc_q[0:1, 0:NT:2, :], 0.0)
            dve.wait_ge(weights_in, 16 * 15)
            for c in range(KC):
                dve.tensor_scalar(wqkv[:, c, :], wqkv[:, c, :], lnw[:, 0, c:c + 1], None, ALU.mult)
                dve.tensor_scalar(w1m[:, c, :], w1m[:, c, :], lnw[:, 1, c:c + 1], None, ALU.mult)
            dve.wait_ge(toeplitz_in, 16 * 8)
            for k in range(2):
                hs = slice(k * (H // 2), (k + 1) * (H // 2))
                m = mtmp[k][:, 0:H // 2 * QW].rearrange("p (h q) -> p h q", q=QW)
                last = dve.tensor_tensor(bias_t[:, hs, :], bias_t[:, hs, :], m, ALU.subtract)
            last.then_inc(table_diff, 1)
            dve.wait_ge(table_exp, 1)
            dve.memset(bias_t[:, :, 0:1], 1.0).then_inc(setup_done, 1)

            def evacuate(part, key, dst, cols=W):
                part.wait_filled(dve, *key)
                dve.tensor_copy(dst, part.g(*key)[0:dst.shape[0], 0:cols]).then_inc(evacuated[part.bank(*key)], 1)

            def stats(src, mv, done):
                for t in range(NT):
                    last = dve.bn_stats(st[:, t, :], src[:, t, :])
                step(last, apart=True)
                for t in range(NT):
                    last = dve.bn_aggr(mv[:, t, :], st[:, t, :])
                last.then_inc(done, 1)

            def front_a(part, j, first):
                if not first:
                    dve.wait_ge(hy_done, 2 * j)
                for b in range(2):
                    part.wait_filled(dve, "tok2", b)
                    dve.tensor_tensor(h0[:, 2 * b, :], part.g("tok2", b)[0:T, 0:D], b2t[:, :], ALU.add)
                    dve.tensor_tensor(h0[0:LASTP, 2 * b + 1, :], part.g("tok2", b)[0:LASTP, D:2 * D],
                                      b2t[0:LASTP, :], ALU.add).then_inc(evacuated[part.bank("tok2", b)], 1)
                for b in range(2):
                    part.wait_evacuated(dve, "tok2", b)
                dve.wait_ge(text_in, 16 * (j + 1))
                stats(h0, mv1, ln1_stats)

            def front_b(part, j):
                dve.wait_ge(ln1_scales, j + 1)
                for t in range(NT):
                    last = dve.tensor_scalar(xs[:, t, :], h0[:, t, :], mv1[:, t, 0:1], lt[:, 5, t:t + 1],
                                             ALU.subtract, ALU.mult)
                last.then_inc(xs_done, 1)
                for t in range(NT):
                    dve.tensor_scalar(xa[:, t, :], h0[:, t, :], mv1[:, t, 0:1], lt[:, 1, t:t + 1],
                                      ALU.subtract, ALU.mult)

            def qk_norm(part, j):
                def sums(t):
                    part.wait_evacuated(dve, "qk", t)
                    step(dve.tensor_tensor(sqb[:, :], qkraw[:, t, :], qkraw[:, t, :], ALU.mult))
                    return dve.reduce_sum(ss[:, t, :], sqb[:, :].rearrange("p (h d) -> p h d", d=HD), AX.X)

                def values(b):
                    part.wait_filled(dve, "v", b)
                    src = part.g("v", b)[0:T, :].rearrange("p (t h d) -> p t h d", t=2, d=HD)
                    dve.tensor_copy(v1[:, 2 * b:2 * b + 2, :, 0:HD], src).then_inc(evacuated[part.bank("v", b)], 1)

                step(sums(0))
                values(0)
                step(sums(1))
                step(sums(2))
                values(1)
                step(sums(3))
                if part.kind != "first":
                    relu(part, [4])
                x_, r_ = ss[:, :, :].rearrange("p t h -> p (t h)"), rn[:, :, :].rearrange("p t h -> p (t h)")
                a_ = nwt[:, :]
                step(dve.tensor_scalar(x_, x_, RMS_EPS, None, ALU.add))
                step(dve.tensor_scalar(a_.bitcast(I32), x_.bitcast(I32), 1, None, ALU.arith_shift_right))
                step(dve.tensor_scalar(r_.bitcast(I32), a_.bitcast(I32), -1.0, float(0x5f3759df), ALU.mult, ALU.add))
                for _ in range(3):
                    step(dve.tensor_tensor(a_, r_, r_, ALU.mult))
                    step(dve.scalar_tensor_tensor(a_, a_, -0.5, x_, ALU.mult, ALU.mult))
                    step(dve.scalar_tensor_tensor(r_, a_, 1.5, r_, ALU.add, ALU.mult))
                step(dve.tensor_tensor(rn[:, :, 0:H], rn[:, :, 0:H], sc_q[:, :, :], ALU.mult))
                for t in range(NT):
                    q = qkraw[:, t, :].rearrange("p (h d) -> p h d", d=HD)
                    last = dve.tensor_tensor(q, q, rn[:, t, :].unsqueeze(2).to_broadcast([T, 2 * H, HD]), ALU.mult)
                last.then_inc(qk_scaled, 1)
                if part.kind != "first":
                    relu(part, [5, 6])
                for t in range(NT):
                    dve.wait_ge(qk_high, NT * j + (t + 1))
                    for s, at in ((0, HD), (H, 2 * HD)):
                        src = qkraw[:, t, s * HD:(s + H) * HD].rearrange("p (h d) -> p h d", d=HD)
                        last = dve.tensor_tensor(qkp[:, t, s:s + H, at:at + HD], src, qkp[:, t, s:s + H, 0:HD],
                                                 ALU.subtract)
                last.then_inc(qk_normed, 1)
                if part.kind != "first":
                    relu(part, [7])
                for c in range(1, H // 2, 2):
                    part.wait_filled(dve, "qkT", c)
                    dve.tensor_copy(qkT[:, c, :, :].rearrange("p s w -> p (s w)"),
                                    part.g("qkT", c)[:, 0:W].bitcast(F16)).then_inc(evacuated[part.bank("qkT", c)], 1)

            def normalise_outputs(j, b):
                dve.wait_ge(pv_done, NG * j + (NG // 2) * (b + 1))
                for half in range(2):
                    y = Y[half][0:T, 0:H * HV].rearrange("p (h d) -> p h d", d=HV)
                    last = dve.reciprocal(yrec[:, half, :], y[:, :, HD])
                step(last)
                for half in range(2):
                    y = Y[half][0:T, 0:H * HV].rearrange("p (h d) -> p h d", d=HV)
                    dst = yn[:, 2 * b + half, :].rearrange("p (h d) -> p h d", d=HD)
                    last = dve.tensor_tensor(dst, y[:, :, 0:HD],
                                             yrec[:, half, :].unsqueeze(2).to_broadcast([T, H, HD]), ALU.mult)
                last.then_inc(y_normed, 1)

            def relu(part, ms):
                for m in ms:
                    part.wait_filled(dve, "w1", m)
                    dve.tensor_scalar(hT[:, m, :], part.g("w1", m)[:, 0:W], 0.0, None,
                                      ALU.max).then_inc(evacuated[part.bank("w1", m)], 1)

            def mlp_out(part, j, b):
                dve.wait_ge(r2_done, j + 1)
                dve.wait_ge(hy_done, 2 * (j + 1))
                part.wait_filled(dve, "w2", b)
                for half in range(2):
                    t = 2 * b + half
                    last = dve.scalar_tensor_tensor(hy[:, t, :], part.g("w2", b)[0:T, half * D:(half + 1) * D],
                                                    r2[:, t:t + 1], hy[:, t, :], ALU.mult, ALU.add)
                last.then_inc(evacuated[part.bank("w2", b)], 1)
                if b == 1:
                    for bb in range(2):
                        part.wait_evacuated(dve, "w2", bb)
                    stats(hy, mv2, ln2_stats)

            def second_norm(part, j):
                dve.wait_ge(ln2_scales, j + 1)
                dve.wait_ge(xn2_stored, 16 * (j + 1))
                for t in range(NT):
                    last = dve.tensor_scalar(xn2[:, t, :], hy[:, t, :], mv2[:, t, 0:1], rstd2[:, t:t + 1],
                                             ALU.subtract, ALU.mult)
                last.then_inc(xn2_done, 1)

            def router_out(part, j):
                for b in range(2):
                    part.wait_filled(dve, "rt", b)
                    at = NT * j + 2 * b
                    dst = logits[:, at:at + 2, :] if isinstance(j, int) else logits[:, bass.ds(at, 2), :]
                    dve.tensor_copy(dst, part.g("rt", b)[0:T, 0:2 * NE].rearrange(
                        "p (t e) -> p t e", e=NE)).then_inc(evacuated[part.bank("rt", b)], 1)

            def tail(part, j):
                for b in range(2):
                    part.wait_filled(dve, "wo", b)
                    dve.tensor_tensor(y2[:, 2 * b:2 * b + 2, :], part.g("wo", b)[0:T, :].rearrange("p (t d) -> p t d", d=D),
                                      xa[:, 2 * b:2 * b + 2, :], ALU.add).then_inc(evacuated[part.bank("wo", b)], 1)

            def masked_probs(part, j, first):
                for g in range(NG):
                    pair = g % (H // 2)
                    dve.wait_ge(exp_done, NG * j + (g + 1))
                    if not (first and g < 2):
                        dve.wait_ge(pv_done, NG * j + (g - 1))
                    dve.tensor_tensor(pm[g % 2][:, :, :], p0[g % 2][:, :, :], bias_t[:, 2 * pair:2 * pair + 2, :],
                                      ALU.mult).then_inc(probs_done, 1)
                    if g == NG // 2:
                        normalise_outputs(j, 0)
                    if not first and g == 9:
                        mlp_out(part, j - 1, 0)
                normalise_outputs(j, 1)
                if not first:
                    mlp_out(part, j - 1, 1)

            part = Part("first", 0)
            front_a(part, 0, True)
            front_b(part, 0)
            qk_norm(part, 0)
            masked_probs(part, 0, True)
            with eng.Fori(1, PAIRS) as i:
                chain.enter(i - 1, 25)
                part = Part("body", i)
                tail(part, i - 1)
                front_a(part, i, False)
                front_b(part, i)
                qk_norm(part, i)
                masked_probs(part, i, False)
                second_norm(part, i - 1)
                router_out(part, i - 1)
            chain.leave(PAIRS - 1)
            j = PAIRS - 1
            part = Part("last", PAIRS)
            tail(part, j)
            relu(part, range(4, MC))
            mlp_out(part, j, 0)
            mlp_out(part, j, 1)
            second_norm(part, j)
            router_out(part, j)

            for b in range(2):
                part.wait_evacuated(dve, "rt", b)
            dve.wait_ge(h1_stored, 16 * (PAIRS + 1))
            dve.wait_ge(xn2_stored, 16 * (PAIRS + 1))
            dve.reduce_max(smax[:, :], logits[:, :, :], AX.X).then_inc(phase2_init, 1)
            dve.wait_ge(phase2_init, 1)
            dve.tensor_tensor(score[:, :, :], logits[:, :, :], smax[:, :].unsqueeze(2).to_broadcast([T, NTILES, NE]),
                              ALU.subtract).then_inc(shifted, 1)
            dve.memset(bitv[:, :], float(1 << 29))
            dve.memset(thr[:, :], 0)
            dve.memset(slot_a[:, NE, :], 0.0)
            dve.memset(slot_b[:, NE, :], -1.0)
            step(dve.memset(zero_w[:, :], 0.0))
            step(dve.tensor_copy(biti[:, :], bitv[:, :]))
            dve.wait_ge(exps_done, 1)
            step(dve.reduce_sum(smax[:, :], score[:, :, :], AX.X))
            step(dve.reciprocal(smax[:, :], smax[:, :]))
            dve.tensor_tensor(score[:, :, :], score[:, :, :], smax[:, :].unsqueeze(2).to_broadcast([T, NTILES, NE]),
                              ALU.mult).then_inc(score_ready, 1)
            dve.wait_ge(score_ready, 1)
            dve.tensor_copy(by_group[:, :, :].rearrange("p g (r e) -> p r g e", e=NE),
                            score[:, :, :].rearrange("p (r g) e -> p r g e", g=GT)).then_inc(score_ready, 1)

            dve.wait_ge(scoreT_filled, 1)
            for k in range(2):
                last = dve.tensor_copy(scoreT[:, k * 4 * T:(k + 1) * 4 * T], SC[1][:, k, 0:4 * T])
            step(last)
            with eng.Fori(0, 30) as k:
                chain.enter(k, 5)
                step(dve.tensor_tensor(cand[:, :], thr[:, :], biti[:, :], ALU.bitwise_or))
                dve.tensor_scalar(hit[:, :], scoreT[:, :], cand[:, :].bitcast(F32), None, ALU.is_ge, ALU.add,
                                  accum_out=cnt[:, 0:1]).then_inc(counts_ready, 1)
                dve.wait_ge(counts_summed, k + 1)
                step(dve.tensor_scalar(kept[:, :], Y[1][:, 0:1], float(CAP), bitv[:, 0:1], ALU.is_ge, ALU.mult))
                step(dve.tensor_tensor(thr[:, :], thr[:, :], kept[:, :], ALU.bitwise_or))
                step(dve.tensor_scalar(bitv[:, :], bitv[:, :], 0.5, None, ALU.mult))
                step(dve.tensor_copy(biti[:, :], bitv[:, :]))
            chain.leave(30)
            tf = thr[:, :].bitcast(F32)
            dve.tensor_scalar(above[:, :], scoreT[:, :], tf, None, ALU.is_gt, ALU.add, accum_out=cnt[:, 1:2])
            dve.tensor_scalar(equal[:, :], scoreT[:, :], tf, None, ALU.is_equal, ALU.add,
                              accum_out=cnt[:, 2:3]).then_inc(counts_ready, 1)
            dve.wait_ge(counts_ready, 31)
            step(dve.tensor_tensor_scan(rank[:, :], equal[:, :], equal[:, :], 0.0, ALU.add, ALU.max))
            dve.wait_ge(offs_summed, 1)
            step(dve.tensor_scalar(need[:, 0:1], Y[1][:, 1:2], -1.0, float(CAP), ALU.mult, ALU.add))
            step(dve.tensor_tensor(need[:, 1:2], need[:, 0:1], Y[1][:, 2:3], ALU.subtract))
            step(dve.scalar_tensor_tensor(hit[:, :], rank[:, :], need[:, 1:2], equal[:, :], ALU.is_le, ALU.mult))
            dve.scalar_tensor_tensor(above[:, :], above[:, :], 0.0, hit[:, :], ALU.add, ALU.add,
                                     accum_out=cnt[:, 3:4]).then_inc(offs_ready, 1)
            dve.wait_ge(offs_ready, 1)
            step(dve.tensor_tensor_scan(rank[:, :], above[:, :], above[:, :], 0.0, ALU.add, ALU.max))
            dve.wait_ge(offs_summed, 2)
            step(dve.scalar_tensor_tensor(rank[:, :], rank[:, :], Y[1][:, 3:4], above[:, :], ALU.add, ALU.mult))
            dve.tensor_scalar(rank[:, :], rank[:, :], -1.0, None, ALU.add).then_inc(pos_ready, 1)
            dve.wait_ge(posT_filled, 1)
            for k in range(2):
                src = SC[1][0:T, k, :].rearrange("p (g r e) -> p g r e", g=GT // 2, e=NE)
                dst = posi[:, :, :].rearrange("p (r g) e -> p g r e", g=GT)[:, k * (GT // 2):(k + 1) * (GT // 2)]
                last = dve.tensor_copy(dst, src)
            step(last)
            step(dve.tensor_scalar(posh[:, :, :], posi[:, :, :], SLOTC - 1, None, ALU.bitwise_and))
            dve.tensor_copy(slot_a[:, 0:NE, :], posh[:, :, :].rearrange("p t e -> p e t"))
            step(dve.tensor_scalar(posi[:, :, :], posi[:, :, :], SLOTC.bit_length() - 1, None, ALU.arith_shift_right))
            step(dve.tensor_copy(slot_b[:, 0:NE, :], posi[:, :, :].rearrange("p t e -> p e t")))

            flat_a = slot_a[:, :, :].rearrange("p e t -> p (e t)")
            flat_b = slot_b[:, :, :].rearrange("p e t -> p (e t)")

            def onehots(k, n, tile_at, wait=True):
                if wait:
                    dve.wait_ge(onehot_used, n - 1)
                bs = flat_b[:, bass.ds(n * LT, LT)].unsqueeze(2).to_broadcast([T, LT, T])
                as_ = flat_a[:, bass.ds(n * LT, LT)].unsqueeze(2).to_broadcast([T, LT, SLOTC])
                ts = iota_b[:, bass.ds(tile_at, LT)].unsqueeze(2).to_broadcast([T, LT, SLOTC])
                dve.tensor_tensor(oh_b[k][:, :, :], bs, iota_b[:, 0:T].unsqueeze(1).to_broadcast([T, LT, T]), ALU.is_equal)
                step(dve.tensor_tensor(eq_a[k][:, :, :], as_, iota_b[:, 0:SLOTC].unsqueeze(1).to_broadcast([T, LT, SLOTC]),
                                       ALU.is_equal))
                dve.tensor_scalar(oh_a[k][:, :, 0, :], eq_a[k][:, :, :], tok_p[:, 0:1], None, ALU.mult)
                dve.tensor_tensor(oh_a[k][:, :, 1, :], eq_a[k][:, :, :], ts, ALU.mult).then_inc(onehot_ready, 1)

            def close_list(e):
                dve.wait_ge(onehot_used, (e + 1) * GROUPS)
                step(dve.tensor_scalar(idx_t[:, :], Y[0][0:T, SLOTC:2 * SLOTC], float(T), None, ALU.mult))
                dst = idx_all[:, bass.ds(e * SLOTC, SLOTC)]
                dve.tensor_tensor(dst, idx_t[:, :], Y[0][0:T, 0:SLOTC], ALU.add).then_inc(list_done, 1)

            for p in range(GROUPS):
                onehots(p % 2, p, p * LT, wait=p >= 2)
            close_list(0)
            dve.wait_ge(filled2[1], 1)
            dve.tensor_copy(xgT[:, 1, :], G2[1][:, 0:W]).then_inc(evacuated2[1], 1)
            dve.wait_ge(fb2_in, 16)

            def group(e, half_n, k, q, last_of_expert):
                n = half_n * 2 + k
                onehots(k, n + GROUPS, (q * 2 + k) * LT)
                if last_of_expert:
                    close_list(e + 1)
                key = ("xT", 1)
                dve.wait_ge(filled2[bank2(key)], count2(n, key))
                dve.tensor_copy(xgT[:, 1, :], G2[bank2(key)][:, 0:W]).then_inc(evacuated2[bank2(key)], 1)
                for b in range(2):
                    key = ("w2", b)
                    dve.wait_ge(filled2[bank2(key)], count2(n, key))
                    bias = fb2b[:, :, :].rearrange("p e d -> p (e d)")[:, bass.ds(e * D, D)]
                    dve.tensor_tensor(biased[:, :, :], G2[bank2(key)][0:T, :].rearrange("p (t d) -> p t d", d=D),
                                      bias.unsqueeze(1).to_broadcast([T, 2, D]), ALU.add).then_inc(evacuated2[bank2(key)], 1)
                    wait_evacuated2(dve, n, key)
                    for half in range(2):
                        t = 2 * b + half
                        last = dve.tensor_scalar(contrib[k][:, t, :], biased[:, half, :],
                                                 xg[k][:, t, bass.ds(e + D, 1)], None, ALU.mult)
                    if b == 1:
                        last.then_inc(contrib_done, 1)
                    else:
                        step(last)

            with eng.Fori(0, NE) as e:
                chain.enter(e, 2 * GROUPS + 1)
                with eng.Fori(0, GROUPS // 2 - 1) as q:
                    chain.enter(q, 4)
                    for k in range(2):
                        group(e, e * (GROUPS // 2) + q, k, q, False)
                chain.leave(GROUPS // 2 - 1)
                for k in range(2):
                    group(e, e * (GROUPS // 2) + (GROUPS // 2 - 1), k, GROUPS // 2 - 1, k == 1)
            chain.leave(NE)

        pool = nc.gpsimd

        @block.gpsimd
        def _(eng):
            chain = Chain(pool, pool_step, lambda: wait_apart(pool))
            step = chain.step
            for s in (xn2_stored, h1_stored):
                pool.sem_inc(s, 16)
            for s in (xn2_done, contrib_done, *evacuated2):
                pool.sem_inc(s, 1)
            step(pool.memset(ident[:, :], 0.0))
            pool.affine_select(out=ident[:, :], in_=ident[:, :], compare_op=ALU.not_equal, fill=1.0, base=0,
                               pattern=[[-1, 128]], channel_multiplier=1).then_inc(pool_consts, 1)
            step(pool.memset(first_col[:, :], 0.0))
            pool.memset(first_col[:, 0:1], 1.0).then_inc(pool_consts, 1)
            pool.memset(ln_eps[:, :], LN_EPS)
            pool.memset(rms_eps[:, :], RMS_EPS)
            pool.memset(neg_half[:, :], -0.5).then_inc(pool_consts, 1)
            pool.iota(diff[:, :], [[1, 128]], base=128, channel_multiplier=-1).then_inc(pool_consts, 1)
            pool.iota(iota_i[:, :], [[1, 128]], base=0, channel_multiplier=0).then_inc(pool_consts, 1)
            pool.iota(tok_pi[:, :], [[1, 1]], base=0, channel_multiplier=1).then_inc(pool_consts, 1)
            pool.wait_ge(pool_consts, 6)

            def rsqrt(dst, src, n):
                return pool.tensor_tensor(dst, src, neg_half[0:T, 0:n], ALU.pow)

            def first_norm(j):
                pool.wait_ge(ln1_stats, j + 1)
                step(pool.tensor_tensor(lt[:, 0, :], mv1[:, :, 1], ln_eps[:, 0:NT], ALU.add))
                step(rsqrt(lt[:, 1, :], lt[:, 0, :], NT))
                step(pool.tensor_tensor(lt[:, 2, :], lt[:, 1, :], lt[:, 1, :], ALU.mult))
                step(pool.tensor_tensor(lt[:, 2, :], lt[:, 2, :], mv1[:, :, 1], ALU.mult))
                step(pool.tensor_tensor(lt[:, 3, :], lt[:, 2, :], rms_eps[:, 0:NT], ALU.add))
                step(rsqrt(lt[:, 4, :], lt[:, 3, :], NT))
                pool.tensor_tensor(lt[:, 5, :], lt[:, 4, :], lt[:, 1, :], ALU.mult).then_inc(ln1_scales, 1)

            def residuals(part, j):
                pool.wait_ge(h1_stored, 16 * (j + 1))
                pool.wait_ge(xn2_done, j + 1)
                for b in range(2):
                    part.wait_evacuated(pool, "wo", b)
                    ts = slice(2 * b, 2 * b + 2)
                    pool.tensor_tensor(hy[:, ts, :], y2[:, ts, :], h0[:, ts, :], ALU.add).then_inc(hy_done, 1)
                pool.wait_ge(y2_sums, j + 1)
                step(pool.tensor_tensor(ss2[:, :], ss2[:, :], rms_eps[:, 0:NT], ALU.add))
                rsqrt(r2[:, :], ss2[:, :], NT).then_inc(r2_done, 1)

            def second_norm(j):
                pool.wait_ge(ln2_stats, j + 1)
                step(pool.tensor_tensor(rstd2[:, :], mv2[:, :, 1], ln_eps[:, 0:NT], ALU.add))
                rsqrt(rstd2[:, :], rstd2[:, :], NT).then_inc(ln2_scales, 1)

            first_norm(0)
            with eng.Fori(1, PAIRS) as i:
                chain.enter(i - 1, 8)
                residuals(Part("body", i), i - 1)
                first_norm(i)
                second_norm(i - 1)
            chain.leave(PAIRS - 1)
            residuals(Part("last", PAIRS), PAIRS - 1)
            second_norm(PAIRS - 1)

            def gather(n, k):
                step(pool.tensor_copy(idx_cur[k][:, :], idx_all[:, bass.ds(n * NT, NT)]), apart=True)
                for t in range(NT):
                    pool.indirect_dma_start(
                        out=xg[k][:, t, :], out_offset=None, in_=xd[:, :],
                        in_offset=bass.IndirectOffsetOnAxis(ap=idx_cur[k][:, t:t + 1], axis=0)).then_inc(gathered[k], 16)

            def scatter(n, k):
                if isinstance(n, int):
                    pool.wait_ge(contrib_done, n + 2)
                else:
                    done = pool.snap(pool.to_reg(n + 2))
                    wait_apart(pool)
                    pool.wait_ge(contrib_done, done)
                for t in range(NT):
                    pool.indirect_dma_start(
                        out=out_rows, out_offset=bass.IndirectOffsetOnAxis(ap=idx_cur[k][:, t:t + 1], axis=0),
                        in_=contrib[k][:, t, :], in_offset=None, compute_op=ALU.add).then_inc(scattered[k], 16)

            def group(half_n, k):
                n = half_n * 2 + k
                pool.wait_ge(contrib_done, n + 1)
                before = (half_n + k) * (16 * NT)
                if not isinstance(before, int) or before:
                    pool.wait_ge(scattered[1 - k], before)
                gather(n + 1, 1 - k)
                scatter(n, k)

            def expert(e, first):
                if not first:
                    former = pool.snap(pool.to_reg(e * (GROUPS // 2 * 16 * NT)))
                    wait_apart(pool)
                    for k in range(2):
                        pool.wait_ge(scattered[k], former)
                else:
                    for k in range(2):
                        group(0, k)
                peeled = int(first)
                with eng.Fori(peeled, GROUPS // 2 - 1) as q:
                    chain.enter(q - peeled, 2)
                    for k in range(2):
                        group(e * (GROUPS // 2) + q, k)
                chain.leave(GROUPS // 2 - 1 - peeled)
                half_n = e * (GROUPS // 2) + (GROUPS // 2 - 1)
                group(half_n, 0)
                pool.wait_ge(list_done, e + 2)
                group(half_n, 1)

            pool.wait_ge(score_stored, 16)
            pool.wait_ge(h1_stored, 16 * (PAIRS + 1))
            pool.wait_ge(xn2_stored, 16 * (PAIRS + 1))
            pool.wait_ge(list_done, 1)
            gather(0, 0)
            expert(0, True)
            with eng.Fori(1, NE) as e:
                chain.enter(e - 1, GROUPS)
                expert(e, False)
            chain.leave(NE - 1)
            for k in range(2):
                pool.wait_ge(scattered[k], NE * GROUPS // 2 * 16 * NT)
            pool.wait_ge(gathered[0], (NE * GROUPS // 2 + 1) * 16 * NT)


_INS = ['x', 'txt', 'L0_tok_W1', 'L0_tok_b1', 'L0_tok_W2', 'L0_tok_b2', 'L0_attn_ln1_w', 'L0_attn_Wq', 'L0_attn_Wk',
        'L0_attn_Wv', 'L0_attn_rel_bias', 'L0_attn_scale', 'L0_attn_Wo', 'L0_attn_ln2_w', 'L0_attn_W1', 'L0_attn_W2',
        'L0_ffn_Wr', 'L0_ffn_W1', 'L0_ffn_b1', 'L0_ffn_W2', 'L0_ffn_b2']
_OUTS = [((64, 228, 256), 'float32')]


def kernel(**inputs):
    import numpy as _np
    import concourse.bacc as _bacc
    from concourse import mybir as _mybir
    from concourse.bass_utils import run_bass_kernel_spmd as _run

    nc = _bacc.Bacc("TRN2", target_bir_lowering=False, num_devices=1)
    arrays, args = {}, []
    for name in _INS:
        a = _np.ascontiguousarray(inputs[name])
        arrays[f"in_{name}_dram"] = a
        args.append(nc.dram_tensor(f"in_{name}_dram", a.shape, _mybir.dt.from_np(a.dtype), kind="ExternalInput").ap())
    for i, (shape, dtype) in enumerate(_OUTS):
        dt = _mybir.dt.from_np(_np.dtype(dtype))
        args.append(nc.dram_tensor(f"out_{i}_dram", shape, dt, kind="ExternalOutput").ap())
    early_fusion_kernel(nc, *args)
    r = _run(nc, [arrays], core_ids=[0])
    return r.results[0]["out_0_dram"]
```

```python
import concourse.bass as bass
from concourse import mybir
from contextlib import ExitStack
import numpy as np


def relative_bucket_runs(distances, buckets, max_distance):
    exact = buckets // 2
    n = np.arange(1, distances, dtype=np.int32)
    large = exact + (np.log(n.astype(np.float32) / np.float32(exact))
                     / np.float32(np.log(max_distance / exact)) * np.float32(buckets - exact)).astype(np.int32)
    bucket = np.where(n < exact, n, np.minimum(large, buckets - 1))
    runs = []
    for d, k in zip(n.tolist(), bucket.tolist()):
        if runs and runs[-1][2] == k:
            runs[-1][1] += 1
        else:
            runs.append([d, 1, k])
    return runs


class Chain:
    def __init__(self, eng, sem, wait_apart):
        self.wait_apart = wait_apart
        self.eng, self.sem, self.base, self.n, self.loops = eng, sem, 0, 0, []

    def step(self, ins, apart=False):
        ins.then_inc(self.sem, 1)
        self.n += 1
        value = self.base + self.n
        if apart and not isinstance(value, int):
            value = self.eng.snap(self.eng.to_reg(value))
            self.wait_apart()
        self.eng.wait_ge(self.sem, value)

    def enter(self, trip, steps):
        self.loops.append((self.base, self.n, steps))
        self.base, self.n = trip * steps + (self.base + self.n), 0

    def leave(self, trips):
        base, n, steps = self.loops.pop()
        assert self.n == steps, (self.n, steps)
        self.base, self.n = base, n + trips * steps


def early_fusion_kernel(nc, x, txt, tok_W1, tok_b1, tok_W2, tok_b2, ln1_w, Wq, Wk, Wv, rel_bias, scale, Wo,
                        ln2_w, W1, W2, Wr, fW1, fb1, fW2, fb2, out):
    F32, BF16, F16, I32, U32 = mybir.dt.float32, mybir.dt.bfloat16, mybir.dt.float16, mybir.dt.int32, mybir.dt.uint32
    ALU, ACT, AX = mybir.AluOpType, mybir.ActivationFunctionType, mybir.AxisListType

    B, C, IMG, _ = x.shape
    TXT, D = txt.shape[1], txt.shape[2]
    PS = 16
    GP = IMG // PS
    NP_ = GP * GP
    S = NP_ + TXT
    T = S // 2
    LASTP = NP_ - T
    N = B * S
    PAIRS = B // 2
    NT = 4
    W = NT * T
    NTILES = N // T
    H = scale.shape[0]
    HD = D // H
    HV = HD + 1
    HP = 64
    NBUCK = rel_bias.shape[0]
    KC = D // 128
    HID = W1.shape[1]
    MC = HID // 128
    NE = Wr.shape[1]
    CAP = max(4, -(-2 * N // NE))
    GROUPS = CAP // W
    SLOTC = CAP // T
    R = 128 // NE
    GT = NTILES // R
    SEG = GT * T
    KROW = C * PS
    HALF = PS // 2
    QW = S + T
    XW = D + NE
    LN_EPS, RMS_EPS = 1e-5, 1e-6
    LT = NTILES // GROUPS
    SAFE = 75.0
    assert CAP == GROUPS * W and T <= 128 and LASTP > 0 and NTILES == R * GT and SLOTC == 32

    xd = nc.dram_tensor("xn_rows", (N, XW), F32)
    zrow_d = nc.dram_tensor("bias_by_distance", (H, T, 2 * S - 1 + T), F32)
    mrow_d = nc.dram_tensor("bias_row_maximum", (H, S), F32)
    out_rows = out.rearrange("b s d -> (b s) d")

    ctx = ExitStack()
    with ctx:
        def sb(name, shape, dt=F32, stack=ctx):
            return stack.enter_context(nc.sbuf_tensor(name, shape, dt))

        def sem(name):
            return ctx.enter_context(nc.semaphore(name))

        logits = sb("logits", [T, NTILES, NE])
        ident = sb("ident", [128, 128])
        group_ones = sb("group_ones", [128, 128])
        earlier_ones = sb("earlier_ones", [128, 128])
        diff = sb("diff", [128, 128], I32)
        difff = sb("difff", [128, 128])
        neg_half = sb("neg_half", [T, 128])
        ln_eps = sb("ln_eps", [T, 128])
        rms_eps = sb("rms_eps", [T, 128])
        tok_p = sb("tok_p", [T, 1])
        tok_pi = sb("tok_pi", [T, 1], I32)
        diff_low = sb("diff_low", [128, 128], I32)
        iota_i = sb("iota_i", [T, 128], I32)
        iota_b = sb("iota_b", [T, 128], BF16)
        first_col = sb("first_col", [T, T])
        fb1c = sb("fb1c", [128, NE, MC])

        p1 = ExitStack()

        def s1(name, shape, dt=F32):
            return sb(name, shape, dt, p1)

        w1t = s1("w1t", [2 * KROW, HALF, D])
        w2t = s1("w2t", [128, KC, D])
        b1t = s1("b1t", [128, KC])
        b2t = s1("b2t", [T, D])
        wqkv = s1("wqkv", [128, KC, 3 * D])
        wo = s1("wo", [128, KC, D])
        w1m = s1("w1m", [128, KC, HID])
        w2m = s1("w2m", [128, MC, D])
        wr = s1("wr", [128, KC, NE])
        lnw = s1("lnw", [128, 2, KC])
        relb = s1("relb", [H, NBUCK])
        sc_col = s1("sc_col", [H, 1])
        zrow = s1("zrow", [H, 2 * S - 1])
        mrow = s1("mrow", [H, S])
        bias_t = s1("bias_t", [T, H, QW])
        sc_bc = s1("sc_bc", [T, H])
        sc_q = s1("sc_q", [T, NT, H])
        shift = s1("shift", [T, 2, H])
        img = [s1(f"img{b}", [2 * KROW, GP * IMG]) for b in range(2)]
        hid = s1("hid", [128, KC, 2 * NP_])
        h0 = s1("h0", [T, NT, D])
        xa = s1("xa", [T, NT, D])
        xs = s1("xs", [T, NT, D])
        xsT = s1("xsT", [128, KC, W])
        qkraw = s1("qkraw", [T, NT, 2 * D])
        sqb = s1("sqb", [T, 2 * D])
        logitsT = sqb[0:NE, 0:W]
        ss = s1("ss", [T, NT, 2 * H])
        rn = s1("rn", [T, NT, 2 * H])
        qkp = s1("qkp", [T, NT, 2 * H, HP], F16)
        qkT = s1("qkT", [128, H // 2, 2, W], F16)
        v1 = s1("v1", [T, NT, H, HV])
        p0 = [s1(f"p0_{k}", [T, 2, QW]) for k in range(2)]
        pm = [s1(f"pm_{k}", [T, 2, QW]) for k in range(2)]
        nwt = s1("nwt", [T, NT * 2 * H])
        ident_h = s1("ident_h", [T, T], F16)
        yrec = s1("yrec", [T, 2, H])
        yn = s1("yn", [T, NT, D])
        yT = s1("yT", [128, KC, W])
        y2 = yn
        h0_copy = s1("h0_copy", [T, NT, D])
        hy = s1("hy", [T, NT, D])
        junk = s1("junk", [T, NT, D], BF16)
        hT = s1("hT", [128, MC, W])
        xn2 = s1("xn2", [T, NT, D])
        st = s1("st", [T, NT, 6])
        mv1 = s1("mv1", [T, NT, 2])
        mv2 = s1("mv2", [T, NT, 2])
        lt = s1("lt", [T, 6, NT])
        ss2 = s1("ss2", [T, NT])
        r2 = s1("r2", [T, NT])
        rstd2 = s1("rstd2", [T, NT])
        mtmp = [hT[0:T, :, :].rearrange("p m w -> p (m w)"), qkT[0:T, :, :, :].rearrange("p c s w -> p (c s w)").bitcast(F32)]
        p1.close()

        def s2(name, shape, dt=F32):
            return sb(name, shape, dt)

        score = s2("score", [T, NTILES, NE])
        by_group = s2("by_group", [T, GT, R * NE])
        smax = s2("smax", [T, NTILES])
        scoreT = s2("scoreT", [128, SEG])
        hit = s2("hit", [128, SEG])
        above = s2("above", [128, SEG])
        equal = s2("equal", [128, SEG])
        rank = s2("rank", [128, SEG])
        bitv = s2("bitv", [128, 1])
        biti = s2("biti", [128, 1], I32)
        cand = s2("cand", [128, 1], I32)
        kept = s2("kept", [128, 1], I32)
        thr = s2("thr", [128, 1], I32)
        cnt = s2("cnt", [128, 4])
        need = s2("need", [128, 2])
        posi = s2("posi", [T, NTILES, NE], I32)
        posh = s2("posh", [T, NTILES, NE], I32)
        slot_a = s2("slot_a", [T, NE + 1, NTILES], BF16)
        slot_b = s2("slot_b", [T, NE + 1, NTILES], BF16)
        oh_b = [s2(f"oh_b{k}", [T, LT, T], BF16) for k in range(2)]
        oh_a = [s2(f"oh_a{k}", [T, LT, 2, SLOTC], BF16) for k in range(2)]
        eq_a = [s2(f"eq_a{k}", [T, LT, SLOTC], BF16) for k in range(2)]
        zero_w = s2("zero_w", [T, T], BF16)
        idx_t = s2("idx_t", [T, 32])
        idx_all = s2("idx_all", [T, (NE + 1) * 32], U32)
        idx_cur = [s2(f"idx_cur{k}", [T, NT], U32) for k in range(2)]
        we1 = [s2(f"we1_{k}", [128, KC, HID]) for k in range(2)]
        we2 = [s2(f"we2_{k}", [128, MC, D]) for k in range(2)]
        fb2b = s2("fb2b", [T, NE, D])
        xg = [s2(f"xg{k}", [T, NT, XW]) for k in range(2)]
        xgT = s2("xgT", [128, KC, W])
        hTe = s2("hTe", [128, MC, W])
        biased = s2("biased", [T, 2, D])
        contrib = [s2(f"contrib{k}", [T, NT, D]) for k in range(2)]

        def pb(name, shape):
            return ctx.enter_context(nc.psum_tensor(name, shape, F32))

        G = [pb(f"G{k}", [128, 512]) for k in range(2)]
        SC = [pb(f"SC{k}", [128, 2, 512]) for k in range(2)]
        Y = [pb(f"Y{k}", [128, 512]) for k in range(2)]

        weights_in, consts_in = sem("weights_in"), sem("consts_in")
        pool_consts = sem("pool_consts")
        zrow_ready, rows_out, toeplitz_in = sem("zrow_ready"), sem("rows_out"), sem("toeplitz_in")
        table_diff, table_exp, setup_done = sem("table_diff"), sem("table_exp"), sem("setup_done")
        img_in = [sem(f"img_in{b}") for b in range(2)]
        text_in = sem("text_in")
        filled = [sem(f"filled{k}") for k in range(2)]
        evacuated = [sem(f"evacuated{k}") for k in range(2)]
        ln1_stats, ln1_scales, xs_done = sem("ln1_stats"), sem("ln1_scales"), sem("xs_done")
        qk_scaled, qk_high, qk_copied, qk_normed = sem("qk_scaled"), sem("qk_high"), sem("qk_copied"), sem("qk_normed")
        scores_done, exp_done, probs_done, pv_done, y_normed = (
            sem("scores_done"), sem("exp_done"), sem("probs_done"), sem("pv_done"), sem("y_normed"))
        h0_kept, xa_done = sem("h0_kept"), sem("xa_done")
        hy_done, y2_sums, r2_done = sem("hy_done"), sem("y2_sums"), sem("r2_done")
        ln2_stats, ln2_scales, xn2_done = sem("ln2_stats"), sem("ln2_scales"), sem("xn2_done")
        h1_stored, xn2_stored = sem("h1_stored"), sem("xn2_stored")
        dve_step, pool_step = sem("dve_step"), sem("pool_step")
        exps_done, score_ready, score_stored = sem("exps_done"), sem("score_ready"), sem("score_stored")
        shifted = sem("shifted")
        scoreT_filled, counts_ready, counts_summed = sem("scoreT_filled"), sem("counts_ready"), sem("counts_summed")
        offs_ready, offs_summed, pos_ready, posT_filled, pos_copied = (
            sem("offs_ready"), sem("offs_summed"), sem("pos_ready"), sem("posT_filled"), sem("pos_copied"))
        phase2_init = sem("phase2_init")
        onehot_ready, onehot_used, list_filled, list_done = (
            sem("onehot_ready"), sem("onehot_used"), sem("list_filled"), sem("list_done"))
        idx_ready = sem("idx_ready")
        gathered = [sem(f"gathered{k}") for k in range(2)]
        scattered = [sem(f"scattered{k}") for k in range(2)]
        expert_in = [sem(f"expert_in{k}") for k in range(2)]
        fb2_in = sem("fb2_in")
        filled2 = [sem(f"filled2_{k}") for k in range(4)]
        evacuated2 = [sem(f"evacuated2_{k}") for k in range(4)]
        contrib_done = sem("contrib_done")

        QKV = [("qk", 0), ("qk", 1), ("qk", 2), ("qk", 3), ("v", 0), ("v", 1)]
        BANKED = {
            "front": ([("xsT", 1)], [("xsT", 0)]),
            "qkv": ([("qk", 0), ("qk", 2), ("v", 0)], [("qk", 1), ("qk", 3), ("v", 1)]),
            "qkT": [("qkT", c) for c in range(H // 2)],
            "after": ([("yT", 1), ("wo", 0), ("y2T", 0)], [("yT", 0), ("wo", 1), ("y2T", 1)]),
            "router": [("x2T", 0), ("x2T", 1), ("rtT", 0), ("rt", 0)],
        }
        EARLY = 3
        w1_blocks = lambda k, lo, hi: [("w1", m) for m in range(lo, hi) if m % 2 == k]
        body = (
            [("tok2", 0)] + BANKED["after"][0] + w1_blocks(0, 0, EARLY) + BANKED["front"][0] + BANKED["qkv"][0]
            + w1_blocks(0, EARLY, MC) + [("w2", 0), ("w2", 1)] + BANKED["router"],
            [("yT", 0), ("tok2", 1)] + BANKED["after"][1][1:] + w1_blocks(1, 0, EARLY) + BANKED["front"][1]
            + w1_blocks(1, EARLY, EARLY + 1) + BANKED["qkv"][1] + w1_blocks(1, EARLY + 1, MC) + BANKED["qkT"],
        )
        ORDER = {
            "first": ([("tok1", 0), ("tok2", 0)] + BANKED["front"][0] + BANKED["qkv"][0] + [("next", 1)],
                      [("tok1", 1), ("tok2", 1)] + BANKED["front"][1] + BANKED["qkv"][1] + BANKED["qkT"] + [("next", 0)]),
            "body": (body[0] + [("next", 1)], body[1] + [("next", 0)]),
            "final": body,
            "last": (BANKED["after"][0] + w1_blocks(0, 0, MC) + [("w2", 0), ("w2", 1)] + BANKED["router"],
                     BANKED["after"][1] + w1_blocks(1, 0, MC)),
        }

        class Part:
            def __init__(self, kind, i):
                self.kind, self.i, self.order = kind, i, ORDER[kind]
                count = lambda k: [len(blocks) for blocks in ORDER[k]]
                if kind == "first":
                    self.base = [0, 0]
                elif kind == "last":
                    self.base = [f + (PAIRS - 2) * b + e for f, b, e in zip(count("first"), count("body"), count("final"))]
                else:
                    self.base = [f + (i - 1) * b for f, b in zip(count("first"), count("body"))]

            def bank(self, *key):
                return 0 if key in self.order[0] else 1

            def count(self, *key):
                k = self.bank(*key)
                return self.base[k] + (self.order[k].index(key) + 1)

            def wait_filled(self, eng, *key):
                eng.wait_ge(filled[self.bank(*key)], self.count(*key))

            def wait_evacuated(self, eng, *key):
                eng.wait_ge(evacuated[self.bank(*key)], self.count(*key))

            def wait_free(self, eng, *key):
                k = self.bank(*key)
                n = self.order[k].index(key)
                if self.kind != "first" or n >= 1:
                    eng.wait_ge(evacuated[k], self.base[k] + n)

            def g(self, *key):
                return G[self.bank(*key)]

        pe = nc.tensor
        NG = H

        def pe_block(part, key, ins):
            ins.then_inc(filled[part.bank(*key)], 1)

        def pe_transposes(part, key, src):
            part.wait_free(pe, *key)
            for t in range(NT):
                last = pe.transpose(part.g(*key)[:, t * T:(t + 1) * T], src(t), ident[0:T, 0:T])
            pe_block(part, key, last)

        def pe_tok1(part, key, steps):
            m = key[1]
            if steps[0] == 0:
                part.wait_free(pe, *key)
            for step_ in steps:
                b, q = step_ // HALF, step_ % HALF
                last = pe.matmul(part.g(*key)[:, b * NP_:(b + 1) * NP_], w1t[:, q, m * 128:(m + 1) * 128],
                                 img[b][:, q:q + PS * (NP_ - 1) + 1:PS], start=q == 0, stop=q == HALF - 1)
            if steps[-1] == 2 * HALF - 1:
                pe_block(part, key, last)

        def pe_tok2(part, j, b):
            if b == 0:
                if part.kind == "first":
                    for m in range(KC):
                        part.wait_evacuated(pe, "tok1", m)
                else:
                    for k in range(2):
                        pe.wait_ge(evacuated[k], part.base[k])
            part.wait_free(pe, "tok2", b)
            for half in range(2):
                n = T if half == 0 else LASTP
                at = b * NP_ + half * T
                for m in range(KC):
                    last = pe.matmul(part.g("tok2", b)[0:n, half * D:(half + 1) * D], hid[:, m, at:at + n],
                                     w2t[:, m, :], start=m == 0, stop=m == KC - 1)
            pe_block(part, ("tok2", b), last)

        def pe_xsT(part, j):
            pe.wait_ge(xs_done, j + 1)
            for c in range(KC):
                pe_transposes(part, ("xsT", c), lambda t: xs[:, t, c * 128:(c + 1) * 128])

        def pe_qkv(part, j):
            for c in range(KC):
                part.wait_evacuated(pe, "xsT", c)
            for key in QKV:
                part.wait_free(pe, *key)
                if key[0] == "qk":
                    t = key[1]
                    for c in range(KC):
                        last = pe.matmul(part.g(*key)[0:T, :], xsT[:, c, t * T:(t + 1) * T], wqkv[:, c, 0:2 * D],
                                         start=c == 0, stop=c == KC - 1)
                else:
                    for half in range(2):
                        t = 2 * key[1] + half
                        for c in range(KC):
                            last = pe.matmul(part.g(*key)[0:T, half * D:(half + 1) * D], xsT[:, c, t * T:(t + 1) * T],
                                             wqkv[:, c, 2 * D:], start=c == 0, stop=c == KC - 1)
                pe_block(part, key, last)

        def pe_qkT(part, j, c):
            if c == 0:
                pe.wait_ge(qk_normed, j + 1)
                pe.wait_ge(qk_copied, j + 1)
            key = ("qkT", c)
            part.wait_free(pe, *key)
            dst = part.g(*key)[:, 0:W].bitcast(F16)
            for s in range(2):
                for t in range(NT):
                    h = s * H + 2 * c
                    last = pe.transpose(dst[:, s * W + t * T:s * W + (t + 1) * T],
                                        qkp[:, t, h:h + 2, :].rearrange("p h d -> p (h d)"), ident_h[:, :])
            pe_block(part, key, last)

        def pe_scores(part, j, g, first):
            b, pair = g // (H // 2), g % (H // 2)
            if b == 0:
                part.wait_evacuated(pe, "qkT", pair)
            if not (first and g < 2):
                pe.wait_ge(exp_done, NG * j + (g - 1))
            for hh in range(2):
                lo = HP * hh
                rows = slice(lo, lo + HP)
                o = b * S
                dst = SC[g % 2]
                pe.matmul(dst[0:T, hh, 0:S], qkT[rows, pair, 1, o:o + T], qkT[rows, pair, 0, o:o + S],
                          start=True, stop=True)
                last = pe.matmul(dst[0:T, hh, S:QW], qkT[rows, pair, 1, o + T:o + S], qkT[rows, pair, 0, o + T:o + S],
                                 start=True, stop=True)
            last.then_inc(scores_done, 1)

        def pe_pv(part, j, g, hh, first):
            b, pair = g // (H // 2), g % (H // 2)
            h = 2 * pair + hh
            if hh == 0:
                pe.wait_ge(probs_done, NG * j + (g + 1))
            if h == 0:
                if not (first and b == 0):
                    pe.wait_ge(y_normed, 2 * j + b)
                pe.matmul(Y[0][0:T, 0:H * HV], first_col[:, :], v1[:, 2 * b + 1, :, :].rearrange("p h d -> p (h d)"),
                          start=True, stop=False, skip_group_check=True)
            cols = slice(h * HV, (h + 1) * HV)
            pe.matmul(Y[1][0:T, cols], pm[g % 2][:, hh, T:S], v1[:, 2 * b, h, :],
                      start=h == 0, stop=False, skip_group_check=True)
            pe.matmul(Y[1][0:T, cols], pm[g % 2][:, hh, S:QW], v1[:, 2 * b + 1, h, :],
                      start=False, stop=h == H - 1, skip_group_check=True)
            last = pe.matmul(Y[0][0:T, cols], pm[g % 2][:, hh, 0:T], v1[:, 2 * b, h, :],
                             start=False, stop=h == H - 1, skip_group_check=True)
            if hh == 1:
                last.then_inc(pv_done, 1)

        def pe_w1(part, m):
            if m == 0:
                for c in range(KC):
                    part.wait_evacuated(pe, "y2T", c)
            part.wait_free(pe, "w1", m)
            for c in range(KC):
                last = pe.matmul(part.g("w1", m)[:, 0:W], w1m[:, c, m * 128:(m + 1) * 128], yT[:, c, :],
                                 start=c == 0, stop=c == KC - 1)
            pe_block(part, ("w1", m), last)

        def pe_w2(part, pieces):
            for n in pieces:
                b, t = n // 8, n // 4
                if n == 0:
                    for m in range(MC - 2, MC):
                        part.wait_evacuated(pe, "w1", m)
                if n % 8 == 0:
                    part.wait_free(pe, "w2", b)
                at = (t % 2) * D
                for m in range(2 * (n % 4), 2 * (n % 4) + 2):
                    last = pe.matmul(part.g("w2", b)[0:T, at:at + D], hT[:, m, t * T:(t + 1) * T], w2m[:, m, :],
                                     start=m == 0, stop=m == MC - 1)
                if n % 8 == 7:
                    pe_block(part, ("w2", b), last)

        SLOTS = {}
        for n, slot in enumerate((1, 2, 3, 4, 5, 6, 7, 9)):
            SLOTS[slot] = ("w2", range(8 + n, 9 + n))
        for n in range(7):
            SLOTS[10 + n] = ("next", 0, range(2 * n, 2 * n + 2))
        SLOTS[18], SLOTS[19] = ("x2T", 0), ("x2T", 1)
        SLOTS[20], SLOTS[21] = ("rtT", 0), ("rtT", 1)
        SLOTS[22] = ("next", 0, range(14, 16))
        SLOTS[23] = ("rt", 0)
        for n in range(8):
            SLOTS[24 + n] = ("next", 1, range(2 * n, 2 * n + 2))

        def pe_slot(part, j, slot):
            work = SLOTS.get(slot, (None,))
            if work[0] == "next":
                if part.kind != "final":
                    if slot == 10:
                        for b in range(2):
                            pe.wait_ge(img_in[b], 16 * 2 * C * (j + 2))
                    pe_tok1(part, ("next", work[1]), work[2])
            elif part.kind == "first":
                return
            elif work[0] == "w2":
                pe_w2(part, work[1])
            elif work[0] == "x2T":
                pe_x2T(part, j - 1, work[1])
            elif work[0] == "rtT":
                pe_rtT(part, work[1])
            elif work[0] == "rt":
                pe_rt(part)

        def pe_attention(part, j):
            first = part.kind == "first"
            w2 = (lambda lo: None) if first else (lambda lo: pe_w2(part, range(lo, lo + 2)))
            w2(0)
            pe_qkT(part, j, 0)
            w2(2)
            pe_qkT(part, j, 1)
            pe_scores(part, j, 0, first)
            w2(4)
            pe_scores(part, j, 1, first)
            pe_qkT(part, j, 2)
            w2(6)
            for g in range(NG):
                pe_slot(part, j, 2 * g)
                if g + 2 < NG:
                    pe_scores(part, j, g + 2, first)
                if g + 3 < H // 2:
                    pe_qkT(part, j, g + 3)
                pe_pv(part, j, g, 0, first)
                pe_slot(part, j, 2 * g + 1)
                pe_pv(part, j, g, 1, first)

        def pe_yT(part, j):
            pe.wait_ge(y_normed, 2 * (j + 1))
            for c in range(KC):
                pe_transposes(part, ("yT", c), lambda t: yn[:, t, c * 128:(c + 1) * 128])

        def pe_wo(part, j):
            for c in range(KC):
                part.wait_evacuated(pe, "yT", c)
            for b in range(2):
                part.wait_free(pe, "wo", b)
                for half in range(2):
                    t = 2 * b + half
                    for c in range(KC):
                        last = pe.matmul(part.g("wo", b)[0:T, half * D:(half + 1) * D], yT[:, c, t * T:(t + 1) * T],
                                         wo[:, c, :], start=c == 0, stop=c == KC - 1)
                pe_block(part, ("wo", b), last)

        def pe_y2T(part, j):
            for b in range(2):
                part.wait_evacuated(pe, "wo", b)
            for c in range(KC):
                pe_transposes(part, ("y2T", c), lambda t: y2[:, t, c * 128:(c + 1) * 128])

        def pe_x2T(part, j, c):
            if c == 0:
                pe.wait_ge(xn2_done, j + 2)
            pe_transposes(part, ("x2T", c), lambda t: xn2[:, t, c * 128:(c + 1) * 128])

        def pe_rtT(part, c):
            part.wait_evacuated(pe, "x2T", c)
            if c == 0:
                part.wait_free(pe, "rtT", 0)
            last = pe.matmul(part.g("rtT", 0)[0:NE, 0:W], wr[:, c, :], xsT[:, c, :], start=c == 0, stop=c == KC - 1)
            if c == KC - 1:
                pe_block(part, ("rtT", 0), last)

        def pe_rt(part):
            copied = part.count("rtT", 0)
            if not isinstance(copied, int):
                copied = pe.snap(pe.to_reg(copied))
                wait_apart(pe)
            pe.wait_ge(evacuated[part.bank("rtT", 0)], copied)
            for t in range(NT):
                last = pe.transpose(part.g("rt", 0)[0:T, t * NE:(t + 1) * NE], logitsT[:, t * T:(t + 1) * T],
                                    ident[0:NE, 0:NE])
            pe_block(part, ("rt", 0), last)

        G2 = [G[0], G[1], SC[0][:, 0, :], SC[0][:, 1, :]]
        BLK = {**{("w1", m): m for m in range(MC)}, ("xT", 0): MC, ("xT", 1): MC + 1, ("w2", 0): MC + 2,
               ("w2", 1): MC + 3}
        NBLK = len(BLK)
        assert NBLK % 4 == 0

        def bank2(key):
            return (2 + BLK[key]) % 4

        def count2(n, key):
            return n * (NBLK // 4) + ((2 + BLK[key]) // 4 + 1)

        def wait_evacuated2(eng, n, key):
            eng.wait_ge(evacuated2[bank2(key)], count2(n, key) + 1)

        def wait_free2(eng, n, key):
            eng.wait_ge(evacuated2[bank2(key)], n * (NBLK // 4) + ((2 + BLK[key]) // 4 + 1))

        def wait_apart(eng):
            eng.wait_ge(pool_consts, 6)

        block = ctx.enter_context(nc.Block())

        @block.sync
        def _(sp):
            for half in range(2):
                for c in range(C):
                    src = tok_W1[c * PS * PS:(c + 1) * PS * PS, :].rearrange("(y x) d -> y x d", x=PS)
                    lo = half * KROW + c * PS
                    sp.dma_start(w1t[lo:lo + PS, :, :], src[:, half * HALF:(half + 1) * HALF, :]).then_inc(weights_in, 16)
            for dst, src in ((w2t, tok_W2), (wo, Wo), (w1m, W1), (w2m, W2), (wr, Wr)):
                sp.dma_start(dst[:, :, :], src.rearrange("(c p) n -> p c n", p=128)).then_inc(weights_in, 16)
            for k, src in enumerate((Wq, Wk, Wv)):
                sp.dma_start(wqkv[:, :, k * D:(k + 1) * D], src.rearrange("(c p) n -> p c n", p=128)).then_inc(weights_in, 16)
            sp.dma_start(b2t[:, :], tok_b2.partition_broadcast(T)).then_inc(weights_in, 16)

            def load_images(j):
                for b in range(2):
                    for half in range(2):
                        for c in range(C):
                            lo = half * KROW + c * PS
                            src = x[2 * j + b] if isinstance(j, int) else x[bass.ds(2 * j + b, 1)].rearrange("o c y x -> (o c) y x")
                            src = src[c].rearrange("(g r) x -> r g x", r=PS)
                            n = IMG - half * HALF
                            dst = img[b][lo:lo + PS, :].rearrange("p (g x) -> p g x", x=IMG)
                            sp.dma_start(dst[:, :, 0:n], src[:, :, half * HALF:]).then_inc(img_in[b], 16)

            def load_text(j):
                if not (isinstance(j, int) and j == 0):
                    sp.wait_ge(h0_kept, j)
                    sp.wait_ge(xa_done, j)
                src = txt[2 * j:2 * j + 2] if isinstance(j, int) else txt[bass.ds(2 * j, 2)]
                sp.dma_start(h0[LASTP:T, 1:NT:2, :], src.rearrange("b s d -> s b d")).then_inc(text_in, 16)

            def store_h1(part, j):
                part.wait_evacuated(sp, "w2", 1)
                dst = out_rows[bass.ds(j * W, W)] if not isinstance(j, int) else out_rows[j * W:(j + 1) * W]
                sp.dma_start(dst.rearrange("(t p) d -> p t d", p=T), hy[:, :, :]).then_inc(h1_stored, 16)

            def store_xn2(j):
                sp.wait_ge(xn2_done, j + 2)
                dst = xd[bass.ds(j * W, W), 0:D] if not isinstance(j, int) else xd[j * W:(j + 1) * W, 0:D]
                sp.dma_start(dst.rearrange("(t p) d -> p t d", p=T), xn2[:, :, :]).then_inc(xn2_stored, 16)

            load_images(0)
            load_text(0)
            sp.wait_ge(zrow_ready, 1)
            pitch = 2 * S - 1 + T
            sp.dma_start(bass.AP(zrow_d, 0, [[T * pitch, H], [pitch + 1, T], [1, 2 * S - 1]]),
                         zrow[:, :].unsqueeze(1).to_broadcast([H, T, 2 * S - 1])).then_inc(rows_out, 16)
            sp.dma_start(mrow_d[:, :], mrow[:, :]).then_inc(rows_out, 16)
            sp.wait_ge(rows_out, 32)
            toep = lambda h, n: bass.AP(zrow_d, h * T * pitch + S - 1, [[pitch, T], [T * pitch, H // 2], [1, n]])
            mx = lambda h, o, n: bass.AP(mrow_d, h * S + o, [[0, T], [S, H // 2], [1, n]])
            for k in range(2):
                h = k * (H // 2)
                m = mtmp[k][:, 0:H // 2 * QW].rearrange("p (h q) -> p h q", q=QW)
                sp.dma_start(bias_t[:, h:h + H // 2, 0:S], toep(h, S)).then_inc(toeplitz_in, 16)
                sp.dma_start(bias_t[:, h:h + H // 2, S:QW], toep(h, T)).then_inc(toeplitz_in, 16)
                sp.dma_start(m[:, :, 0:S], mx(h, 0, S)).then_inc(toeplitz_in, 16)
                sp.dma_start(m[:, :, S:QW], mx(h, T, T)).then_inc(toeplitz_in, 16)
            first = Part("first", 0)
            first.wait_filled(sp, "tok1", 1)
            load_images(1)
            load_text(1)
            first.wait_filled(sp, "next", 1)
            load_images(2)
            with sp.Fori(1, PAIRS - 2) as i:
                part = Part("body", i)
                load_text(i + 1)
                store_h1(part, i - 1)
                store_xn2(i - 1)
                part.wait_filled(sp, "next", 1)
                load_images(i + 2)
            load_text(PAIRS - 1)
            for i, kind in ((PAIRS - 2, "body"), (PAIRS - 1, "final"), (PAIRS, "last")):
                store_h1(Part(kind, i), i - 1)
                store_xn2(i - 1)
            sp.wait_ge(phase2_init, 1)
            for e in range(2):
                sp.dma_start(we1[e][:, :, :], fW1[e].rearrange("(c p) n -> p c n", p=128)).then_inc(expert_in[e], 16)
                sp.dma_start(we2[e][:, :, :], fW2[e].rearrange("(c p) n -> p c n", p=128)).then_inc(expert_in[e], 16)
            sp.dma_start(fb2b[:, :, :], fb2.partition_broadcast(T)).then_inc(fb2_in, 16)
            sp.wait_ge(score_ready, 1)
            sp.dma_start(xd[:, D:XW].rearrange("(t p) e -> p t e", p=T), score[:, :, :]).then_inc(score_stored, 16)
            for e in range(2, NE):
                n = (e - 2) * GROUPS + GROUPS - 1
                sp.wait_ge(filled2[bank2(("w2", 1))], count2(n, ("w2", 1)))
                sp.dma_start(we1[e % 2][:, :, :], fW1[e].rearrange("(c p) n -> p c n", p=128)).then_inc(expert_in[e % 2], 16)
                sp.dma_start(we2[e % 2][:, :, :], fW2[e].rearrange("(c p) n -> p c n", p=128)).then_inc(expert_in[e % 2], 16)
            sp.wait_ge(h1_stored, 16 * (PAIRS + 1))
            sp.wait_ge(xn2_stored, 16 * (PAIRS + 1))
            sp.wait_ge(score_stored, 16)

        @block.tensor
        def _(eng):
            pe.wait_ge(weights_in, 16 * 15)
            pe.wait_ge(pool_consts, 6)
            part = Part("first", 0)
            for b in range(2):
                pe.wait_ge(img_in[b], 16 * 2 * C)
            for m in range(KC):
                pe_tok1(part, ("tok1", m), range(2 * HALF))
            for b in range(2):
                pe_tok2(part, 0, b)
            pe.wait_ge(setup_done, 1)
            pe_xsT(part, 0)
            pe_qkv(part, 0)
            pe_attention(part, 0)

            def iteration(part, i):
                pe_tok2(part, i, 0)
                pe_yT(part, i - 1)
                pe_tok2(part, i, 1)
                pe_wo(part, i - 1)
                pe_y2T(part, i - 1)
                for m in range(EARLY):
                    pe_w1(part, m)
                pe_xsT(part, i)
                pe_w1(part, EARLY)
                pe_qkv(part, i)
                for m in range(EARLY + 1, MC):
                    pe_w1(part, m)
                pe_attention(part, i)

            with eng.Fori(1, PAIRS - 1) as i:
                iteration(Part("body", i), i)
            iteration(Part("final", PAIRS - 1), PAIRS - 1)
            part = Part("last", PAIRS)
            pe_yT(part, PAIRS - 1)
            pe_wo(part, PAIRS - 1)
            pe_y2T(part, PAIRS - 1)
            for m in range(MC):
                pe_w1(part, m)
            pe_w2(part, range(16))
            for c in range(KC):
                pe_x2T(part, PAIRS - 1, c)
            for c in range(KC):
                pe_rtT(part, c)
            pe_rt(part)

            pe.wait_ge(score_ready, 2)
            for g in range(GT):
                last = pe.transpose(SC[1][:, g // 4, (g % 4) * T:(g % 4 + 1) * T], by_group[:, g, :],
                                    ident[0:T, 0:T])
            last.then_inc(scoreT_filled, 1)
            with eng.Fori(0, 30) as k:
                pe.wait_ge(counts_ready, k + 1)
                pe.matmul(Y[1][:, 0:1], group_ones[:, :], cnt[:, 0:1], start=True, stop=True).then_inc(counts_summed, 1)
            pe.wait_ge(counts_ready, 31)
            pe.matmul(Y[1][:, 1:2], group_ones[:, :], cnt[:, 1:2], start=True, stop=True)
            pe.matmul(Y[1][:, 2:3], earlier_ones[:, :], cnt[:, 2:3], start=True, stop=True).then_inc(offs_summed, 1)
            pe.wait_ge(offs_ready, 1)
            pe.matmul(Y[1][:, 3:4], earlier_ones[:, :], cnt[:, 3:4], start=True, stop=True).then_inc(offs_summed, 1)
            pe.wait_ge(pos_ready, 1)
            for g in range(GT):
                last = pe.transpose(SC[1][0:T, g // 4, (g % 4) * 128:(g % 4 + 1) * 128], rank[:, g * T:(g + 1) * T],
                                    ident[:, :])
            last.then_inc(posT_filled, 1)

            def clear_list():
                pe.matmul(Y[0][0:T, 0:2 * SLOTC], zero_w[:, :], iota_b[:, 0:2 * SLOTC],
                          start=True, stop=False, skip_group_check=True)

            def list_part(k, n):
                pe.wait_ge(onehot_ready, n + 1)
                for t in range(LT):
                    last = pe.matmul(Y[0][0:T, 0:2 * SLOTC], oh_b[k][:, t, :],
                                     oh_a[k][:, t, :, :].rearrange("p a b -> p (a b)"),
                                     start=False, stop=False, skip_group_check=True)
                last.then_inc(onehot_used, 1)

            def row_transposes(k, banks):
                for c in range(KC):
                    for t in range(NT):
                        last = pe.transpose(G2[banks[c]][:, t * T:(t + 1) * T], xg[k][:, t, c * 128:(c + 1) * 128],
                                            ident[0:T, 0:T])
                    last.then_inc(filled2[banks[c]], 1)

            def w1_block(eb, n, m):
                key = ("w1", m)
                wait_free2(pe, n, key)
                for c in range(KC):
                    last = pe.matmul(G2[bank2(key)][:, 0:W], we1[eb][:, c, m * 128:(m + 1) * 128], xgT[:, c, :],
                                     start=c == 0, stop=c == KC - 1)
                last.then_inc(filled2[bank2(key)], 1)

            def group(eb, half_n, k):
                n = half_n * 2 + k
                for m in range(MC // 2):
                    w1_block(eb, n, m)
                list_part(k, n + GROUPS)
                for m in range(MC // 2, MC):
                    w1_block(eb, n, m)
                pe.wait_ge(gathered[1 - k], (half_n + (1 + k)) * (16 * NT))
                for c in range(KC):
                    wait_free2(pe, n, ("xT", c))
                row_transposes(1 - k, [bank2(("xT", c)) for c in range(KC)])
                for m in range(MC - 4, MC):
                    wait_evacuated2(pe, n, ("w1", m))
                for b in range(2):
                    key = ("w2", b)
                    wait_free2(pe, n, key)
                    for half in range(2):
                        t = 2 * b + half
                        for m in range(MC):
                            last = pe.matmul(G2[bank2(key)][0:T, half * D:(half + 1) * D],
                                             hTe[:, m, t * T:(t + 1) * T], we2[eb][:, m, :],
                                             start=m == 0, stop=m == MC - 1)
                    last.then_inc(filled2[bank2(key)], 1)
                for c in range(KC):
                    wait_evacuated2(pe, n, ("xT", c))

            pe.wait_ge(onehot_ready, 1)
            clear_list()
            for p in range(GROUPS):
                list_part(p % 2, p)
            pe.wait_ge(gathered[0], 16 * NT)
            row_transposes(0, [0, 1])
            for c in range(KC):
                pe.wait_ge(evacuated2[c], 2)
            with eng.Fori(0, NE // 2) as E:
                for eb in range(2):
                    e = E * 2 + eb
                    pe.wait_ge(expert_in[eb], (E + 1) * 32)
                    pe.wait_ge(list_done, e + 1)
                    clear_list()
                    with eng.Fori(0, GROUPS // 2) as q:
                        for k in range(2):
                            group(eb, e * (GROUPS // 2) + q, k)

        act = nc.scalar

        def act_evacuate(part, key, dst, cols=W):
            part.wait_filled(act, *key)
            act.copy(dst, part.g(*key)[0:dst.shape[0], 0:cols]).then_inc(evacuated[part.bank(*key)], 1)

        @block.scalar
        def _(eng):
            with nc.allow_non_contiguous_dma(reason="small vectors of weights"):
                act.dma_start(relb[:, :], rel_bias.rearrange("k h -> h k")).then_inc(consts_in, 16)
                act.dma_start(sc_col[:, :], scale.rearrange("(h o) -> h o", o=1)).then_inc(consts_in, 16)
                act.dma_start(sc_bc[:, :], scale.partition_broadcast(T)).then_inc(consts_in, 16)
                act.dma_start(lnw[:, 0, :], ln1_w.rearrange("(c p) -> p c", p=128)).then_inc(consts_in, 16)
                act.dma_start(lnw[:, 1, :], ln2_w.rearrange("(c p) -> p c", p=128)).then_inc(consts_in, 16)
                act.dma_start(b1t[:, :], tok_b1.rearrange("(c p) -> p c", p=128)).then_inc(consts_in, 16)
                for e in range(NE):
                    act.dma_start(fb1c[:, e, :], fb1[e].rearrange("(m p) -> p m", p=128)).then_inc(consts_in, 16)

            def qkT_evacuate(eng, part, c):
                part.wait_filled(eng, "qkT", c)
                eng.copy(qkT[:, c, :, :].rearrange("p s w -> p (s w)"),
                         part.g("qkT", c)[:, 0:W].bitcast(F16)).then_inc(evacuated[part.bank("qkT", c)], 1)

            def silu(part, key):
                part.wait_filled(act, *key)
                act.activation(hid[:, key[1], :], part.g(*key)[:, 0:2 * NP_], ACT.Silu,
                               bias=b1t[:, key[1]:key[1] + 1]).then_inc(evacuated[part.bank(*key)], 1)

            def xs_transposed(part):
                for c in range(KC):
                    act_evacuate(part, ("xsT", c), xsT[:, c, :])

            def queries_keys(part, j):
                if part.kind != "first":
                    act.wait_ge(qk_normed, j)
                for t in range(NT):
                    act_evacuate(part, ("qk", t), qkraw[:, t, :], 2 * D)
                for b in range(2):
                    part.wait_filled(act, "v", b)
                    src = part.g("v", b)[0:T, :].rearrange("p (t h d) -> p t h d", t=2, d=HD)
                    act.copy(v1[:, 2 * b:2 * b + 2, :, 0:HD], src).then_inc(evacuated[part.bank("v", b)], 1)

            def high_parts(j, tiles):
                for t in tiles:
                    act.wait_ge(qk_scaled, NT * j + (t + 1))
                    src = qkraw[:, t, :].rearrange("p (h d) -> p h d", d=HD)
                    act.copy(qkp[:, t, :, 0:HD], src).then_inc(qk_high, 1)

            def exps(part, j):
                first = part.kind == "first"
                qkT_evacuate(act, part, 0)
                for g in range(NG):
                    act.wait_ge(scores_done, NG * j + (g + 1))
                    if not (first and g < 2):
                        act.wait_ge(probs_done, NG * j + (g - 1))
                    act.activation(p0[g % 2][:, :, :], SC[g % 2][0:T, :, 0:QW], ACT.Exp).then_inc(exp_done, 1)
                    if g % 2 == 0 and g + 2 < H // 2:
                        qkT_evacuate(act, part, g + 2)
                    if not first and 10 <= g < 10 + KC:
                        x2_transposed(part, g - 10)
                if part.kind != "final":
                    for m in range(KC):
                        silu(part, ("next", m))

            def squares(part):
                for b in range(2):
                    part.wait_evacuated(act, "wo", b)
                    for half in range(2):
                        t = 2 * b + half
                        last = act.activation(junk[:, t, :], y2[:, t, :], ACT.Square, scale=D ** -0.5,
                                              accum_out=ss2[:, t:t + 1])
                last.then_inc(y2_sums, 1)

            def y2_transposed(part):
                for c in range(KC):
                    act_evacuate(part, ("y2T", c), yT[:, c, :])

            def relu(part, ms):
                for m in ms:
                    part.wait_filled(act, "w1", m)
                    act.activation(hT[:, m, :], part.g("w1", m)[:, 0:W], ACT.Relu).then_inc(evacuated[part.bank("w1", m)], 1)

            def yT_evacuate(part):
                for c in range(KC):
                    act_evacuate(part, ("yT", c), yT[:, c, :])

            def x2_transposed(part, c):
                act_evacuate(part, ("x2T", c), xsT[:, c, :])

            act.wait_ge(consts_in, 16 * (6 + NE))
            act.wait_ge(table_diff, 1)
            act.activation(bias_t[:, :, :], bias_t[:, :, :], ACT.Exp).then_inc(table_exp, 1)
            part = Part("first", 0)
            for m in range(KC):
                silu(part, ("tok1", m))
            xs_transposed(part)
            queries_keys(part, 0)
            high_parts(0, range(NT))
            exps(part, 0)

            def iteration(part, i):
                yT_evacuate(part)
                y2_transposed(part)
                squares(part)
                relu(part, range(EARLY))
                xs_transposed(part)
                relu(part, [EARLY])
                queries_keys(part, i)
                relu(part, range(EARLY + 1, MC - 2))
                high_parts(i, range(3))
                relu(part, [MC - 2])
                high_parts(i, range(3, NT))
                relu(part, [MC - 1])
                exps(part, i)

            with eng.Fori(1, PAIRS - 1) as i:
                iteration(Part("body", i), i)
            iteration(Part("final", PAIRS - 1), PAIRS - 1)
            part = Part("last", PAIRS)
            yT_evacuate(part)
            y2_transposed(part)
            squares(part)
            relu(part, range(4))
            for c in range(KC):
                x2_transposed(part, c)

            act.wait_ge(shifted, 1)
            act.activation(score[:, :, :], score[:, :, :], ACT.Exp).then_inc(exps_done, 1)
            act.wait_ge(filled2[0], 1)
            act.copy(xgT[:, 0, :], G2[0][:, 0:W]).then_inc(evacuated2[0], 1)
            with eng.Fori(0, NE) as e:
                with eng.Fori(0, GROUPS) as g:
                    n = e * GROUPS + g
                    for m in range(MC):
                        key = ("w1", m)
                        act.wait_ge(filled2[bank2(key)], count2(n, key))
                        bias = fb1c[:, :, :].rearrange("p e m -> p (e m)")[:, bass.ds(e * MC + m, 1)]
                        act.activation(hTe[:, m, :], G2[bank2(key)][:, 0:W], ACT.Gelu,
                                       bias=bias).then_inc(evacuated2[bank2(key)], 1)
                    key = ("xT", 0)
                    act.wait_ge(filled2[bank2(key)], count2(n, key))
                    act.copy(xgT[:, 0, :], G2[bank2(key)][:, 0:W]).then_inc(evacuated2[bank2(key)], 1)

        dve = nc.vector

        @block.vector
        def _(eng):
            chain = Chain(dve, dve_step, lambda: wait_apart(dve))
            step = chain.step

            dve.wait_ge(pool_consts, 6)
            dve.tensor_scalar(diff_low[:, :], diff[:, :], NE - 1, None, ALU.bitwise_and)
            step(dve.tensor_scalar(difff[:, :], diff[:, :], 128.0, None, ALU.is_gt))
            step(dve.tensor_scalar(group_ones[:, :], diff_low[:, :], 0.0, None, ALU.is_equal))
            dve.tensor_tensor(earlier_ones[:, :], difff[:, :], group_ones[:, :], ALU.mult)
            dve.tensor_copy(iota_b[:, :], iota_i[:, :])
            dve.tensor_copy(tok_p[:, :], tok_pi[:, :])
            dve.memset(zrow[:, 0:S], -3.0e38)
            dve.memset(mrow[:, 0:1], 0.0)
            dve.wait_ge(consts_in, 16 * (6 + NE))
            step(dve.tensor_scalar(relb[:, :], relb[:, :], sc_col[:, 0:1], None, ALU.mult))
            for d, n, k in relative_bucket_runs(S, NBUCK, 128):
                last = dve.tensor_copy(zrow[:, S - 1 + d:S - 1 + d + n], relb[:, k:k + 1].to_broadcast([H, n]))
            step(last)
            dve.tensor_tensor_scan(mrow[:, 1:S], zrow[:, S:2 * S - 1], zrow[:, S:2 * S - 1], -3.0e38,
                                   ALU.max, ALU.max).then_inc(zrow_ready, 1)
            step(dve.tensor_scalar(shift[:, 0, :], sc_bc[:, :], -1.0, None, ALU.mult))
            step(dve.tensor_tensor(shift[:, 0, :], shift[:, 0, :], sc_bc[:, :], ALU.max))
            step(dve.tensor_scalar(shift[:, 1, :], shift[:, 0, :], -1.0, SAFE, ALU.mult, ALU.add))
            step(dve.tensor_scalar(shift[:, 1, :], shift[:, 1, :], 0.0, None, ALU.min))
            dve.memset(v1[:, :, :, :], 1.0)
            step(dve.memset(qkp[:, :, :, :], 0.0))
            for t in range(NT):
                dve.tensor_copy(qkp[:, t, 0:H, 3 * HD], shift[:, 1, :])
                last = dve.tensor_copy(sc_q[:, t, :], sc_bc[:, :])
            step(last)
            dve.memset(qkp[:, :, H:2 * H, 3 * HD:3 * HD + 1], 1.0)
            dve.memset(qkp[0:1, 0:NT:2, 0:H, 3 * HD:3 * HD + 1], 0.0)
            dve.tensor_copy(ident_h[:, :], ident[0:T, 0:T])
            dve.memset(sc_q[0:1, 0:NT:2, :], 0.0)
            dve.wait_ge(weights_in, 16 * 15)
            for c in range(KC):
                dve.tensor_scalar(wqkv[:, c, :], wqkv[:, c, :], lnw[:, 0, c:c + 1], None, ALU.mult)
                dve.tensor_scalar(w1m[:, c, :], w1m[:, c, :], lnw[:, 1, c:c + 1], None, ALU.mult)
            dve.wait_ge(toeplitz_in, 16 * 8)
            for k in range(2):
                hs = slice(k * (H // 2), (k + 1) * (H // 2))
                m = mtmp[k][:, 0:H // 2 * QW].rearrange("p (h q) -> p h q", q=QW)
                last = dve.tensor_tensor(bias_t[:, hs, :], bias_t[:, hs, :], m, ALU.subtract)
            last.then_inc(table_diff, 1)
            dve.wait_ge(table_exp, 1)
            dve.memset(bias_t[:, :, 0:1], 1.0).then_inc(setup_done, 1)

            def evacuate(part, key, dst, cols=W):
                part.wait_filled(dve, *key)
                dve.tensor_copy(dst, part.g(*key)[0:dst.shape[0], 0:cols]).then_inc(evacuated[part.bank(*key)], 1)

            def stats(src, mv, done):
                for t in range(NT):
                    last = dve.bn_stats(st[:, t, :], src[:, t, :])
                step(last, apart=True)
                for t in range(NT):
                    last = dve.bn_aggr(mv[:, t, :], st[:, t, :])
                last.then_inc(done, 1)

            def front_a(part, j, first):
                if not first:
                    dve.wait_ge(h0_kept, j)
                for b in range(2):
                    part.wait_filled(dve, "tok2", b)
                    dve.tensor_tensor(h0[:, 2 * b, :], part.g("tok2", b)[0:T, 0:D], b2t[:, :], ALU.add)
                    dve.tensor_tensor(h0[0:LASTP, 2 * b + 1, :], part.g("tok2", b)[0:LASTP, D:2 * D],
                                      b2t[0:LASTP, :], ALU.add).then_inc(evacuated[part.bank("tok2", b)], 1)
                for b in range(2):
                    part.wait_evacuated(dve, "tok2", b)
                dve.wait_ge(text_in, 16 * (j + 1))
                stats(h0, mv1, ln1_stats)

            def front_b(part, j):
                dve.wait_ge(ln1_scales, j + 1)
                for t in range(NT):
                    last = dve.tensor_scalar(xs[:, t, :], h0[:, t, :], mv1[:, t, 0:1], lt[:, 5, t:t + 1],
                                             ALU.subtract, ALU.mult)
                last.then_inc(xs_done, 1)
                if part.kind != "first":
                    for b in range(2):
                        part.wait_evacuated(dve, "wo", b)
                for t in range(NT):
                    last = dve.tensor_scalar(xa[:, t, :], h0[:, t, :], mv1[:, t, 0:1], lt[:, 1, t:t + 1],
                                             ALU.subtract, ALU.mult)
                last.then_inc(xa_done, 1)

            def qk_norm(part, j):
                def sums(t):
                    part.wait_evacuated(dve, "qk", t)
                    step(dve.tensor_tensor(sqb[:, :], qkraw[:, t, :], qkraw[:, t, :], ALU.mult))
                    return dve.reduce_sum(ss[:, t, :], sqb[:, :].rearrange("p (h d) -> p h d", d=HD), AX.X)

                for t in range(NT):
                    step(sums(t))
                x_, r_ = ss[:, :, :].rearrange("p t h -> p (t h)"), rn[:, :, :].rearrange("p t h -> p (t h)")
                a_ = nwt[:, :]
                step(dve.tensor_scalar(x_, x_, RMS_EPS, None, ALU.add))
                step(dve.tensor_scalar(a_.bitcast(I32), x_.bitcast(I32), 1, None, ALU.arith_shift_right))
                step(dve.tensor_scalar(r_.bitcast(I32), a_.bitcast(I32), -1.0, float(0x5f3759df), ALU.mult, ALU.add))
                for _ in range(3):
                    step(dve.tensor_tensor(a_, r_, r_, ALU.mult))
                    step(dve.scalar_tensor_tensor(a_, a_, -0.5, x_, ALU.mult, ALU.mult))
                    step(dve.scalar_tensor_tensor(r_, a_, 1.5, r_, ALU.add, ALU.mult))
                step(dve.tensor_tensor(rn[:, :, 0:H], rn[:, :, 0:H], sc_q[:, :, :], ALU.mult))
                for t in range(NT):
                    q = qkraw[:, t, :].rearrange("p (h d) -> p h d", d=HD)
                    dve.tensor_tensor(q, q, rn[:, t, :].unsqueeze(2).to_broadcast([T, 2 * H, HD]),
                                      ALU.mult).then_inc(qk_scaled, 1)
                for t in range(NT):
                    dve.wait_ge(qk_high, NT * j + (t + 1))
                    for s, at in ((0, HD), (H, 2 * HD)):
                        src = qkraw[:, t, s * HD:(s + H) * HD].rearrange("p (h d) -> p h d", d=HD)
                        dve.tensor_tensor(qkp[:, t, s:s + H, at:at + HD], src, qkp[:, t, s:s + H, 0:HD], ALU.subtract)
                    last = dve.tensor_copy(qkp[:, t, H:2 * H, HD:2 * HD], qkp[:, t, H:2 * H, 0:HD])
                last.then_inc(qk_normed, 1)

            def qkT_evacuate(part, c):
                part.wait_filled(dve, "qkT", c)
                dve.tensor_copy(qkT[:, c, :, :].rearrange("p s w -> p (s w)"),
                                part.g("qkT", c)[:, 0:W].bitcast(F16)).then_inc(evacuated[part.bank("qkT", c)], 1)

            def normalise_outputs(j, b):
                dve.wait_ge(pv_done, NG * j + (NG // 2) * (b + 1))
                for half in range(2):
                    y = Y[half][0:T, 0:H * HV].rearrange("p (h d) -> p h d", d=HV)
                    last = dve.reciprocal(yrec[:, half, :], y[:, :, HD])
                step(last)
                for half in range(2):
                    y = Y[half][0:T, 0:H * HV].rearrange("p (h d) -> p h d", d=HV)
                    dst = yn[:, 2 * b + half, :].rearrange("p (h d) -> p h d", d=HD)
                    last = dve.tensor_tensor(dst, y[:, :, 0:HD],
                                             yrec[:, half, :].unsqueeze(2).to_broadcast([T, H, HD]), ALU.mult)
                last.then_inc(y_normed, 1)

            def relu(part, ms):
                for m in ms:
                    part.wait_filled(dve, "w1", m)
                    dve.tensor_scalar(hT[:, m, :], part.g("w1", m)[:, 0:W], 0.0, None,
                                      ALU.max).then_inc(evacuated[part.bank("w1", m)], 1)

            def mlp_out(part, j, b):
                dve.wait_ge(r2_done, j + 1)
                dve.wait_ge(hy_done, 2 * (j + 1))
                part.wait_filled(dve, "w2", b)
                for half in range(2):
                    t = 2 * b + half
                    last = dve.scalar_tensor_tensor(hy[:, t, :], part.g("w2", b)[0:T, half * D:(half + 1) * D],
                                                    r2[:, t:t + 1], hy[:, t, :], ALU.mult, ALU.add)
                last.then_inc(evacuated[part.bank("w2", b)], 1)
                if b == 1:
                    part.wait_evacuated(dve, "w2", b)
                    stats(hy, mv2, ln2_stats)

            def second_norm(part, j):
                dve.wait_ge(ln2_scales, j + 1)
                dve.wait_ge(xn2_stored, 16 * (j + 1))
                for t in range(NT):
                    last = dve.tensor_scalar(xn2[:, t, :], hy[:, t, :], mv2[:, t, 0:1], rstd2[:, t:t + 1],
                                             ALU.subtract, ALU.mult)
                last.then_inc(xn2_done, 1)

            def router_transposed(part):
                evacuate(part, ("rtT", 0), logitsT)

            def router_out(part, j):
                part.wait_filled(dve, "rt", 0)
                at = NT * j
                dst = logits[:, at:at + NT, :] if isinstance(j, int) else logits[:, bass.ds(at, NT), :]
                dve.tensor_copy(dst, part.g("rt", 0)[0:T, 0:NT * NE].rearrange(
                    "p (t e) -> p t e", e=NE)).then_inc(evacuated[part.bank("rt", 0)], 1)

            def tail(part, j):
                for b in range(2):
                    part.wait_filled(dve, "wo", b)
                    dve.tensor_tensor(y2[:, 2 * b:2 * b + 2, :], part.g("wo", b)[0:T, :].rearrange("p (t d) -> p t d", d=D),
                                      xa[:, 2 * b:2 * b + 2, :], ALU.add).then_inc(evacuated[part.bank("wo", b)], 1)

            def masked_probs(part, j):
                first = part.kind == "first"
                qkT_evacuate(part, 1)
                for g in range(NG):
                    pair = g % (H // 2)
                    dve.wait_ge(exp_done, NG * j + (g + 1))
                    if not (first and g < 2):
                        dve.wait_ge(pv_done, NG * j + (g - 1))
                    dve.tensor_tensor(pm[g % 2][:, :, :], p0[g % 2][:, :, :], bias_t[:, 2 * pair:2 * pair + 2, :],
                                      ALU.mult).then_inc(probs_done, 1)
                    if g % 2 == 0 and g + 3 < H // 2:
                        qkT_evacuate(part, g + 3)
                    if g == NG // 2:
                        normalise_outputs(j, 0)
                    if not first and g == 0:
                        mlp_out(part, j - 1, 0)
                    if not first and g == 5:
                        mlp_out(part, j - 1, 1)
                    if not first and g == 7:
                        second_norm(part, j - 1)
                    if not first and g == 11:
                        router_transposed(part)
                    if not first and g == 12:
                        router_out(part, j - 1)
                normalise_outputs(j, 1)

            part = Part("first", 0)
            front_a(part, 0, True)
            front_b(part, 0)
            qk_norm(part, 0)
            masked_probs(part, 0)

            def iteration(part, i):
                front_a(part, i, False)
                tail(part, i - 1)
                front_b(part, i)
                qk_norm(part, i)
                masked_probs(part, i)

            with eng.Fori(1, PAIRS - 1) as i:
                chain.enter(i - 1, 25)
                iteration(Part("body", i), i)
            chain.leave(PAIRS - 2)
            iteration(Part("final", PAIRS - 1), PAIRS - 1)
            j = PAIRS - 1
            part = Part("last", PAIRS)
            tail(part, j)
            relu(part, range(4, MC))
            mlp_out(part, j, 0)
            mlp_out(part, j, 1)
            second_norm(part, j)
            router_transposed(part)
            router_out(part, j)

            part.wait_evacuated(dve, "rt", 0)
            dve.wait_ge(h1_stored, 16 * (PAIRS + 1))
            dve.wait_ge(xn2_stored, 16 * (PAIRS + 1))
            dve.reduce_max(smax[:, :], logits[:, :, :], AX.X).then_inc(phase2_init, 1)
            dve.wait_ge(phase2_init, 1)
            dve.tensor_tensor(score[:, :, :], logits[:, :, :], smax[:, :].unsqueeze(2).to_broadcast([T, NTILES, NE]),
                              ALU.subtract).then_inc(shifted, 1)
            dve.memset(bitv[:, :], float(1 << 29))
            dve.memset(thr[:, :], 0)
            dve.memset(slot_a[:, NE, :], 0.0)
            dve.memset(slot_b[:, NE, :], -1.0)
            step(dve.memset(zero_w[:, :], 0.0))
            step(dve.tensor_copy(biti[:, :], bitv[:, :]))
            dve.wait_ge(exps_done, 1)
            step(dve.reduce_sum(smax[:, :], score[:, :, :], AX.X))
            step(dve.reciprocal(smax[:, :], smax[:, :]))
            dve.tensor_tensor(score[:, :, :], score[:, :, :], smax[:, :].unsqueeze(2).to_broadcast([T, NTILES, NE]),
                              ALU.mult).then_inc(score_ready, 1)
            dve.wait_ge(score_ready, 1)
            dve.tensor_copy(by_group[:, :, :].rearrange("p g (r e) -> p r g e", e=NE),
                            score[:, :, :].rearrange("p (r g) e -> p r g e", g=GT)).then_inc(score_ready, 1)

            dve.wait_ge(scoreT_filled, 1)
            for k in range(2):
                last = dve.tensor_copy(scoreT[:, k * 4 * T:(k + 1) * 4 * T], SC[1][:, k, 0:4 * T])
            step(last)
            with eng.Fori(0, 30) as k:
                chain.enter(k, 5)
                step(dve.tensor_tensor(cand[:, :], thr[:, :], biti[:, :], ALU.bitwise_or))
                dve.tensor_scalar(hit[:, :], scoreT[:, :], cand[:, :].bitcast(F32), None, ALU.is_ge, ALU.add,
                                  accum_out=cnt[:, 0:1]).then_inc(counts_ready, 1)
                dve.wait_ge(counts_summed, k + 1)
                step(dve.tensor_scalar(kept[:, :], Y[1][:, 0:1], float(CAP), bitv[:, 0:1], ALU.is_ge, ALU.mult))
                step(dve.tensor_tensor(thr[:, :], thr[:, :], kept[:, :], ALU.bitwise_or))
                step(dve.tensor_scalar(bitv[:, :], bitv[:, :], 0.5, None, ALU.mult))
                step(dve.tensor_copy(biti[:, :], bitv[:, :]))
            chain.leave(30)
            tf = thr[:, :].bitcast(F32)
            dve.tensor_scalar(above[:, :], scoreT[:, :], tf, None, ALU.is_gt, ALU.add, accum_out=cnt[:, 1:2])
            dve.tensor_scalar(equal[:, :], scoreT[:, :], tf, None, ALU.is_equal, ALU.add,
                              accum_out=cnt[:, 2:3]).then_inc(counts_ready, 1)
            dve.wait_ge(counts_ready, 31)
            step(dve.tensor_tensor_scan(rank[:, :], equal[:, :], equal[:, :], 0.0, ALU.add, ALU.max))
            dve.wait_ge(offs_summed, 1)
            step(dve.tensor_scalar(need[:, 0:1], Y[1][:, 1:2], -1.0, float(CAP), ALU.mult, ALU.add))
            step(dve.tensor_tensor(need[:, 1:2], need[:, 0:1], Y[1][:, 2:3], ALU.subtract))
            step(dve.scalar_tensor_tensor(hit[:, :], rank[:, :], need[:, 1:2], equal[:, :], ALU.is_le, ALU.mult))
            dve.scalar_tensor_tensor(above[:, :], above[:, :], 0.0, hit[:, :], ALU.add, ALU.add,
                                     accum_out=cnt[:, 3:4]).then_inc(offs_ready, 1)
            dve.wait_ge(offs_ready, 1)
            step(dve.tensor_tensor_scan(rank[:, :], above[:, :], above[:, :], 0.0, ALU.add, ALU.max))
            dve.wait_ge(offs_summed, 2)
            step(dve.scalar_tensor_tensor(rank[:, :], rank[:, :], Y[1][:, 3:4], above[:, :], ALU.add, ALU.mult))
            dve.tensor_scalar(rank[:, :], rank[:, :], -1.0, None, ALU.add).then_inc(pos_ready, 1)
            dve.wait_ge(posT_filled, 1)
            for k in range(2):
                src = SC[1][0:T, k, :].rearrange("p (g r e) -> p g r e", g=GT // 2, e=NE)
                dst = posi[:, :, :].rearrange("p (r g) e -> p g r e", g=GT)[:, k * (GT // 2):(k + 1) * (GT // 2)]
                last = dve.tensor_copy(dst, src)
            step(last)
            step(dve.tensor_scalar(posh[:, :, :], posi[:, :, :], SLOTC - 1, None, ALU.bitwise_and))
            dve.tensor_copy(slot_a[:, 0:NE, :], posh[:, :, :].rearrange("p t e -> p e t"))
            step(dve.tensor_scalar(posi[:, :, :], posi[:, :, :], SLOTC.bit_length() - 1, None, ALU.arith_shift_right))
            step(dve.tensor_copy(slot_b[:, 0:NE, :], posi[:, :, :].rearrange("p t e -> p e t")))

            flat_a = slot_a[:, :, :].rearrange("p e t -> p (e t)")
            flat_b = slot_b[:, :, :].rearrange("p e t -> p (e t)")

            def onehots(k, n, tile_at, wait=True):
                if wait:
                    dve.wait_ge(onehot_used, n - 1)
                bs = flat_b[:, bass.ds(n * LT, LT)].unsqueeze(2).to_broadcast([T, LT, T])
                as_ = flat_a[:, bass.ds(n * LT, LT)].unsqueeze(2).to_broadcast([T, LT, SLOTC])
                ts = iota_b[:, bass.ds(tile_at, LT)].unsqueeze(2).to_broadcast([T, LT, SLOTC])
                dve.tensor_tensor(oh_b[k][:, :, :], bs, iota_b[:, 0:T].unsqueeze(1).to_broadcast([T, LT, T]), ALU.is_equal)
                step(dve.tensor_tensor(eq_a[k][:, :, :], as_, iota_b[:, 0:SLOTC].unsqueeze(1).to_broadcast([T, LT, SLOTC]),
                                       ALU.is_equal))
                dve.tensor_scalar(oh_a[k][:, :, 0, :], eq_a[k][:, :, :], tok_p[:, 0:1], None, ALU.mult)
                dve.tensor_tensor(oh_a[k][:, :, 1, :], eq_a[k][:, :, :], ts, ALU.mult).then_inc(onehot_ready, 1)

            def close_list(e):
                dve.wait_ge(onehot_used, (e + 1) * GROUPS)
                step(dve.tensor_scalar(idx_t[:, :], Y[0][0:T, SLOTC:2 * SLOTC], float(T), None, ALU.mult))
                dst = idx_all[:, bass.ds(e * SLOTC, SLOTC)]
                dve.tensor_tensor(dst, idx_t[:, :], Y[0][0:T, 0:SLOTC], ALU.add).then_inc(list_done, 1)

            for p in range(GROUPS):
                onehots(p % 2, p, p * LT, wait=p >= 2)
            close_list(0)
            dve.wait_ge(filled2[1], 1)
            dve.tensor_copy(xgT[:, 1, :], G2[1][:, 0:W]).then_inc(evacuated2[1], 1)
            dve.wait_ge(fb2_in, 16)

            def group(e, half_n, k, q, last_of_expert):
                n = half_n * 2 + k
                onehots(k, n + GROUPS, (q * 2 + k) * LT)
                if last_of_expert:
                    close_list(e + 1)
                key = ("xT", 1)
                dve.wait_ge(filled2[bank2(key)], count2(n, key))
                dve.tensor_copy(xgT[:, 1, :], G2[bank2(key)][:, 0:W]).then_inc(evacuated2[bank2(key)], 1)
                for b in range(2):
                    key = ("w2", b)
                    dve.wait_ge(filled2[bank2(key)], count2(n, key))
                    bias = fb2b[:, :, :].rearrange("p e d -> p (e d)")[:, bass.ds(e * D, D)]
                    dve.tensor_tensor(biased[:, :, :], G2[bank2(key)][0:T, :].rearrange("p (t d) -> p t d", d=D),
                                      bias.unsqueeze(1).to_broadcast([T, 2, D]), ALU.add).then_inc(evacuated2[bank2(key)], 1)
                    wait_evacuated2(dve, n, key)
                    for half in range(2):
                        t = 2 * b + half
                        last = dve.tensor_scalar(contrib[k][:, t, :], biased[:, half, :],
                                                 xg[k][:, t, bass.ds(e + D, 1)], None, ALU.mult)
                    if b == 1:
                        last.then_inc(contrib_done, 1)
                    else:
                        step(last)

            with eng.Fori(0, NE) as e:
                chain.enter(e, 2 * GROUPS + 1)
                with eng.Fori(0, GROUPS // 2 - 1) as q:
                    chain.enter(q, 4)
                    for k in range(2):
                        group(e, e * (GROUPS // 2) + q, k, q, False)
                chain.leave(GROUPS // 2 - 1)
                for k in range(2):
                    group(e, e * (GROUPS // 2) + (GROUPS // 2 - 1), k, GROUPS // 2 - 1, k == 1)
            chain.leave(NE)

        pool = nc.gpsimd

        @block.gpsimd
        def _(eng):
            chain = Chain(pool, pool_step, lambda: wait_apart(pool))
            step = chain.step
            for s in (xn2_stored, h1_stored):
                pool.sem_inc(s, 16)
            for s in (xn2_done, contrib_done, *evacuated2):
                pool.sem_inc(s, 1)
            step(pool.memset(ident[:, :], 0.0))
            pool.affine_select(out=ident[:, :], in_=ident[:, :], compare_op=ALU.not_equal, fill=1.0, base=0,
                               pattern=[[-1, 128]], channel_multiplier=1).then_inc(pool_consts, 1)
            step(pool.memset(first_col[:, :], 0.0))
            pool.memset(first_col[:, 0:1], 1.0).then_inc(pool_consts, 1)
            pool.memset(ln_eps[:, :], LN_EPS)
            pool.memset(rms_eps[:, :], RMS_EPS)
            pool.memset(neg_half[:, :], -0.5).then_inc(pool_consts, 1)
            pool.iota(diff[:, :], [[1, 128]], base=128, channel_multiplier=-1).then_inc(pool_consts, 1)
            pool.iota(iota_i[:, :], [[1, 128]], base=0, channel_multiplier=0).then_inc(pool_consts, 1)
            pool.iota(tok_pi[:, :], [[1, 1]], base=0, channel_multiplier=1).then_inc(pool_consts, 1)
            pool.wait_ge(pool_consts, 6)

            def rsqrt(dst, src, n):
                return pool.tensor_tensor(dst, src, neg_half[0:T, 0:n], ALU.pow)

            def first_norm(j):
                pool.wait_ge(ln1_stats, j + 1)
                step(pool.tensor_tensor(lt[:, 0, :], mv1[:, :, 1], ln_eps[:, 0:NT], ALU.add))
                step(rsqrt(lt[:, 1, :], lt[:, 0, :], NT))
                step(pool.tensor_tensor(lt[:, 2, :], lt[:, 1, :], lt[:, 1, :], ALU.mult))
                step(pool.tensor_tensor(lt[:, 2, :], lt[:, 2, :], mv1[:, :, 1], ALU.mult))
                step(pool.tensor_tensor(lt[:, 3, :], lt[:, 2, :], rms_eps[:, 0:NT], ALU.add))
                step(rsqrt(lt[:, 4, :], lt[:, 3, :], NT))
                pool.tensor_tensor(lt[:, 5, :], lt[:, 4, :], lt[:, 1, :], ALU.mult).then_inc(ln1_scales, 1)

            def residuals(part, j):
                pool.wait_ge(h1_stored, 16 * (j + 1))
                pool.wait_ge(xn2_done, j + 1)
                for b in range(2):
                    part.wait_evacuated(pool, "wo", b)
                    ts = slice(2 * b, 2 * b + 2)
                    pool.tensor_tensor(hy[:, ts, :], y2[:, ts, :], h0_copy[:, ts, :], ALU.add).then_inc(hy_done, 1)

            def keep_h0(j):
                pool.tensor_copy(h0_copy[:, :, :], h0[:, :, :]).then_inc(h0_kept, 1)

            def second_rms(j):
                pool.wait_ge(y2_sums, j + 1)
                step(pool.tensor_tensor(ss2[:, :], ss2[:, :], rms_eps[:, 0:NT], ALU.add))
                rsqrt(r2[:, :], ss2[:, :], NT).then_inc(r2_done, 1)

            def second_norm(j):
                pool.wait_ge(ln2_stats, j + 1)
                step(pool.tensor_tensor(rstd2[:, :], mv2[:, :, 1], ln_eps[:, 0:NT], ALU.add))
                rsqrt(rstd2[:, :], rstd2[:, :], NT).then_inc(ln2_scales, 1)

            def high_parts_again(j):
                for t in range(NT):
                    scaled = NT * j + (t + 1)
                    if not isinstance(scaled, int):
                        scaled = pool.snap(pool.to_reg(scaled))
                        wait_apart(pool)
                    pool.wait_ge(qk_scaled, scaled)
                    src = qkraw[:, t, 0:D].rearrange("p (h d) -> p h d", d=HD)
                    last = pool.tensor_copy(qkp[:, t, 0:H, 2 * HD:3 * HD], src)
                last.then_inc(qk_copied, 1)

            first_norm(0)
            keep_h0(0)
            high_parts_again(0)

            def iteration(part, i):
                first_norm(i)
                residuals(part, i - 1)
                second_rms(i - 1)
                keep_h0(i)
                high_parts_again(i)
                second_norm(i - 1)

            with eng.Fori(1, PAIRS - 1) as i:
                chain.enter(i - 1, 8)
                iteration(Part("body", i), i)
            chain.leave(PAIRS - 2)
            iteration(Part("final", PAIRS - 1), PAIRS - 1)
            residuals(Part("last", PAIRS), PAIRS - 1)
            second_rms(PAIRS - 1)
            second_norm(PAIRS - 1)

            def gather(n, k):
                step(pool.tensor_copy(idx_cur[k][:, :], idx_all[:, bass.ds(n * NT, NT)]), apart=True)
                for t in range(NT):
                    pool.indirect_dma_start(
                        out=xg[k][:, t, :], out_offset=None, in_=xd[:, :],
                        in_offset=bass.IndirectOffsetOnAxis(ap=idx_cur[k][:, t:t + 1], axis=0)).then_inc(gathered[k], 16)

            def scatter(n, k):
                if isinstance(n, int):
                    pool.wait_ge(contrib_done, n + 2)
                else:
                    done = pool.snap(pool.to_reg(n + 2))
                    wait_apart(pool)
                    pool.wait_ge(contrib_done, done)
                for t in range(NT):
                    pool.indirect_dma_start(
                        out=out_rows, out_offset=bass.IndirectOffsetOnAxis(ap=idx_cur[k][:, t:t + 1], axis=0),
                        in_=contrib[k][:, t, :], in_offset=None, compute_op=ALU.add).then_inc(scattered[k], 16)

            def group(half_n, k):
                n = half_n * 2 + k
                pool.wait_ge(contrib_done, n + 1)
                before = (half_n + k) * (16 * NT)
                if not isinstance(before, int) or before:
                    pool.wait_ge(scattered[1 - k], before)
                gather(n + 1, 1 - k)
                scatter(n, k)

            def expert(e, first):
                if not first:
                    former = pool.snap(pool.to_reg(e * (GROUPS // 2 * 16 * NT)))
                    wait_apart(pool)
                    for k in range(2):
                        pool.wait_ge(scattered[k], former)
                else:
                    for k in range(2):
                        group(0, k)
                peeled = int(first)
                with eng.Fori(peeled, GROUPS // 2 - 1) as q:
                    chain.enter(q - peeled, 2)
                    for k in range(2):
                        group(e * (GROUPS // 2) + q, k)
                chain.leave(GROUPS // 2 - 1 - peeled)
                half_n = e * (GROUPS // 2) + (GROUPS // 2 - 1)
                group(half_n, 0)
                pool.wait_ge(list_done, e + 2)
                group(half_n, 1)

            pool.wait_ge(score_stored, 16)
            pool.wait_ge(h1_stored, 16 * (PAIRS + 1))
            pool.wait_ge(xn2_stored, 16 * (PAIRS + 1))
            pool.wait_ge(list_done, 1)
            gather(0, 0)
            expert(0, True)
            with eng.Fori(1, NE) as e:
                chain.enter(e - 1, GROUPS)
                expert(e, False)
            chain.leave(NE - 1)
            for k in range(2):
                pool.wait_ge(scattered[k], NE * GROUPS // 2 * 16 * NT)
            pool.wait_ge(gathered[0], (NE * GROUPS // 2 + 1) * 16 * NT)


_INS = ['x', 'txt', 'L0_tok_W1', 'L0_tok_b1', 'L0_tok_W2', 'L0_tok_b2', 'L0_attn_ln1_w', 'L0_attn_Wq', 'L0_attn_Wk',
        'L0_attn_Wv', 'L0_attn_rel_bias', 'L0_attn_scale', 'L0_attn_Wo', 'L0_attn_ln2_w', 'L0_attn_W1', 'L0_attn_W2',
        'L0_ffn_Wr', 'L0_ffn_W1', 'L0_ffn_b1', 'L0_ffn_W2', 'L0_ffn_b2']
_OUTS = [((64, 228, 256), 'float32')]


def kernel(**inputs):
    import numpy as _np
    import concourse.bacc as _bacc
    from concourse import mybir as _mybir
    from concourse.bass_utils import run_bass_kernel_spmd as _run

    nc = _bacc.Bacc("TRN2", target_bir_lowering=False, num_devices=1)
    arrays, args = {}, []
    for name in _INS:
        a = _np.ascontiguousarray(inputs[name])
        arrays[f"in_{name}_dram"] = a
        args.append(nc.dram_tensor(f"in_{name}_dram", a.shape, _mybir.dt.from_np(a.dtype), kind="ExternalInput").ap())
    for i, (shape, dtype) in enumerate(_OUTS):
        dt = _mybir.dt.from_np(_np.dtype(dtype))
        args.append(nc.dram_tensor(f"out_{i}_dram", shape, dt, kind="ExternalOutput").ap())
    early_fusion_kernel(nc, *args)
    r = _run(nc, [arrays], core_ids=[0])
    return r.results[0]["out_0_dram"]
```

```python
import concourse.bass as bass
from concourse import mybir
from contextlib import ExitStack
import numpy as np


def relative_bucket_runs(distances, buckets, max_distance):
    exact = buckets // 2
    n = np.arange(1, distances, dtype=np.int32)
    large = exact + (np.log(n.astype(np.float32) / np.float32(exact))
                     / np.float32(np.log(max_distance / exact)) * np.float32(buckets - exact)).astype(np.int32)
    bucket = np.where(n < exact, n, np.minimum(large, buckets - 1))
    runs = []
    for d, k in zip(n.tolist(), bucket.tolist()):
        if runs and runs[-1][2] == k:
            runs[-1][1] += 1
        else:
            runs.append([d, 1, k])
    return runs


class Chain:
    def __init__(self, eng, sem, wait_apart):
        self.wait_apart = wait_apart
        self.eng, self.sem, self.base, self.n, self.loops = eng, sem, 0, 0, []

    def step(self, ins, apart=False):
        ins.then_inc(self.sem, 1)
        self.n += 1
        value = self.base + self.n
        if apart and not isinstance(value, int):
            value = self.eng.snap(self.eng.to_reg(value))
            self.wait_apart()
        self.eng.wait_ge(self.sem, value)

    def enter(self, trip, steps):
        self.loops.append((self.base, self.n, steps))
        self.base, self.n = trip * steps + (self.base + self.n), 0

    def leave(self, trips):
        base, n, steps = self.loops.pop()
        assert self.n == steps, (self.n, steps)
        self.base, self.n = base, n + trips * steps


def early_fusion_kernel(nc, x, txt, tok_W1, tok_b1, tok_W2, tok_b2, ln1_w, Wq, Wk, Wv, rel_bias, scale, Wo,
                        ln2_w, W1, W2, Wr, fW1, fb1, fW2, fb2, out):
    F32, BF16, F16, I32, U32 = mybir.dt.float32, mybir.dt.bfloat16, mybir.dt.float16, mybir.dt.int32, mybir.dt.uint32
    ALU, ACT, AX = mybir.AluOpType, mybir.ActivationFunctionType, mybir.AxisListType

    B, C, IMG, _ = x.shape
    TXT, D = txt.shape[1], txt.shape[2]
    PS = 16
    GP = IMG // PS
    NP_ = GP * GP
    S = NP_ + TXT
    T = S // 2
    LASTP = NP_ - T
    N = B * S
    PAIRS = B // 2
    NT = 4
    W = NT * T
    NTILES = N // T
    H = scale.shape[0]
    HD = D // H
    HV = HD + 1
    HP = 64
    NBUCK = rel_bias.shape[0]
    KC = D // 128
    HID = W1.shape[1]
    MC = HID // 128
    NE = Wr.shape[1]
    CAP = max(4, -(-2 * N // NE))
    GROUPS = CAP // W
    SLOTC = CAP // T
    R = 128 // NE
    GT = NTILES // R
    SEG = GT * T
    KROW = C * PS
    HALF = PS // 2
    QW = S + T
    XW = D + NE
    LN_EPS, RMS_EPS = 1e-5, 1e-6
    LT = NTILES // GROUPS
    SAFE = 75.0
    assert CAP == GROUPS * W and T <= 128 and LASTP > 0 and NTILES == R * GT and SLOTC == 32

    xd = nc.dram_tensor("xn_rows", (N, XW), F32)
    zrow_d = nc.dram_tensor("bias_by_distance", (H, T, 2 * S - 1 + T), F32)
    mrow_d = nc.dram_tensor("bias_row_maximum", (H, S), F32)
    out_rows = out.rearrange("b s d -> (b s) d")

    ctx = ExitStack()
    with ctx:
        def sb(name, shape, dt=F32, stack=ctx):
            return stack.enter_context(nc.sbuf_tensor(name, shape, dt))

        def sem(name):
            return ctx.enter_context(nc.semaphore(name))

        logits = sb("logits", [T, NTILES, NE])
        ident = sb("ident", [128, 128])
        group_ones = sb("group_ones", [128, 128])
        earlier_ones = sb("earlier_ones", [128, 128])
        diff = sb("diff", [128, 128], I32)
        difff = sb("difff", [128, 128])
        neg_half = sb("neg_half", [T, 128])
        ln_eps = sb("ln_eps", [T, 128])
        rms_eps = sb("rms_eps", [T, 128])
        tok_p = sb("tok_p", [T, 1])
        tok_pi = sb("tok_pi", [T, 1], I32)
        diff_low = sb("diff_low", [128, 128], I32)
        iota_i = sb("iota_i", [T, 128], I32)
        iota_b = sb("iota_b", [T, 128], BF16)
        first_col = sb("first_col", [T, T])
        all_ones = sb("all_ones", [128, 128])
        fb1c = sb("fb1c", [128, NE, MC])

        p1 = ExitStack()

        def s1(name, shape, dt=F32):
            return sb(name, shape, dt, p1)

        w1t = s1("w1t", [2 * KROW, HALF, D])
        w2t = s1("w2t", [128, KC, D])
        b1t = s1("b1t", [128, KC])
        b2t = s1("b2t", [T, D])
        wqkv = s1("wqkv", [128, KC, 3 * D])
        wo = s1("wo", [128, KC, D])
        w1m = s1("w1m", [128, KC, HID])
        w2m = s1("w2m", [128, MC, D])
        wr = s1("wr", [128, KC, NE])
        lnw = s1("lnw", [128, 2, KC])
        relb = s1("relb", [H, NBUCK])
        sc_col = s1("sc_col", [H, 1])
        zrow = s1("zrow", [H, 2 * S - 1])
        mrow = s1("mrow", [H, S])
        bias_t = s1("bias_t", [T, H, QW])
        sc_bc = s1("sc_bc", [T, H])
        sc_q = s1("sc_q", [T, NT, H])
        shift = s1("shift", [T, 2, H])
        img = [s1(f"img{b}", [2 * KROW, GP * IMG]) for b in range(2)]
        hid = s1("hid", [128, KC, 2 * NP_])
        h0 = s1("h0", [T, NT, D])
        xa = s1("xa", [T, NT, D])
        xs = s1("xs", [T, NT, D])
        xsT = s1("xsT", [128, KC, W])
        qkraw = s1("qkraw", [T, NT, 2 * D])
        sqb = s1("sqb", [T, 2 * D])
        logitsT = sqb[0:NE, 0:W]
        ss = s1("ss", [T, NT, 2 * H])
        rn = s1("rn", [T, NT, 2 * H])
        qkp = s1("qkp", [T, NT, 2 * H, HP], F16)
        qkT = s1("qkT", [128, H // 2, 2, W], F16)
        v1 = s1("v1", [T, NT, H, HV])
        p0 = [s1(f"p0_{k}", [T, 2, QW]) for k in range(2)]
        pm = [s1(f"pm_{k}", [T, 2, QW]) for k in range(2)]
        nwt = s1("nwt", [T, NT * 2 * H])
        ident_h = s1("ident_h", [T, T], F16)
        yrec = s1("yrec", [T, 2, H])
        yn = s1("yn", [T, NT, D])
        yT = s1("yT", [128, KC, W])
        y2 = yn
        h0_copy = s1("h0_copy", [T, NT, D])
        hy = s1("hy", [T, NT, D])
        junk = s1("junk", [T, NT, D], BF16)
        hT = s1("hT", [128, MC, W])
        xn2 = s1("xn2", [T, NT, D])
        st = s1("st", [T, NT, 6])
        mv1 = s1("mv1", [T, NT, 2])
        mv2 = s1("mv2", [T, NT, 2])
        lt = s1("lt", [T, 6, NT])
        ss2 = s1("ss2", [T, NT])
        r2 = s1("r2", [T, NT])
        rstd2 = s1("rstd2", [T, NT])
        mtmp = [hT[0:T, :, :].rearrange("p m w -> p (m w)"), qkT[0:T, :, :, :].rearrange("p c s w -> p (c s w)").bitcast(F32)]
        p1.close()

        def s2(name, shape, dt=F32):
            return sb(name, shape, dt)

        score = s2("score", [T, NTILES, NE])
        by_group = s2("by_group", [T, GT, R * NE])
        smax = s2("smax", [T, NTILES])
        scoreT = s2("scoreT", [128, SEG])
        hit = s2("hit", [128, SEG])
        above = s2("above", [128, SEG])
        equal = s2("equal", [128, SEG])
        rank = s2("rank", [128, SEG])
        bitv = s2("bitv", [128, 1])
        biti = s2("biti", [128, 1], I32)
        cand = s2("cand", [128, 1], I32)
        kept = s2("kept", [128, 1], I32)
        thr = s2("thr", [128, 1], I32)
        cnt = s2("cnt", [128, 4])
        need = s2("need", [128, 2])
        posi = s2("posi", [T, NTILES, NE], I32)
        posh = s2("posh", [T, NTILES, NE], I32)
        slot_a = s2("slot_a", [T, NE + 1, NTILES], BF16)
        slot_b = s2("slot_b", [T, NE + 1, NTILES], BF16)
        oh_b = [s2(f"oh_b{k}", [T, LT, T], BF16) for k in range(2)]
        oh_a = [s2(f"oh_a{k}", [T, LT, 2, SLOTC], BF16) for k in range(2)]
        eq_a = [s2(f"eq_a{k}", [T, LT, SLOTC], BF16) for k in range(2)]
        zero_w = s2("zero_w", [T, T], BF16)
        idx_t = s2("idx_t", [T, 32])
        idx_all = s2("idx_all", [T, (NE + 1) * 32], U32)
        idx_cur = [s2(f"idx_cur{k}", [T, NT], U32) for k in range(2)]
        we1 = [s2(f"we1_{k}", [128, KC, HID]) for k in range(2)]
        we2 = [s2(f"we2_{k}", [128, MC, D]) for k in range(2)]
        fb2b = s2("fb2b", [T, NE, D])
        xg = [s2(f"xg{k}", [T, NT, XW]) for k in range(2)]
        xgT = s2("xgT", [128, 2, KC, W], F16)
        hTe = s2("hTe", [128, MC, W])
        hTs = s2("hTs", [128, 2, MC, W], F16)
        ws1 = [s2(f"ws1_{k}", [128, 2, KC, HID], F16) for k in range(2)]
        ws2 = [s2(f"ws2_{k}", [128, 2, MC, D], F16) for k in range(2)]
        sumsq = s2("sumsq", [128, 3, NE])
        b1sq = s2("b1sq", [128, NE, MC])
        norms = s2("norms", [128, 3, NE])
        half_exp = s2("half_exp", [128, 3, NE], I32)
        scales = s2("scales", [128, 3, NE], I32)
        unscales = s2("unscales", [128, 4, NE], I32)
        biased = s2("biased", [T, 2, D])
        contrib = [s2(f"contrib{k}", [T, NT, D]) for k in range(2)]

        def pb(name, shape):
            return ctx.enter_context(nc.psum_tensor(name, shape, F32))

        G = [pb(f"G{k}", [128, 512]) for k in range(2)]
        SC = [pb(f"SC{k}", [128, 2, 512]) for k in range(2)]
        Y = [pb(f"Y{k}", [128, 512]) for k in range(2)]

        tok_in, qkv_in, weights_in, consts_in = sem("tok_in"), sem("qkv_in"), sem("weights_in"), sem("consts_in")
        pool_consts = sem("pool_consts")
        zrow_ready, rows_out, toeplitz_in = sem("zrow_ready"), sem("rows_out"), sem("toeplitz_in")
        table_diff, table_exp, setup_done = sem("table_diff"), sem("table_exp"), sem("setup_done")
        img_in = [sem(f"img_in{b}") for b in range(2)]
        text_in = sem("text_in")
        filled = [sem(f"filled{k}") for k in range(2)]
        evacuated = [sem(f"evacuated{k}") for k in range(2)]
        ln1_stats, ln1_scales, xs_done = sem("ln1_stats"), sem("ln1_scales"), sem("xs_done")
        qk_scaled, qk_high, qk_copied, qk_normed = sem("qk_scaled"), sem("qk_high"), sem("qk_copied"), sem("qk_normed")
        scores_done, exp_done, probs_done, pv_done, y_normed = (
            sem("scores_done"), sem("exp_done"), sem("probs_done"), sem("pv_done"), sem("y_normed"))
        h0_kept, xa_done = sem("h0_kept"), sem("xa_done")
        hy_done, y2_sums, r2_done = sem("hy_done"), sem("y2_sums"), sem("r2_done")
        ln2_stats, ln2_scales, xn2_done = sem("ln2_stats"), sem("ln2_scales"), sem("xn2_done")
        h1_stored, xn2_stored = sem("h1_stored"), sem("xn2_stored")
        dve_step, pool_step = sem("dve_step"), sem("pool_step")
        exps_done, score_ready, score_stored = sem("exps_done"), sem("score_ready"), sem("score_stored")
        shifted = sem("shifted")
        scoreT_filled, counts_ready, counts_summed = sem("scoreT_filled"), sem("counts_ready"), sem("counts_summed")
        offs_ready, offs_summed, pos_ready, posT_filled, pos_copied = (
            sem("offs_ready"), sem("offs_summed"), sem("pos_ready"), sem("posT_filled"), sem("pos_copied"))
        phase2_init = sem("phase2_init")
        onehot_ready, onehot_used, list_filled, list_done = (
            sem("onehot_ready"), sem("onehot_used"), sem("list_filled"), sem("list_done"))
        idx_ready = sem("idx_ready")
        gathered = [sem(f"gathered{k}") for k in range(2)]
        scattered = [sem(f"scattered{k}") for k in range(2)]
        expert_in = [sem(f"expert_in{k}") for k in range(2)]
        fb2_in = sem("fb2_in")
        filled2 = [sem(f"filled2_{k}") for k in range(4)]
        evacuated2 = [sem(f"evacuated2_{k}") for k in range(4)]
        contrib_done = sem("contrib_done")
        squares_done, norms_summed, scales_ready = sem("squares_done"), sem("norms_summed"), sem("scales_ready")
        split_high, split_done = sem("split_high"), sem("split_done")
        h_high, h_split, x_high = sem("h_high"), sem("h_split"), sem("x_high")

        QKV = [("qk", 0), ("qk", 1), ("qk", 2), ("qk", 3), ("v", 0), ("v", 1)]
        BANKED = {
            "front": ([("xsT", 1)], [("xsT", 0)]),
            "qkv": ([("qk", 0), ("qk", 2), ("v", 0)], [("qk", 1), ("qk", 3), ("v", 1)]),
            "qkT": [("qkT", c) for c in range(H // 2)],
            "after": ([("yT", 1), ("wo", 0), ("y2T", 0)], [("yT", 0), ("wo", 1), ("y2T", 1)]),
            "router": [("x2T", 0), ("x2T", 1), ("rtT", 0), ("rt", 0)],
        }
        EARLY = 3
        w1_blocks = lambda k, lo, hi: [("w1", m) for m in range(lo, hi) if m % 2 == k]
        body = (
            [("tok2", 0)] + BANKED["after"][0] + w1_blocks(0, 0, EARLY) + BANKED["front"][0] + BANKED["qkv"][0]
            + w1_blocks(0, EARLY, MC) + [("w2", 0), ("w2", 1)] + BANKED["router"],
            [("yT", 0), ("tok2", 1)] + BANKED["after"][1][1:] + w1_blocks(1, 0, EARLY) + BANKED["front"][1]
            + w1_blocks(1, EARLY, EARLY + 1) + BANKED["qkv"][1] + w1_blocks(1, EARLY + 1, MC) + BANKED["qkT"],
        )
        ORDER = {
            "first": ([("tok1", 0), ("tok2", 0)] + BANKED["front"][0] + BANKED["qkv"][0] + [("next", 1)],
                      [("tok1", 1), ("tok2", 1)] + BANKED["front"][1] + BANKED["qkv"][1] + BANKED["qkT"] + [("next", 0)]),
            "body": (body[0] + [("next", 1)], body[1] + [("next", 0)]),
            "final": body,
            "last": (BANKED["after"][0] + w1_blocks(0, 0, MC) + [("w2", 0), ("w2", 1)] + BANKED["router"],
                     BANKED["after"][1] + w1_blocks(1, 0, MC)),
        }

        class Part:
            def __init__(self, kind, i):
                self.kind, self.i, self.order = kind, i, ORDER[kind]
                count = lambda k: [len(blocks) for blocks in ORDER[k]]
                if kind == "first":
                    self.base = [0, 0]
                elif kind == "last":
                    self.base = [f + (PAIRS - 2) * b + e for f, b, e in zip(count("first"), count("body"), count("final"))]
                else:
                    self.base = [f + (i - 1) * b for f, b in zip(count("first"), count("body"))]

            def bank(self, *key):
                return 0 if key in self.order[0] else 1

            def count(self, *key):
                k = self.bank(*key)
                return self.base[k] + (self.order[k].index(key) + 1)

            def wait_filled(self, eng, *key):
                eng.wait_ge(filled[self.bank(*key)], self.count(*key))

            def wait_evacuated(self, eng, *key):
                eng.wait_ge(evacuated[self.bank(*key)], self.count(*key))

            def wait_free(self, eng, *key):
                k = self.bank(*key)
                n = self.order[k].index(key)
                if self.kind != "first" or n >= 1:
                    eng.wait_ge(evacuated[k], self.base[k] + n)

            def g(self, *key):
                return G[self.bank(*key)]

        pe = nc.tensor
        NG = H

        def pe_block(part, key, ins):
            ins.then_inc(filled[part.bank(*key)], 1)

        def pe_transposes(part, key, src):
            part.wait_free(pe, *key)
            for t in range(NT):
                last = pe.transpose(part.g(*key)[:, t * T:(t + 1) * T], src(t), ident[0:T, 0:T])
            pe_block(part, key, last)

        def pe_tok1(part, key, steps, j):
            m = key[1]
            if steps[0] == 0:
                if m == 0:
                    for b in range(2):
                        pe.wait_ge(img_in[b], 16 * 2 * C * (j + 1))
                part.wait_free(pe, *key)
            for step_ in steps:
                b, q = step_ // HALF, step_ % HALF
                last = pe.matmul(part.g(*key)[:, b * NP_:(b + 1) * NP_], w1t[:, q, m * 128:(m + 1) * 128],
                                 img[b][:, q:q + PS * (NP_ - 1) + 1:PS], start=q == 0, stop=q == HALF - 1)
            if steps[-1] == 2 * HALF - 1:
                pe_block(part, key, last)

        def pe_tok2(part, j, b):
            if b == 0:
                if part.kind == "first":
                    for m in range(KC):
                        part.wait_evacuated(pe, "tok1", m)
                else:
                    for k in range(2):
                        pe.wait_ge(evacuated[k], part.base[k])
            part.wait_free(pe, "tok2", b)
            for half in range(2):
                n = T if half == 0 else LASTP
                at = b * NP_ + half * T
                for m in range(KC):
                    last = pe.matmul(part.g("tok2", b)[0:n, half * D:(half + 1) * D], hid[:, m, at:at + n],
                                     w2t[:, m, :], start=m == 0, stop=m == KC - 1)
            pe_block(part, ("tok2", b), last)

        def pe_xsT(part, j):
            pe.wait_ge(xs_done, j + 1)
            for c in range(KC):
                pe_transposes(part, ("xsT", c), lambda t: xs[:, t, c * 128:(c + 1) * 128])

        def pe_qkv(part, j):
            for c in range(KC):
                part.wait_evacuated(pe, "xsT", c)
            for key in QKV:
                part.wait_free(pe, *key)
                if key[0] == "qk":
                    t = key[1]
                    for c in range(KC):
                        last = pe.matmul(part.g(*key)[0:T, :], xsT[:, c, t * T:(t + 1) * T], wqkv[:, c, 0:2 * D],
                                         start=c == 0, stop=c == KC - 1)
                else:
                    for half in range(2):
                        t = 2 * key[1] + half
                        for c in range(KC):
                            last = pe.matmul(part.g(*key)[0:T, half * D:(half + 1) * D], xsT[:, c, t * T:(t + 1) * T],
                                             wqkv[:, c, 2 * D:], start=c == 0, stop=c == KC - 1)
                pe_block(part, key, last)

        def pe_qkT(part, j, c):
            if c == 0:
                pe.wait_ge(qk_normed, j + 1)
                pe.wait_ge(qk_copied, j + 1)
            key = ("qkT", c)
            part.wait_free(pe, *key)
            dst = part.g(*key)[:, 0:W].bitcast(F16)
            for s in range(2):
                for t in range(NT):
                    h = s * H + 2 * c
                    last = pe.transpose(dst[:, s * W + t * T:s * W + (t + 1) * T],
                                        qkp[:, t, h:h + 2, :].rearrange("p h d -> p (h d)"), ident_h[:, :])
            pe_block(part, key, last)

        def pe_scores(part, j, g, first):
            b, pair = g // (H // 2), g % (H // 2)
            if b == 0:
                part.wait_evacuated(pe, "qkT", pair)
            if not (first and g < 2):
                pe.wait_ge(exp_done, NG * j + (g - 1))
            for hh in range(2):
                lo = HP * hh
                rows = slice(lo, lo + HP)
                o = b * S
                dst = SC[g % 2]
                pe.matmul(dst[0:T, hh, 0:S], qkT[rows, pair, 1, o:o + T], qkT[rows, pair, 0, o:o + S],
                          start=True, stop=True)
                last = pe.matmul(dst[0:T, hh, S:QW], qkT[rows, pair, 1, o + T:o + S], qkT[rows, pair, 0, o + T:o + S],
                                 start=True, stop=True)
            last.then_inc(scores_done, 1)

        def pe_pv(part, j, g, hh, first):
            b, pair = g // (H // 2), g % (H // 2)
            h = 2 * pair + hh
            if hh == 0:
                pe.wait_ge(probs_done, NG * j + (g + 1))
            if h == 0:
                if not (first and b == 0):
                    pe.wait_ge(y_normed, 2 * j + b)
                pe.matmul(Y[0][0:T, 0:H * HV], first_col[:, :], v1[:, 2 * b + 1, :, :].rearrange("p h d -> p (h d)"),
                          start=True, stop=False, skip_group_check=True)
            cols = slice(h * HV, (h + 1) * HV)
            pe.matmul(Y[1][0:T, cols], pm[g % 2][:, hh, T:S], v1[:, 2 * b, h, :],
                      start=h == 0, stop=False, skip_group_check=True)
            pe.matmul(Y[1][0:T, cols], pm[g % 2][:, hh, S:QW], v1[:, 2 * b + 1, h, :],
                      start=False, stop=h == H - 1, skip_group_check=True)
            last = pe.matmul(Y[0][0:T, cols], pm[g % 2][:, hh, 0:T], v1[:, 2 * b, h, :],
                             start=False, stop=h == H - 1, skip_group_check=True)
            if hh == 1:
                last.then_inc(pv_done, 1)

        def pe_w1(part, m):
            part.wait_free(pe, "w1", m)
            for c in range(KC):
                if m == 0:
                    part.wait_evacuated(pe, "y2T", c)
                last = pe.matmul(part.g("w1", m)[:, 0:W], w1m[:, c, m * 128:(m + 1) * 128], yT[:, c, :],
                                 start=c == 0, stop=c == KC - 1)
            pe_block(part, ("w1", m), last)

        def pe_w2(part, pieces):
            for n in pieces:
                b, t = n // 8, n // 4
                if n == 0:
                    for m in range(MC - 2, MC):
                        part.wait_evacuated(pe, "w1", m)
                if n % 8 == 0:
                    part.wait_free(pe, "w2", b)
                at = (t % 2) * D
                for m in range(2 * (n % 4), 2 * (n % 4) + 2):
                    last = pe.matmul(part.g("w2", b)[0:T, at:at + D], hT[:, m, t * T:(t + 1) * T], w2m[:, m, :],
                                     start=m == 0, stop=m == MC - 1)
                if n % 8 == 7:
                    pe_block(part, ("w2", b), last)

        SLOTS = {n: [] for n in range(2 * NG)}
        for n, slot in enumerate((0, 1, 3, 4, 5, 6, 7, 8, 9, 10)):
            SLOTS[slot].append(("w2", range(6 + n, 7 + n)))
        for slot, work in ((20, ("x2T", 0)), (21, ("x2T", 1)), (22, ("rtT", 0)), (23, ("rtT", 1)), (25, ("rt", 0))):
            SLOTS[slot].append(work)
        for m, steps in ((0, {11: 2, 12: 1, 13: 2, 14: 2, 15: 1, 16: 3, 17: 1, 18: 2, 19: 1, 24: 1}),
                         (1, {26: 3, 27: 3, 28: 3, 29: 3, 30: 2, 31: 2})):
            at = 0
            for slot, n in steps.items():
                SLOTS[slot].append(("next", m, range(at, at + n)))
                at += n
            assert at == 2 * HALF

        def pe_slot(part, j, slot):
            for work in SLOTS[slot]:
                if work[0] == "next" and part.kind != "final":
                    pe_tok1(part, ("next", work[1]), work[2], j + 1)
                elif part.kind != "first":
                    if work[0] == "w2":
                        pe_w2(part, work[1])
                    elif work[0] == "x2T":
                        pe_x2T(part, j - 1, work[1])
                    elif work[0] == "rtT":
                        pe_rtT(part, work[1])
                    elif work[0] == "rt":
                        pe_rt(part)

        def pe_attention(part, j):
            first = part.kind == "first"
            w2 = (lambda lo: None) if first else (lambda lo: pe_w2(part, range(lo, lo + 2)))
            w2(0)
            pe_qkT(part, j, 0)
            w2(2)
            pe_qkT(part, j, 1)
            pe_scores(part, j, 0, first)
            w2(4)
            pe_scores(part, j, 1, first)
            pe_qkT(part, j, 2)
            for g in range(NG):
                pe_slot(part, j, 2 * g)
                if g + 2 < NG:
                    pe_scores(part, j, g + 2, first)
                if g + 3 < H // 2:
                    pe_qkT(part, j, g + 3)
                pe_pv(part, j, g, 0, first)
                pe_slot(part, j, 2 * g + 1)
                pe_pv(part, j, g, 1, first)

        def pe_yT(part, j):
            pe.wait_ge(y_normed, 2 * (j + 1))
            for c in range(KC):
                pe_transposes(part, ("yT", c), lambda t: yn[:, t, c * 128:(c + 1) * 128])

        def pe_wo(part, j):
            for c in range(KC):
                part.wait_evacuated(pe, "yT", c)
            for b in range(2):
                part.wait_free(pe, "wo", b)
                for half in range(2):
                    t = 2 * b + half
                    for c in range(KC):
                        last = pe.matmul(part.g("wo", b)[0:T, half * D:(half + 1) * D], yT[:, c, t * T:(t + 1) * T],
                                         wo[:, c, :], start=c == 0, stop=c == KC - 1)
                pe_block(part, ("wo", b), last)

        def pe_y2T(part, j):
            for b in range(2):
                part.wait_evacuated(pe, "wo", b)
            for c in range(KC):
                pe_transposes(part, ("y2T", c), lambda t: y2[:, t, c * 128:(c + 1) * 128])

        def pe_x2T(part, j, c):
            if c == 0:
                pe.wait_ge(xn2_done, j + 2)
            pe_transposes(part, ("x2T", c), lambda t: xn2[:, t, c * 128:(c + 1) * 128])

        def pe_rtT(part, c):
            part.wait_evacuated(pe, "x2T", c)
            if c == 0:
                part.wait_free(pe, "rtT", 0)
            last = pe.matmul(part.g("rtT", 0)[0:NE, 0:W], wr[:, c, :], xsT[:, c, :], start=c == 0, stop=c == KC - 1)
            if c == KC - 1:
                pe_block(part, ("rtT", 0), last)

        def pe_rt(part):
            copied = part.count("rtT", 0)
            if not isinstance(copied, int):
                copied = pe.snap(pe.to_reg(copied))
                wait_apart(pe)
            pe.wait_ge(evacuated[part.bank("rtT", 0)], copied)
            for t in range(NT):
                last = pe.transpose(part.g("rt", 0)[0:T, t * NE:(t + 1) * NE], logitsT[:, t * T:(t + 1) * T],
                                    ident[0:NE, 0:NE])
            pe_block(part, ("rt", 0), last)

        G2 = [G[0], G[1], SC[0][:, 0, :], SC[0][:, 1, :]]
        BLK = {**{("w1", m): m for m in range(MC)}, ("w2", 0): MC, ("xT", 0): MC + 1, ("xT", 1): MC + 2,
               ("w2", 1): MC + 3}
        NBLK = len(BLK)
        assert NBLK % 4 == 0

        PARTS = ((0, 0), (0, 1), (1, 0))
        LOADS = NE // 2 * 32
        PIECES = 8

        def piece(buffers, p):
            flat = buffers[p // 4].rearrange("p a b -> p (a b)")
            n = flat.shape[1] // 4
            return flat[:, (p % 4) * n:(p % 4 + 1) * n]

        def split_pieces(eb, part, p):
            return piece((ws1[eb][:, part, :, :], ws2[eb][:, part, :, :]), p)

        def scale_at(tensor, kind, e, rows=128):
            flat = tensor[0:rows, :, :].rearrange("p k e -> p (k e)").bitcast(F32)
            at = e + kind * NE
            return flat[:, at:at + 1] if isinstance(at, int) else flat[:, bass.ds(at, 1)]

        def bank2(key):
            return (2 + BLK[key]) % 4

        def count2(n, key):
            return n * (NBLK // 4) + ((2 + BLK[key]) // 4 + 1)

        def wait_evacuated2(eng, n, key):
            eng.wait_ge(evacuated2[bank2(key)], count2(n, key) + 1)

        def wait_free2(eng, n, key):
            eng.wait_ge(evacuated2[bank2(key)], n * (NBLK // 4) + ((2 + BLK[key]) // 4 + 1))

        def wait_apart(eng):
            eng.wait_ge(pool_consts, 6)

        block = ctx.enter_context(nc.Block())

        @block.sync
        def _(sp):
            for half in range(2):
                for c in range(C):
                    src = tok_W1[c * PS * PS:(c + 1) * PS * PS, :].rearrange("(y x) d -> y x d", x=PS)
                    lo = half * KROW + c * PS
                    sp.dma_start(w1t[lo:lo + PS, :, :], src[:, half * HALF:(half + 1) * HALF, :]).then_inc(tok_in, 16)

            def load_images(j):
                for b in range(2):
                    for half in range(2):
                        for c in range(C):
                            lo = half * KROW + c * PS
                            src = x[2 * j + b] if isinstance(j, int) else x[bass.ds(2 * j + b, 1)].rearrange("o c y x -> (o c) y x")
                            src = src[c].rearrange("(g r) x -> r g x", r=PS)
                            n = IMG - half * HALF
                            dst = img[b][lo:lo + PS, :].rearrange("p (g x) -> p g x", x=IMG)
                            sp.dma_start(dst[:, :, 0:n], src[:, :, half * HALF:]).then_inc(img_in[b], 16)

            def load_text(j):
                if not (isinstance(j, int) and j == 0):
                    sp.wait_ge(h0_kept, j)
                    sp.wait_ge(xa_done, j)
                src = txt[2 * j:2 * j + 2] if isinstance(j, int) else txt[bass.ds(2 * j, 2)]
                sp.dma_start(h0[LASTP:T, 1:NT:2, :], src.rearrange("b s d -> s b d")).then_inc(text_in, 16)

            def store_h1(part, j):
                part.wait_evacuated(sp, "w2", 1)
                dst = out_rows[bass.ds(j * W, W)] if not isinstance(j, int) else out_rows[j * W:(j + 1) * W]
                sp.dma_start(dst.rearrange("(t p) d -> p t d", p=T), hy[:, :, :]).then_inc(h1_stored, 16)

            def store_xn2(j):
                sp.wait_ge(xn2_done, j + 2)
                dst = xd[bass.ds(j * W, W), 0:D] if not isinstance(j, int) else xd[j * W:(j + 1) * W, 0:D]
                sp.dma_start(dst.rearrange("(t p) d -> p t d", p=T), xn2[:, :, :]).then_inc(xn2_stored, 16)

            load_images(0)
            sp.dma_start(w2t[:, :, :], tok_W2.rearrange("(c p) n -> p c n", p=128)).then_inc(tok_in, 16)
            sp.dma_start(b2t[:, :], tok_b2.partition_broadcast(T)).then_inc(tok_in, 16)
            load_text(0)
            for k, src in enumerate((Wq, Wk, Wv)):
                sp.dma_start(wqkv[:, :, k * D:(k + 1) * D], src.rearrange("(c p) n -> p c n", p=128)).then_inc(qkv_in, 16)
            sp.wait_ge(zrow_ready, 1)
            pitch = 2 * S - 1 + T
            sp.dma_start(bass.AP(zrow_d, 0, [[T * pitch, H], [pitch + 1, T], [1, 2 * S - 1]]),
                         zrow[:, :].unsqueeze(1).to_broadcast([H, T, 2 * S - 1])).then_inc(rows_out, 16)
            sp.dma_start(mrow_d[:, :], mrow[:, :]).then_inc(rows_out, 16)
            sp.wait_ge(rows_out, 32)
            toep = lambda h, n: bass.AP(zrow_d, h * T * pitch + S - 1, [[pitch, T], [T * pitch, H // 2], [1, n]])
            mx = lambda h, o, n: bass.AP(mrow_d, h * S + o, [[0, T], [S, H // 2], [1, n]])
            for k in range(2):
                h = k * (H // 2)
                m = mtmp[k][:, 0:H // 2 * QW].rearrange("p (h q) -> p h q", q=QW)
                sp.dma_start(bias_t[:, h:h + H // 2, 0:S], toep(h, S)).then_inc(toeplitz_in, 16)
                sp.dma_start(bias_t[:, h:h + H // 2, S:QW], toep(h, T)).then_inc(toeplitz_in, 16)
                sp.dma_start(m[:, :, 0:S], mx(h, 0, S)).then_inc(toeplitz_in, 16)
                sp.dma_start(m[:, :, S:QW], mx(h, T, T)).then_inc(toeplitz_in, 16)
            for dst, src in ((wo, Wo), (w1m, W1), (w2m, W2), (wr, Wr)):
                sp.dma_start(dst[:, :, :], src.rearrange("(c p) n -> p c n", p=128)).then_inc(weights_in, 16)
            first = Part("first", 0)
            first.wait_filled(sp, "tok1", 1)
            load_images(1)
            load_text(1)
            first.wait_filled(sp, "next", 1)
            load_images(2)
            with sp.Fori(1, PAIRS - 2) as i:
                part = Part("body", i)
                load_text(i + 1)
                store_h1(part, i - 1)
                store_xn2(i - 1)
                part.wait_filled(sp, "next", 1)
                load_images(i + 2)
            load_text(PAIRS - 1)
            for i, kind in ((PAIRS - 2, "body"), (PAIRS - 1, "final"), (PAIRS, "last")):
                store_h1(Part(kind, i), i - 1)
                store_xn2(i - 1)
            sp.wait_ge(phase2_init, 1)
            def load_expert(e):
                src = min(e, NE - 1)
                sp.dma_start(we1[e % 2][:, :, :], fW1[src].rearrange("(c p) n -> p c n", p=128)).then_inc(expert_in[e % 2], 16)
                sp.dma_start(we2[e % 2][:, :, :], fW2[src].rearrange("(c p) n -> p c n", p=128)).then_inc(expert_in[e % 2], 16)

            for e in range(2):
                load_expert(e)
            sp.dma_start(fb2b[:, :, :], fb2.partition_broadcast(T)).then_inc(fb2_in, 16)
            sp.wait_ge(score_ready, 1)
            sp.dma_start(xd[:, D:XW].rearrange("(t p) e -> p t e", p=T), score[:, :, :]).then_inc(score_stored, 16)
            for e in range(2, NE):
                sp.wait_ge(squares_done, 2 * (e - 1))
                load_expert(e)
            for e in range(2):
                sp.wait_ge(squares_done, 2 * (NE - 1 + e))
                load_expert(e)
            for e in range(2, NE + 1):
                sp.wait_ge(split_done, PIECES * (e - 1))
                load_expert(e)
            sp.wait_ge(h1_stored, 16 * (PAIRS + 1))
            sp.wait_ge(xn2_stored, 16 * (PAIRS + 1))
            sp.wait_ge(score_stored, 16)

        @block.tensor
        def _(eng):
            pe.wait_ge(tok_in, 16 * (2 * C + 2))
            pe.wait_ge(pool_consts, 6)
            part = Part("first", 0)
            for m in range(KC):
                pe_tok1(part, ("tok1", m), range(2 * HALF), 0)
            for b in range(2):
                pe_tok2(part, 0, b)
            pe.wait_ge(setup_done, 1)
            pe_xsT(part, 0)
            pe_qkv(part, 0)
            pe_attention(part, 0)

            pe.wait_ge(weights_in, 16 * 4)
            pe.wait_ge(setup_done, 2)

            def iteration(part, i):
                pe_tok2(part, i, 0)
                pe_yT(part, i - 1)
                pe_tok2(part, i, 1)
                pe_wo(part, i - 1)
                pe_y2T(part, i - 1)
                for m in range(EARLY):
                    pe_w1(part, m)
                pe_xsT(part, i)
                pe_w1(part, EARLY)
                pe_qkv(part, i)
                for m in range(EARLY + 1, MC):
                    pe_w1(part, m)
                pe_attention(part, i)

            with eng.Fori(1, PAIRS - 1) as i:
                iteration(Part("body", i), i)
            iteration(Part("final", PAIRS - 1), PAIRS - 1)
            part = Part("last", PAIRS)
            pe_yT(part, PAIRS - 1)
            pe_wo(part, PAIRS - 1)
            pe_y2T(part, PAIRS - 1)
            for m in range(MC):
                pe_w1(part, m)
            pe_w2(part, range(16))
            for c in range(KC):
                pe_x2T(part, PAIRS - 1, c)
            for c in range(KC):
                pe_rtT(part, c)
            pe_rt(part)

            pe.wait_ge(score_ready, 2)
            for g in range(GT):
                last = pe.transpose(SC[1][:, g // 4, (g % 4) * T:(g % 4 + 1) * T], by_group[:, g, :],
                                    ident[0:T, 0:T])
            last.then_inc(scoreT_filled, 1)
            with eng.Fori(0, 30) as k:
                pe.wait_ge(counts_ready, k + 1)
                pe.matmul(Y[1][:, 0:1], group_ones[:, :], cnt[:, 0:1], start=True, stop=True).then_inc(counts_summed, 1)
            pe.wait_ge(squares_done, 2 * NE)
            pe.matmul(SC[0][:, 1, 0:3 * NE], all_ones[:, :], sumsq[:, :, :].rearrange("p k e -> p (k e)"),
                      start=True, stop=True).then_inc(norms_summed, 1)
            pe.wait_ge(counts_ready, 31)
            pe.matmul(Y[1][:, 1:2], group_ones[:, :], cnt[:, 1:2], start=True, stop=True)
            pe.matmul(Y[1][:, 2:3], earlier_ones[:, :], cnt[:, 2:3], start=True, stop=True).then_inc(offs_summed, 1)
            pe.wait_ge(offs_ready, 1)
            pe.matmul(Y[1][:, 3:4], earlier_ones[:, :], cnt[:, 3:4], start=True, stop=True).then_inc(offs_summed, 1)
            pe.wait_ge(pos_ready, 1)
            for g in range(GT):
                last = pe.transpose(SC[1][0:T, g // 4, (g % 4) * 128:(g % 4 + 1) * 128], rank[:, g * T:(g + 1) * T],
                                    ident[:, :])
            last.then_inc(posT_filled, 1)

            def clear_list():
                pe.matmul(Y[0][0:T, 0:2 * SLOTC], zero_w[:, :], iota_b[:, 0:2 * SLOTC],
                          start=True, stop=False, skip_group_check=True)

            def list_part(k, n):
                pe.wait_ge(onehot_ready, n + 1)
                for t in range(LT):
                    last = pe.matmul(Y[0][0:T, 0:2 * SLOTC], oh_b[k][:, t, :],
                                     oh_a[k][:, t, :, :].rearrange("p a b -> p (a b)"),
                                     start=False, stop=False, skip_group_check=True)
                last.then_inc(onehot_used, 1)

            def row_transposes(k, banks):
                for c in range(KC):
                    for t in range(NT):
                        last = pe.transpose(G2[banks[c]][:, t * T:(t + 1) * T], xg[k][:, t, c * 128:(c + 1) * 128],
                                            ident[0:T, 0:T])
                    last.then_inc(filled2[banks[c]], 1)

            def w1_block(eb, n, m):
                key = ("w1", m)
                wait_free2(pe, n, key)
                for c in range(KC):
                    for i, (wp, xp) in enumerate(PARTS):
                        last = pe.matmul(G2[bank2(key)][:, 0:W], ws1[eb][:, wp, c, m * 128:(m + 1) * 128], xgT[:, xp, c, :],
                                         start=c == 0 and i == 0, stop=c == KC - 1 and i == len(PARTS) - 1)
                last.then_inc(filled2[bank2(key)], 1)

            def group(eb, half_n, k):
                n = half_n * 2 + k
                for m in range(MC):
                    w1_block(eb, n, m)
                    if m == MC - 3:
                        list_part(k, n + GROUPS)
                for b in range(2):
                    if b == 1:
                        pe.wait_ge(gathered[1 - k], (half_n + (1 + k)) * (16 * NT))
                        for c in range(KC):
                            wait_free2(pe, n, ("xT", c))
                        row_transposes(1 - k, [bank2(("xT", c)) for c in range(KC)])
                    key = ("w2", b)
                    wait_free2(pe, n, key)
                    for half in range(2):
                        t = 2 * b + half
                        for m in range(MC):
                            if t == 0:
                                pe.wait_ge(h_split, (n + 1) * MC + (m + 1))
                            for i, (hp, wp) in enumerate(PARTS):
                                last = pe.matmul(G2[bank2(key)][0:T, half * D:(half + 1) * D],
                                                 hTs[:, hp, m, t * T:(t + 1) * T], ws2[eb][:, wp, m, :],
                                                 start=m == 0 and i == 0, stop=m == MC - 1 and i == len(PARTS) - 1)
                    last.then_inc(filled2[bank2(key)], 1)
                for c in range(KC):
                    wait_evacuated2(pe, n, ("xT", c))

            pe.wait_ge(onehot_ready, 1)
            clear_list()
            for p in range(GROUPS):
                list_part(p % 2, p)
            pe.wait_ge(gathered[0], 16 * NT)
            row_transposes(0, [0, 1])
            for c in range(KC):
                pe.wait_ge(evacuated2[c], 2)
            with eng.Fori(0, NE // 2) as E:
                for eb in range(2):
                    e = E * 2 + eb
                    pe.wait_ge(split_done, (e + 1) * PIECES)
                    pe.wait_ge(list_done, e + 1)
                    clear_list()
                    with eng.Fori(0, GROUPS // 2) as q:
                        for k in range(2):
                            group(eb, e * (GROUPS // 2) + q, k)

        act = nc.scalar

        def act_evacuate(part, key, dst, cols=W):
            part.wait_filled(act, *key)
            act.copy(dst, part.g(*key)[0:dst.shape[0], 0:cols]).then_inc(evacuated[part.bank(*key)], 1)

        @block.scalar
        def _(eng):
            with nc.allow_non_contiguous_dma(reason="small vectors of weights"):
                act.dma_start(relb[:, :], rel_bias.rearrange("k h -> h k")).then_inc(consts_in, 16)
                act.dma_start(sc_col[:, :], scale.rearrange("(h o) -> h o", o=1)).then_inc(consts_in, 16)
                act.dma_start(sc_bc[:, :], scale.partition_broadcast(T)).then_inc(consts_in, 16)
                act.dma_start(lnw[:, 0, :], ln1_w.rearrange("(c p) -> p c", p=128)).then_inc(consts_in, 16)
                act.dma_start(lnw[:, 1, :], ln2_w.rearrange("(c p) -> p c", p=128)).then_inc(consts_in, 16)
                act.dma_start(b1t[:, :], tok_b1.rearrange("(c p) -> p c", p=128)).then_inc(consts_in, 16)
                for e in range(NE):
                    act.dma_start(fb1c[:, e, :], fb1[e].rearrange("(m p) -> p m", p=128)).then_inc(consts_in, 16)

            def qkT_evacuate(eng, part, c):
                part.wait_filled(eng, "qkT", c)
                eng.copy(qkT[:, c, :, :].rearrange("p s w -> p (s w)"),
                         part.g("qkT", c)[:, 0:W].bitcast(F16)).then_inc(evacuated[part.bank("qkT", c)], 1)

            def silu(part, key):
                part.wait_filled(act, *key)
                act.activation(hid[:, key[1], :], part.g(*key)[:, 0:2 * NP_], ACT.Silu,
                               bias=b1t[:, key[1]:key[1] + 1]).then_inc(evacuated[part.bank(*key)], 1)

            def xs_transposed(part):
                for c in range(KC):
                    act_evacuate(part, ("xsT", c), xsT[:, c, :])

            def queries_keys(part, j):
                if part.kind != "first":
                    act.wait_ge(qk_normed, j)
                for t in range(NT):
                    act_evacuate(part, ("qk", t), qkraw[:, t, :], 2 * D)
                for b in range(2):
                    part.wait_filled(act, "v", b)
                    src = part.g("v", b)[0:T, :].rearrange("p (t h d) -> p t h d", t=2, d=HD)
                    act.copy(v1[:, 2 * b:2 * b + 2, :, 0:HD], src).then_inc(evacuated[part.bank("v", b)], 1)

            def high_parts(j, tiles):
                for t in tiles:
                    act.wait_ge(qk_scaled, NT * j + (t + 1))
                    src = qkraw[:, t, :].rearrange("p (h d) -> p h d", d=HD)
                    act.copy(qkp[:, t, :, 0:HD], src).then_inc(qk_high, 1)

            def exps(part, j):
                first = part.kind == "first"
                qkT_evacuate(act, part, 0)
                for g in range(NG):
                    act.wait_ge(scores_done, NG * j + (g + 1))
                    if not (first and g < 2):
                        act.wait_ge(probs_done, NG * j + (g - 1))
                    act.activation(p0[g % 2][:, :, :], SC[g % 2][0:T, :, 0:QW], ACT.Exp).then_inc(exp_done, 1)
                    if g % 2 == 0 and g + 2 < H // 2:
                        qkT_evacuate(act, part, g + 2)
                    if not first and 11 <= g < 11 + KC:
                        x2_transposed(part, g - 11)
                if part.kind != "final":
                    for m in range(KC):
                        silu(part, ("next", m))

            def squares(part):
                for b in range(2):
                    part.wait_evacuated(act, "wo", b)
                    for half in range(2):
                        t = 2 * b + half
                        last = act.activation(junk[:, t, :], y2[:, t, :], ACT.Square, scale=D ** -0.5,
                                              accum_out=ss2[:, t:t + 1])
                last.then_inc(y2_sums, 1)

            def y2_transposed(part):
                for c in range(KC):
                    act_evacuate(part, ("y2T", c), yT[:, c, :])

            def relu(part, ms):
                for m in ms:
                    part.wait_filled(act, "w1", m)
                    act.activation(hT[:, m, :], part.g("w1", m)[:, 0:W], ACT.Relu).then_inc(evacuated[part.bank("w1", m)], 1)

            def yT_evacuate(part):
                for c in range(KC):
                    act_evacuate(part, ("yT", c), yT[:, c, :])

            def x2_transposed(part, c):
                act_evacuate(part, ("x2T", c), xsT[:, c, :])

            act.wait_ge(consts_in, 16 * (6 + NE))
            part = Part("first", 0)
            for m in range(KC):
                silu(part, ("tok1", m))
            xs_transposed(part)
            queries_keys(part, 0)
            high_parts(0, range(NT))
            act.wait_ge(table_diff, 1)
            act.activation(bias_t[:, :, :], bias_t[:, :, :], ACT.Exp).then_inc(table_exp, 1)
            exps(part, 0)

            def iteration(part, i):
                yT_evacuate(part)
                y2_transposed(part)
                squares(part)
                relu(part, range(EARLY))
                xs_transposed(part)
                relu(part, [EARLY])
                queries_keys(part, i)
                relu(part, range(EARLY + 1, MC - 2))
                high_parts(i, range(3))
                relu(part, [MC - 2])
                high_parts(i, range(3, NT))
                relu(part, [MC - 1])
                exps(part, i)

            with eng.Fori(1, PAIRS - 1) as i:
                iteration(Part("body", i), i)
            iteration(Part("final", PAIRS - 1), PAIRS - 1)
            part = Part("last", PAIRS)
            yT_evacuate(part)
            y2_transposed(part)
            squares(part)
            relu(part, range(4))
            for c in range(KC):
                x2_transposed(part, c)

            act.wait_ge(shifted, 1)
            act.activation(score[:, :, :], score[:, :, :], ACT.Exp).then_inc(exps_done, 1)
            for e in range(NE):
                act.wait_ge(expert_in[e % 2], 32 * (e // 2 + 1))
                for k, w in enumerate((we1, we2)):
                    if e or k:
                        act.wait_ge(squares_done, 2 * e + k)
                    src = w[e % 2][:, :, :].rearrange("p a b -> p (a b)")
                    act.activation(hTe[:, :, :].rearrange("p m w -> p (m w)")[:, 0:src.shape[1]], src, ACT.Square,
                                   accum_out=sumsq[:, k, e:e + 1]).then_inc(squares_done, 1)

            def split_piece(eb, e, p):
                act.activation(split_pieces(eb, 0, p), piece((we1[eb][:, :, :], we2[eb][:, :, :]), p), ACT.Identity,
                               scale=scale_at(scales, p // 4, e)).then_inc(split_high, 1)

            act.wait_ge(scales_ready, 1)
            act.wait_ge(expert_in[0], LOADS + 32)
            for p in range(PIECES):
                split_piece(0, 0, p)
            for c in range(KC):
                act.wait_ge(filled2[c], 1)
                act.copy(xgT[:, 0, c, :], G2[c][:, 0:W]).then_inc(x_high, 1)

            def group(e, n, split):
                def high(m):
                    key = ("w1", m)
                    copied = act.snap(act.to_reg(count2(n, key) + 1))
                    wait_apart(act)
                    act.wait_ge(evacuated2[bank2(key)], copied)
                    act.activation(hTs[:, 0, m, :], hTe[:, m, :], ACT.Identity,
                                   scale=scale_at(scales, 2, e)).then_inc(h_high, 1)

                act.wait_ge(h_split, (n + 1) * MC)
                for m in range(MC):
                    key = ("w1", m)
                    act.wait_ge(filled2[bank2(key)], count2(n, key))
                    bias = fb1c[:, :, :].rearrange("p e m -> p (e m)")[:, bass.ds(e * MC + m, 1)]
                    act.activation(hTe[:, m, :], G2[bank2(key)][:, 0:W], ACT.Gelu, bias=bias,
                                   scale=scale_at(unscales, 0, e)).then_inc(evacuated2[bank2(key)], 1)
                    if m:
                        high(m - 1)
                high(MC - 1)
                if split is not None:
                    for p in range(PIECES):
                        split_piece(split, e + 1, p)
                for c in range(KC):
                    key = ("xT", c)
                    act.wait_ge(filled2[bank2(key)], count2(n, key))
                    act.activation(xgT[:, 0, c, :], G2[bank2(key)][:, 0:W], ACT.Identity).then_inc(x_high, 1)

            with eng.Fori(0, NE // 2) as E:
                for eb in range(2):
                    e = E * 2 + eb
                    with eng.Fori(0, GROUPS - 1) as g:
                        group(e, e * GROUPS + g, None)
                    act.wait_ge(expert_in[1 - eb], (E + (1 + eb)) * 32 + LOADS)
                    group(e, e * GROUPS + (GROUPS - 1), 1 - eb)

        dve = nc.vector

        @block.vector
        def _(eng):
            chain = Chain(dve, dve_step, lambda: wait_apart(dve))
            step = chain.step

            dve.wait_ge(pool_consts, 6)
            dve.tensor_scalar(diff_low[:, :], diff[:, :], NE - 1, None, ALU.bitwise_and)
            step(dve.tensor_scalar(difff[:, :], diff[:, :], 128.0, None, ALU.is_gt))
            step(dve.tensor_scalar(group_ones[:, :], diff_low[:, :], 0.0, None, ALU.is_equal))
            dve.tensor_tensor(earlier_ones[:, :], difff[:, :], group_ones[:, :], ALU.mult)
            dve.tensor_copy(iota_b[:, :], iota_i[:, :])
            dve.tensor_copy(tok_p[:, :], tok_pi[:, :])
            dve.memset(zrow[:, 0:S], -3.0e38)
            dve.memset(mrow[:, 0:1], 0.0)
            dve.wait_ge(consts_in, 16 * (6 + NE))
            step(dve.tensor_scalar(relb[:, :], relb[:, :], sc_col[:, 0:1], None, ALU.mult))
            for d, n, k in relative_bucket_runs(S, NBUCK, 128):
                last = dve.tensor_copy(zrow[:, S - 1 + d:S - 1 + d + n], relb[:, k:k + 1].to_broadcast([H, n]))
            step(last)
            dve.tensor_tensor_scan(mrow[:, 1:S], zrow[:, S:2 * S - 1], zrow[:, S:2 * S - 1], -3.0e38,
                                   ALU.max, ALU.max).then_inc(zrow_ready, 1)
            step(dve.tensor_scalar(shift[:, 0, :], sc_bc[:, :], -1.0, None, ALU.mult))
            step(dve.tensor_tensor(shift[:, 0, :], shift[:, 0, :], sc_bc[:, :], ALU.max))
            step(dve.tensor_scalar(shift[:, 1, :], shift[:, 0, :], -1.0, SAFE, ALU.mult, ALU.add))
            step(dve.tensor_scalar(shift[:, 1, :], shift[:, 1, :], 0.0, None, ALU.min))
            dve.memset(v1[:, :, :, :], 1.0)
            step(dve.memset(qkp[:, :, :, :], 0.0))
            for t in range(NT):
                dve.tensor_copy(qkp[:, t, 0:H, 3 * HD], shift[:, 1, :])
                last = dve.tensor_copy(sc_q[:, t, :], sc_bc[:, :])
            step(last)
            dve.memset(qkp[:, :, H:2 * H, 3 * HD:3 * HD + 1], 1.0)
            dve.memset(qkp[0:1, 0:NT:2, 0:H, 3 * HD:3 * HD + 1], 0.0)
            dve.tensor_copy(ident_h[:, :], ident[0:T, 0:T])
            dve.memset(sc_q[0:1, 0:NT:2, :], 0.0)
            dve.wait_ge(qkv_in, 16 * 3)
            for c in range(KC):
                last = dve.tensor_scalar(wqkv[:, c, :], wqkv[:, c, :], lnw[:, 0, c:c + 1], None, ALU.mult)
            last.then_inc(setup_done, 1)
            dve.wait_ge(tok_in, 16 * (2 * C + 2))

            def bias_table():
                dve.wait_ge(toeplitz_in, 16 * 8)
                for k in range(2):
                    hs = slice(k * (H // 2), (k + 1) * (H // 2))
                    m = mtmp[k][:, 0:H // 2 * QW].rearrange("p (h q) -> p h q", q=QW)
                    last = dve.tensor_tensor(bias_t[:, hs, :], bias_t[:, hs, :], m, ALU.subtract)
                last.then_inc(table_diff, 1)
                dve.wait_ge(weights_in, 16 * 4)
                for c in range(KC):
                    last = dve.tensor_scalar(w1m[:, c, :], w1m[:, c, :], lnw[:, 1, c:c + 1], None, ALU.mult)
                last.then_inc(setup_done, 1)
                dve.wait_ge(table_exp, 1)
                step(dve.memset(bias_t[:, :, 0:1], 1.0))

            def evacuate(part, key, dst, cols=W):
                part.wait_filled(dve, *key)
                dve.tensor_copy(dst, part.g(*key)[0:dst.shape[0], 0:cols]).then_inc(evacuated[part.bank(*key)], 1)

            def stats(src, mv, done):
                for t in range(NT):
                    last = dve.bn_stats(st[:, t, :], src[:, t, :])
                step(last, apart=True)
                for t in range(NT):
                    last = dve.bn_aggr(mv[:, t, :], st[:, t, :])
                last.then_inc(done, 1)

            def front_a(part, j, first):
                if not first:
                    dve.wait_ge(h0_kept, j)
                for b in range(2):
                    part.wait_filled(dve, "tok2", b)
                    dve.tensor_tensor(h0[:, 2 * b, :], part.g("tok2", b)[0:T, 0:D], b2t[:, :], ALU.add)
                    dve.tensor_tensor(h0[0:LASTP, 2 * b + 1, :], part.g("tok2", b)[0:LASTP, D:2 * D],
                                      b2t[0:LASTP, :], ALU.add).then_inc(evacuated[part.bank("tok2", b)], 1)
                for b in range(2):
                    part.wait_evacuated(dve, "tok2", b)
                dve.wait_ge(text_in, 16 * (j + 1))
                stats(h0, mv1, ln1_stats)

            def front_b(part, j):
                dve.wait_ge(ln1_scales, j + 1)
                for t in range(NT):
                    last = dve.tensor_scalar(xs[:, t, :], h0[:, t, :], mv1[:, t, 0:1], lt[:, 5, t:t + 1],
                                             ALU.subtract, ALU.mult)
                last.then_inc(xs_done, 1)
                if part.kind != "first":
                    for b in range(2):
                        part.wait_evacuated(dve, "wo", b)
                for t in range(NT):
                    last = dve.tensor_scalar(xa[:, t, :], h0[:, t, :], mv1[:, t, 0:1], lt[:, 1, t:t + 1],
                                             ALU.subtract, ALU.mult)
                last.then_inc(xa_done, 1)

            def qk_norm(part, j):
                def sums(t):
                    part.wait_evacuated(dve, "qk", t)
                    step(dve.tensor_tensor(sqb[:, :], qkraw[:, t, :], qkraw[:, t, :], ALU.mult))
                    return dve.reduce_sum(ss[:, t, :], sqb[:, :].rearrange("p (h d) -> p h d", d=HD), AX.X)

                for t in range(NT):
                    step(sums(t))
                x_, r_ = ss[:, :, :].rearrange("p t h -> p (t h)"), rn[:, :, :].rearrange("p t h -> p (t h)")
                a_ = nwt[:, :]
                step(dve.tensor_scalar(x_, x_, RMS_EPS, None, ALU.add))
                step(dve.tensor_scalar(a_.bitcast(I32), x_.bitcast(I32), 1, None, ALU.arith_shift_right))
                step(dve.tensor_scalar(r_.bitcast(I32), a_.bitcast(I32), -1.0, float(0x5f3759df), ALU.mult, ALU.add))
                for _ in range(3):
                    step(dve.tensor_tensor(a_, r_, r_, ALU.mult))
                    step(dve.scalar_tensor_tensor(a_, a_, -0.5, x_, ALU.mult, ALU.mult))
                    step(dve.scalar_tensor_tensor(r_, a_, 1.5, r_, ALU.add, ALU.mult))
                step(dve.tensor_tensor(rn[:, :, 0:H], rn[:, :, 0:H], sc_q[:, :, :], ALU.mult))
                for t in range(NT):
                    q = qkraw[:, t, :].rearrange("p (h d) -> p h d", d=HD)
                    dve.tensor_tensor(q, q, rn[:, t, :].unsqueeze(2).to_broadcast([T, 2 * H, HD]),
                                      ALU.mult).then_inc(qk_scaled, 1)
                for t in range(NT):
                    dve.wait_ge(qk_high, NT * j + (t + 1))
                    for s, at in ((0, HD), (H, 2 * HD)):
                        src = qkraw[:, t, s * HD:(s + H) * HD].rearrange("p (h d) -> p h d", d=HD)
                        dve.tensor_tensor(qkp[:, t, s:s + H, at:at + HD], src, qkp[:, t, s:s + H, 0:HD], ALU.subtract)
                    last = dve.tensor_copy(qkp[:, t, H:2 * H, HD:2 * HD], qkp[:, t, H:2 * H, 0:HD])
                last.then_inc(qk_normed, 1)

            def qkT_evacuate(part, c):
                part.wait_filled(dve, "qkT", c)
                dve.tensor_copy(qkT[:, c, :, :].rearrange("p s w -> p (s w)"),
                                part.g("qkT", c)[:, 0:W].bitcast(F16)).then_inc(evacuated[part.bank("qkT", c)], 1)

            def normalise_outputs(j, b):
                dve.wait_ge(pv_done, NG * j + (NG // 2) * (b + 1))
                for half in range(2):
                    y = Y[half][0:T, 0:H * HV].rearrange("p (h d) -> p h d", d=HV)
                    last = dve.reciprocal(yrec[:, half, :], y[:, :, HD])
                step(last)
                for half in range(2):
                    y = Y[half][0:T, 0:H * HV].rearrange("p (h d) -> p h d", d=HV)
                    dst = yn[:, 2 * b + half, :].rearrange("p (h d) -> p h d", d=HD)
                    last = dve.tensor_tensor(dst, y[:, :, 0:HD],
                                             yrec[:, half, :].unsqueeze(2).to_broadcast([T, H, HD]), ALU.mult)
                last.then_inc(y_normed, 1)

            def relu(part, ms):
                for m in ms:
                    part.wait_filled(dve, "w1", m)
                    dve.tensor_scalar(hT[:, m, :], part.g("w1", m)[:, 0:W], 0.0, None,
                                      ALU.max).then_inc(evacuated[part.bank("w1", m)], 1)

            def mlp_out(part, j, b):
                dve.wait_ge(r2_done, j + 1)
                dve.wait_ge(hy_done, 2 * (j + 1))
                part.wait_filled(dve, "w2", b)
                for half in range(2):
                    t = 2 * b + half
                    last = dve.scalar_tensor_tensor(hy[:, t, :], part.g("w2", b)[0:T, half * D:(half + 1) * D],
                                                    r2[:, t:t + 1], hy[:, t, :], ALU.mult, ALU.add)
                last.then_inc(evacuated[part.bank("w2", b)], 1)
                if b == 1:
                    part.wait_evacuated(dve, "w2", b)
                    stats(hy, mv2, ln2_stats)

            def second_norm(part, j):
                dve.wait_ge(ln2_scales, j + 1)
                dve.wait_ge(xn2_stored, 16 * (j + 1))
                for t in range(NT):
                    last = dve.tensor_scalar(xn2[:, t, :], hy[:, t, :], mv2[:, t, 0:1], rstd2[:, t:t + 1],
                                             ALU.subtract, ALU.mult)
                last.then_inc(xn2_done, 1)

            def router_transposed(part):
                evacuate(part, ("rtT", 0), logitsT)

            def router_out(part, j):
                part.wait_filled(dve, "rt", 0)
                at = NT * j
                dst = logits[:, at:at + NT, :] if isinstance(j, int) else logits[:, bass.ds(at, NT), :]
                dve.tensor_copy(dst, part.g("rt", 0)[0:T, 0:NT * NE].rearrange(
                    "p (t e) -> p t e", e=NE)).then_inc(evacuated[part.bank("rt", 0)], 1)

            def tail(part, j):
                for b in range(2):
                    part.wait_filled(dve, "wo", b)
                    dve.tensor_tensor(y2[:, 2 * b:2 * b + 2, :], part.g("wo", b)[0:T, :].rearrange("p (t d) -> p t d", d=D),
                                      xa[:, 2 * b:2 * b + 2, :], ALU.add).then_inc(evacuated[part.bank("wo", b)], 1)

            def masked_probs(part, j):
                first = part.kind == "first"
                qkT_evacuate(part, 1)
                for g in range(NG):
                    pair = g % (H // 2)
                    dve.wait_ge(exp_done, NG * j + (g + 1))
                    if not (first and g < 2):
                        dve.wait_ge(pv_done, NG * j + (g - 1))
                    dve.tensor_tensor(pm[g % 2][:, :, :], p0[g % 2][:, :, :], bias_t[:, 2 * pair:2 * pair + 2, :],
                                      ALU.mult).then_inc(probs_done, 1)
                    if g % 2 == 0 and g + 3 < H // 2:
                        qkT_evacuate(part, g + 3)
                    if g == NG // 2:
                        normalise_outputs(j, 0)
                    if not first and g == 1:
                        mlp_out(part, j - 1, 0)
                    if not first and g == 6:
                        mlp_out(part, j - 1, 1)
                    if not first and g == 8:
                        second_norm(part, j - 1)
                    if not first and g == 12:
                        router_transposed(part)
                    if not first and g == 13:
                        router_out(part, j - 1)
                normalise_outputs(j, 1)

            part = Part("first", 0)
            front_a(part, 0, True)
            front_b(part, 0)
            qk_norm(part, 0)
            bias_table()
            masked_probs(part, 0)

            def iteration(part, i):
                front_a(part, i, False)
                tail(part, i - 1)
                front_b(part, i)
                qk_norm(part, i)
                masked_probs(part, i)

            with eng.Fori(1, PAIRS - 1) as i:
                chain.enter(i - 1, 25)
                iteration(Part("body", i), i)
            chain.leave(PAIRS - 2)
            iteration(Part("final", PAIRS - 1), PAIRS - 1)
            j = PAIRS - 1
            part = Part("last", PAIRS)
            tail(part, j)
            relu(part, range(4, MC))
            mlp_out(part, j, 0)
            mlp_out(part, j, 1)
            second_norm(part, j)
            router_transposed(part)
            router_out(part, j)

            part.wait_evacuated(dve, "rt", 0)
            dve.wait_ge(h1_stored, 16 * (PAIRS + 1))
            dve.wait_ge(xn2_stored, 16 * (PAIRS + 1))
            dve.reduce_max(smax[:, :], logits[:, :, :], AX.X).then_inc(phase2_init, 1)
            dve.wait_ge(phase2_init, 1)
            dve.tensor_tensor(score[:, :, :], logits[:, :, :], smax[:, :].unsqueeze(2).to_broadcast([T, NTILES, NE]),
                              ALU.subtract).then_inc(shifted, 1)
            dve.memset(bitv[:, :], float(1 << 29))
            step(dve.tensor_tensor(b1sq[:, :, :], fb1c[:, :, :], fb1c[:, :, :], ALU.mult))
            dve.reduce_sum(sumsq[:, 2, :], b1sq[:, :, :], AX.X)
            dve.memset(all_ones[:, :], 1.0)
            dve.memset(thr[:, :], 0)
            dve.memset(slot_a[:, NE, :], 0.0)
            dve.memset(slot_b[:, NE, :], -1.0)
            step(dve.memset(zero_w[:, :], 0.0))
            step(dve.tensor_copy(biti[:, :], bitv[:, :]))
            dve.wait_ge(exps_done, 1)
            step(dve.reduce_sum(smax[:, :], score[:, :, :], AX.X))
            step(dve.reciprocal(smax[:, :], smax[:, :]))
            dve.tensor_tensor(score[:, :, :], score[:, :, :], smax[:, :].unsqueeze(2).to_broadcast([T, NTILES, NE]),
                              ALU.mult).then_inc(score_ready, 1)
            dve.wait_ge(score_ready, 1)
            dve.tensor_copy(by_group[:, :, :].rearrange("p g (r e) -> p r g e", e=NE),
                            score[:, :, :].rearrange("p (r g) e -> p r g e", g=GT)).then_inc(score_ready, 1)

            dve.wait_ge(scoreT_filled, 1)
            for k in range(2):
                last = dve.tensor_copy(scoreT[:, k * 4 * T:(k + 1) * 4 * T], SC[1][:, k, 0:4 * T])
            step(last)
            with eng.Fori(0, 30) as k:
                chain.enter(k, 4)
                step(dve.tensor_tensor(cand[:, :], thr[:, :], biti[:, :], ALU.bitwise_or))
                dve.tensor_scalar(hit[:, :], scoreT[:, :], cand[:, :].bitcast(F32), None, ALU.is_ge, ALU.add,
                                  accum_out=cnt[:, 0:1]).then_inc(counts_ready, 1)
                step(dve.tensor_scalar(biti[:, :], bitv[:, :], 0.5, None, ALU.mult))
                dve.wait_ge(counts_summed, k + 1)
                step(dve.tensor_scalar(kept[:, :], Y[1][:, 0:1], float(CAP), bitv[:, 0:1], ALU.is_ge, ALU.mult))
                dve.tensor_scalar(bitv[:, :], bitv[:, :], 0.5, None, ALU.mult)
                step(dve.tensor_tensor(thr[:, :], thr[:, :], kept[:, :], ALU.bitwise_or))
            chain.leave(30)
            tf = thr[:, :].bitcast(F32)
            dve.tensor_scalar(above[:, :], scoreT[:, :], tf, None, ALU.is_gt, ALU.add, accum_out=cnt[:, 1:2])
            dve.tensor_scalar(equal[:, :], scoreT[:, :], tf, None, ALU.is_equal, ALU.add,
                              accum_out=cnt[:, 2:3]).then_inc(counts_ready, 1)
            dve.wait_ge(counts_ready, 31)
            step(dve.tensor_tensor_scan(rank[:, :], equal[:, :], equal[:, :], 0.0, ALU.add, ALU.max))
            dve.wait_ge(offs_summed, 1)
            step(dve.tensor_scalar(need[:, 0:1], Y[1][:, 1:2], -1.0, float(CAP), ALU.mult, ALU.add))
            step(dve.tensor_tensor(need[:, 1:2], need[:, 0:1], Y[1][:, 2:3], ALU.subtract))
            step(dve.scalar_tensor_tensor(hit[:, :], rank[:, :], need[:, 1:2], equal[:, :], ALU.is_le, ALU.mult))
            dve.scalar_tensor_tensor(above[:, :], above[:, :], 0.0, hit[:, :], ALU.add, ALU.add,
                                     accum_out=cnt[:, 3:4]).then_inc(offs_ready, 1)
            dve.wait_ge(offs_ready, 1)
            step(dve.tensor_tensor_scan(rank[:, :], above[:, :], above[:, :], 0.0, ALU.add, ALU.max))
            dve.wait_ge(offs_summed, 2)
            step(dve.scalar_tensor_tensor(rank[:, :], rank[:, :], Y[1][:, 3:4], above[:, :], ALU.add, ALU.mult))
            dve.tensor_scalar(rank[:, :], rank[:, :], -1.0, None, ALU.add).then_inc(pos_ready, 1)
            dve.wait_ge(posT_filled, 1)
            for k in range(2):
                src = SC[1][0:T, k, :].rearrange("p (g r e) -> p g r e", g=GT // 2, e=NE)
                dst = posi[:, :, :].rearrange("p (r g) e -> p g r e", g=GT)[:, k * (GT // 2):(k + 1) * (GT // 2)]
                last = dve.tensor_copy(dst, src)
            step(last)
            step(dve.tensor_scalar(posh[:, :, :], posi[:, :, :], SLOTC - 1, None, ALU.bitwise_and))
            dve.tensor_copy(slot_a[:, 0:NE, :], posh[:, :, :].rearrange("p t e -> p e t"))
            step(dve.tensor_scalar(posi[:, :, :], posi[:, :, :], SLOTC.bit_length() - 1, None, ALU.arith_shift_right))
            step(dve.tensor_copy(slot_b[:, 0:NE, :], posi[:, :, :].rearrange("p t e -> p e t")))

            flat_a = slot_a[:, :, :].rearrange("p e t -> p (e t)")
            flat_b = slot_b[:, :, :].rearrange("p e t -> p (e t)")

            def onehots(k, n, tile_at, wait=True):
                if wait:
                    dve.wait_ge(onehot_used, n - 1)
                bs = flat_b[:, bass.ds(n * LT, LT)].unsqueeze(2).to_broadcast([T, LT, T])
                as_ = flat_a[:, bass.ds(n * LT, LT)].unsqueeze(2).to_broadcast([T, LT, SLOTC])
                ts = iota_b[:, bass.ds(tile_at, LT)].unsqueeze(2).to_broadcast([T, LT, SLOTC])
                dve.tensor_tensor(oh_b[k][:, :, :], bs, iota_b[:, 0:T].unsqueeze(1).to_broadcast([T, LT, T]), ALU.is_equal)
                step(dve.tensor_tensor(eq_a[k][:, :, :], as_, iota_b[:, 0:SLOTC].unsqueeze(1).to_broadcast([T, LT, SLOTC]),
                                       ALU.is_equal))
                dve.tensor_scalar(oh_a[k][:, :, 0, :], eq_a[k][:, :, :], tok_p[:, 0:1], None, ALU.mult)
                dve.tensor_tensor(oh_a[k][:, :, 1, :], eq_a[k][:, :, :], ts, ALU.mult).then_inc(onehot_ready, 1)

            def close_list(e):
                dve.wait_ge(onehot_used, (e + 1) * GROUPS)
                step(dve.tensor_scalar(idx_t[:, :], Y[0][0:T, SLOTC:2 * SLOTC], float(T), None, ALU.mult))
                dst = idx_all[:, bass.ds(e * SLOTC, SLOTC)]
                dve.tensor_tensor(dst, idx_t[:, :], Y[0][0:T, 0:SLOTC], ALU.add).then_inc(list_done, 1)

            for p in range(GROUPS):
                onehots(p % 2, p, p * LT, wait=p >= 2)
            close_list(0)

            dve.wait_ge(norms_summed, 1)
            step(dve.tensor_copy(norms[:, :, :], SC[0][:, 1, 0:3 * NE].rearrange("p (k e) -> p k e", e=NE)))
            step(dve.tensor_scalar(norms[:, 2, :], norms[:, 2, :], 2.0, None, ALU.mult))
            step(dve.scalar_tensor_tensor(norms[:, 2, :], norms[:, 0, :], 512.0, norms[:, 2, :], ALU.mult, ALU.add))
            step(dve.tensor_scalar(half_exp[:, :, :], norms[:, :, :].bitcast(I32), 23, None, ALU.arith_shift_right))
            step(dve.tensor_scalar(half_exp[:, :, :], half_exp[:, :, :], 1.0, None, ALU.add))
            step(dve.tensor_scalar(half_exp[:, :, :], half_exp[:, :, :], 1, None, ALU.arith_shift_right))
            step(dve.tensor_scalar(scales[:, :, :], half_exp[:, :, :], -float(1 << 23), float(204 << 23), ALU.mult, ALU.add))
            step(dve.tensor_scalar(unscales[:, 0:3, :], half_exp[:, :, :], float(1 << 23), float(50 << 23), ALU.mult, ALU.add))
            dve.tensor_tensor(unscales[:, 3, :].bitcast(F32), unscales[:, 1, :].bitcast(F32),
                              unscales[:, 2, :].bitcast(F32), ALU.mult).then_inc(scales_ready, 1)
            dve.wait_ge(scales_ready, 1)

            def split_low(eb, e, p):
                dve.wait_ge(split_high, e * PIECES + (p + 1))
                dve.scalar_tensor_tensor(split_pieces(eb, 1, p), piece((we1[eb][:, :, :], we2[eb][:, :, :]), p), scale_at(scales, p // 4, e),
                                         split_pieces(eb, 0, p), ALU.mult, ALU.subtract).then_inc(split_done, 1)

            def x_low(c, bank, n):
                dve.wait_ge(x_high, n * KC + (c + 1))
                dve.tensor_tensor(xgT[:, 1, c, :], G2[bank][:, 0:W], xgT[:, 0, c, :],
                                  ALU.subtract).then_inc(evacuated2[bank], 1)

            for p in range(PIECES):
                split_low(0, 0, p)
            for c in range(KC):
                x_low(c, c, 0)
            dve.wait_ge(fb2_in, 16)

            def group(e, eb, half_n, k, q, last_of_expert):
                n = half_n * 2 + k
                def h_low(m):
                    dve.wait_ge(h_high, n * MC + (m + 1))
                    dve.scalar_tensor_tensor(hTs[:, 1, m, :], hTe[:, m, :], scale_at(scales, 2, e), hTs[:, 0, m, :],
                                             ALU.mult, ALU.subtract).then_inc(h_split, 1)

                onehots(k, n + GROUPS, (q * 2 + k) * LT)
                for m in range(MC - 1):
                    h_low(m)
                if last_of_expert:
                    close_list(e + 1)
                h_low(MC - 1)
                if last_of_expert:
                    for p in range(PIECES):
                        split_low(1 - eb, e + 1, p)
                for b in range(2):
                    key = ("w2", b)
                    dve.wait_ge(filled2[bank2(key)], count2(n, key))
                    bias = fb2b[:, :, :].rearrange("p e d -> p (e d)")[:, bass.ds(e * D, D)]
                    dve.scalar_tensor_tensor(biased[:, :, :], G2[bank2(key)][0:T, :].rearrange("p (t d) -> p t d", d=D),
                                             scale_at(unscales, 3, e, T), bias.unsqueeze(1).to_broadcast([T, 2, D]),
                                             ALU.mult, ALU.add).then_inc(evacuated2[bank2(key)], 1)
                    wait_evacuated2(dve, n, key)
                    for half in range(2):
                        t = 2 * b + half
                        last = dve.tensor_scalar(contrib[k][:, t, :], biased[:, half, :],
                                                 xg[k][:, t, bass.ds(e + D, 1)], None, ALU.mult)
                    if b == 1:
                        last.then_inc(contrib_done, 1)
                    else:
                        step(last)
                        for c in range(KC):
                            x_low(c, bank2(("xT", c)), n + 1)

            with eng.Fori(0, NE // 2) as E:
                chain.enter(E, 2 * (2 * GROUPS + 1))
                for eb in range(2):
                    e = E * 2 + eb
                    with eng.Fori(0, GROUPS // 2 - 1) as q:
                        chain.enter(q, 4)
                        for k in range(2):
                            group(e, eb, e * (GROUPS // 2) + q, k, q, False)
                    chain.leave(GROUPS // 2 - 1)
                    for k in range(2):
                        group(e, eb, e * (GROUPS // 2) + (GROUPS // 2 - 1), k, GROUPS // 2 - 1, k == 1)
            chain.leave(NE // 2)

        pool = nc.gpsimd

        @block.gpsimd
        def _(eng):
            chain = Chain(pool, pool_step, lambda: wait_apart(pool))
            step = chain.step
            for s in (xn2_stored, h1_stored):
                pool.sem_inc(s, 16)
            for s in (xn2_done, contrib_done, *evacuated2):
                pool.sem_inc(s, 1)
            pool.sem_inc(h_split, MC)
            step(pool.memset(ident[:, :], 0.0))
            pool.affine_select(out=ident[:, :], in_=ident[:, :], compare_op=ALU.not_equal, fill=1.0, base=0,
                               pattern=[[-1, 128]], channel_multiplier=1).then_inc(pool_consts, 1)
            step(pool.memset(first_col[:, :], 0.0))
            pool.memset(first_col[:, 0:1], 1.0).then_inc(pool_consts, 1)
            pool.memset(ln_eps[:, :], LN_EPS)
            pool.memset(rms_eps[:, :], RMS_EPS)
            pool.memset(neg_half[:, :], -0.5).then_inc(pool_consts, 1)
            pool.iota(diff[:, :], [[1, 128]], base=128, channel_multiplier=-1).then_inc(pool_consts, 1)
            pool.iota(iota_i[:, :], [[1, 128]], base=0, channel_multiplier=0).then_inc(pool_consts, 1)
            pool.iota(tok_pi[:, :], [[1, 1]], base=0, channel_multiplier=1).then_inc(pool_consts, 1)
            pool.wait_ge(pool_consts, 6)

            def rsqrt(dst, src, n):
                return pool.tensor_tensor(dst, src, neg_half[0:T, 0:n], ALU.pow)

            def first_norm(j):
                pool.wait_ge(ln1_stats, j + 1)
                step(pool.tensor_tensor(lt[:, 0, :], mv1[:, :, 1], ln_eps[:, 0:NT], ALU.add))
                step(rsqrt(lt[:, 1, :], lt[:, 0, :], NT))
                step(pool.tensor_tensor(lt[:, 2, :], lt[:, 1, :], lt[:, 1, :], ALU.mult))
                step(pool.tensor_tensor(lt[:, 2, :], lt[:, 2, :], mv1[:, :, 1], ALU.mult))
                step(pool.tensor_tensor(lt[:, 3, :], lt[:, 2, :], rms_eps[:, 0:NT], ALU.add))
                step(rsqrt(lt[:, 4, :], lt[:, 3, :], NT))
                pool.tensor_tensor(lt[:, 5, :], lt[:, 4, :], lt[:, 1, :], ALU.mult).then_inc(ln1_scales, 1)

            def residuals(part, j):
                pool.wait_ge(h1_stored, 16 * (j + 1))
                pool.wait_ge(xn2_done, j + 1)
                for b in range(2):
                    part.wait_evacuated(pool, "wo", b)
                    ts = slice(2 * b, 2 * b + 2)
                    pool.tensor_tensor(hy[:, ts, :], y2[:, ts, :], h0_copy[:, ts, :], ALU.add).then_inc(hy_done, 1)

            def keep_h0(j):
                pool.tensor_copy(h0_copy[:, :, :], h0[:, :, :]).then_inc(h0_kept, 1)

            def second_rms(j):
                pool.wait_ge(y2_sums, j + 1)
                step(pool.tensor_tensor(ss2[:, :], ss2[:, :], rms_eps[:, 0:NT], ALU.add))
                rsqrt(r2[:, :], ss2[:, :], NT).then_inc(r2_done, 1)

            def second_norm(j):
                pool.wait_ge(ln2_stats, j + 1)
                step(pool.tensor_tensor(rstd2[:, :], mv2[:, :, 1], ln_eps[:, 0:NT], ALU.add))
                rsqrt(rstd2[:, :], rstd2[:, :], NT).then_inc(ln2_scales, 1)

            def high_parts_again(j):
                for t in range(NT):
                    scaled = NT * j + (t + 1)
                    if not isinstance(scaled, int):
                        scaled = pool.snap(pool.to_reg(scaled))
                        wait_apart(pool)
                    pool.wait_ge(qk_scaled, scaled)
                    src = qkraw[:, t, 0:D].rearrange("p (h d) -> p h d", d=HD)
                    last = pool.tensor_copy(qkp[:, t, 0:H, 2 * HD:3 * HD], src)
                last.then_inc(qk_copied, 1)

            first_norm(0)
            keep_h0(0)
            high_parts_again(0)

            def iteration(part, i):
                first_norm(i)
                residuals(part, i - 1)
                second_rms(i - 1)
                keep_h0(i)
                high_parts_again(i)
                second_norm(i - 1)

            with eng.Fori(1, PAIRS - 1) as i:
                chain.enter(i - 1, 8)
                iteration(Part("body", i), i)
            chain.leave(PAIRS - 2)
            iteration(Part("final", PAIRS - 1), PAIRS - 1)
            residuals(Part("last", PAIRS), PAIRS - 1)
            second_rms(PAIRS - 1)
            second_norm(PAIRS - 1)

            def gather(n, k):
                step(pool.tensor_copy(idx_cur[k][:, :], idx_all[:, bass.ds(n * NT, NT)]), apart=True)
                for t in range(NT):
                    pool.indirect_dma_start(
                        out=xg[k][:, t, :], out_offset=None, in_=xd[:, :],
                        in_offset=bass.IndirectOffsetOnAxis(ap=idx_cur[k][:, t:t + 1], axis=0)).then_inc(gathered[k], 16)

            def scatter(n, k):
                if isinstance(n, int):
                    pool.wait_ge(contrib_done, n + 2)
                else:
                    done = pool.snap(pool.to_reg(n + 2))
                    wait_apart(pool)
                    pool.wait_ge(contrib_done, done)
                for t in range(NT):
                    pool.indirect_dma_start(
                        out=out_rows, out_offset=bass.IndirectOffsetOnAxis(ap=idx_cur[k][:, t:t + 1], axis=0),
                        in_=contrib[k][:, t, :], in_offset=None, compute_op=ALU.add).then_inc(scattered[k], 16)

            def group(half_n, k):
                n = half_n * 2 + k
                pool.wait_ge(contrib_done, n + 1)
                before = (half_n + k) * (16 * NT)
                if not isinstance(before, int) or before:
                    pool.wait_ge(scattered[1 - k], before)
                gather(n + 1, 1 - k)
                scatter(n, k)

            def expert(e, first):
                if not first:
                    former = pool.snap(pool.to_reg(e * (GROUPS // 2 * 16 * NT)))
                    wait_apart(pool)
                    for k in range(2):
                        pool.wait_ge(scattered[k], former)
                else:
                    for k in range(2):
                        group(0, k)
                peeled = int(first)
                with eng.Fori(peeled, GROUPS // 2 - 1) as q:
                    chain.enter(q - peeled, 2)
                    for k in range(2):
                        group(e * (GROUPS // 2) + q, k)
                chain.leave(GROUPS // 2 - 1 - peeled)
                half_n = e * (GROUPS // 2) + (GROUPS // 2 - 1)
                group(half_n, 0)
                pool.wait_ge(list_done, e + 2)
                group(half_n, 1)

            pool.wait_ge(score_stored, 16)
            pool.wait_ge(h1_stored, 16 * (PAIRS + 1))
            pool.wait_ge(xn2_stored, 16 * (PAIRS + 1))
            pool.wait_ge(list_done, 1)
            gather(0, 0)
            expert(0, True)
            with eng.Fori(1, NE) as e:
                chain.enter(e - 1, GROUPS)
                expert(e, False)
            chain.leave(NE - 1)
            for k in range(2):
                pool.wait_ge(scattered[k], NE * GROUPS // 2 * 16 * NT)
            pool.wait_ge(gathered[0], (NE * GROUPS // 2 + 1) * 16 * NT)


_INS = ['x', 'txt', 'L0_tok_W1', 'L0_tok_b1', 'L0_tok_W2', 'L0_tok_b2', 'L0_attn_ln1_w', 'L0_attn_Wq', 'L0_attn_Wk',
        'L0_attn_Wv', 'L0_attn_rel_bias', 'L0_attn_scale', 'L0_attn_Wo', 'L0_attn_ln2_w', 'L0_attn_W1', 'L0_attn_W2',
        'L0_ffn_Wr', 'L0_ffn_W1', 'L0_ffn_b1', 'L0_ffn_W2', 'L0_ffn_b2']
_OUTS = [((64, 228, 256), 'float32')]


def kernel(**inputs):
    import numpy as _np
    import concourse.bacc as _bacc
    from concourse import mybir as _mybir
    from concourse.bass_utils import run_bass_kernel_spmd as _run

    nc = _bacc.Bacc("TRN2", target_bir_lowering=False, num_devices=1)
    arrays, args = {}, []
    for name in _INS:
        a = _np.ascontiguousarray(inputs[name])
        arrays[f"in_{name}_dram"] = a
        args.append(nc.dram_tensor(f"in_{name}_dram", a.shape, _mybir.dt.from_np(a.dtype), kind="ExternalInput").ap())
    for i, (shape, dtype) in enumerate(_OUTS):
        dt = _mybir.dt.from_np(_np.dtype(dtype))
        args.append(nc.dram_tensor(f"out_{i}_dram", shape, dt, kind="ExternalOutput").ap())
    early_fusion_kernel(nc, *args)
    r = _run(nc, [arrays], core_ids=[0])
    return r.results[0]["out_0_dram"]
```
